# Optimizing a Trainium2 kernel written in Bass

```python
import numpy as np
import jax
import jax.numpy as jnp

def _softmax(x, axis=-1):
    return jax.nn.softmax(x, axis=axis)

def _gelu(x):
    return jax.nn.gelu(x, approximate=True)

def _silu(x):
    return jax.nn.silu(x)

def _sigmoid(x):
    return jax.nn.sigmoid(x)

def _layernorm(x, axis=-1, eps=1e-05):
    m = jnp.mean(x, axis=axis, keepdims=True)
    v = jnp.var(x, axis=axis, keepdims=True)
    return (x - m) / jnp.sqrt(v + eps)

def _scatter_add(tgt, idx, src, axis=0):
    return tgt.at[idx].add(src)

def _segment_sum(src, seg, n):
    return jax.ops.segment_sum(src, seg, n)
kernel_name = 'mk_xattn_seq_d2_seqx_r8_bd6df9'

def setup_inputs(seed: int=0):
    np.random.seed(seed)
    _w = jnp.asarray

    def _rec_inputs():
        import jax
        import jax.numpy as jnp
        _rk = jax.random.key(seed)
        x = -0.000125 + 0.9999 * jax.random.normal(jax.random.fold_in(_rk, 1), (4, 256, 256), jnp.float32)
        _lenS = 256 - jax.random.randint(jax.random.fold_in(_rk, 7), (4,), 0, max(1, 256 // 4) + 1, jnp.int32)
        _lenS2 = 512 - jax.random.randint(jax.random.fold_in(_rk, 8), (4,), 0, max(1, 512 // 4) + 1, jnp.int32)
        _ctx_2048P = jax.random.normal(jax.random.fold_in(_rk, 11), (4, 16, 256), jnp.float32)
        _ctx_2048c = jax.random.dirichlet(jax.random.fold_in(_rk, 511), 0.3 * jnp.ones((16,), jnp.float32), (4, 512))
        _ctx_2048t = jnp.einsum('bsk,bkd->bsd', _ctx_2048c, _ctx_2048P)
        _ctx_2048t = _ctx_2048t * jax.lax.rsqrt(jnp.mean(jnp.square(_ctx_2048t)) + 1e-12) * 0.953939
        ctx_2048 = -0.00401388 + 1.00018 * (_ctx_2048t + 0.3 * jax.random.normal(jax.random.fold_in(_rk, 611), (4, 512, 256), jnp.float32))
        return (x, ctx_2048)
    x, ctx_2048 = _rec_inputs()

    def _L0_xattn_setup():
        import jax, jax.numpy as jnp
        import numpy as np
        H = 256
        B, L, S = (4, 512, 10)
        key = jax.random.key(seed)
        k1, k2, k3, k4, k5, k6 = jax.random.split(key, 6)
        scale = 1.0 / np.sqrt(H)
        return {'h_english': jax.random.normal(k1, (B, L, H), dtype=jnp.float32), 'h_lojban': jax.random.normal(k2, (B, S, H), dtype=jnp.float32), 'w_q': jax.random.normal(k3, (H, H), dtype=jnp.float32) * scale, 'w_k': jax.random.normal(k4, (H, H), dtype=jnp.float32) * scale, 'w_v': jax.random.normal(k5, (H, H), dtype=jnp.float32) * scale, 'w_o': jax.random.normal(k6, (H, H), dtype=jnp.float32) * scale, 'alpha': jnp.float32(0.1)}
    _L0_xattn_all = _L0_xattn_setup()
    _L0_xattn_in = {k: v for k, v in _L0_xattn_all.items() if k in ('w_q', 'w_k', 'w_v', 'w_o', 'alpha')}
    del _L0_xattn_all

    def _L1_xattn_setup():
        import jax, jax.numpy as jnp
        import numpy as np
        B, Q, S1, S2 = (4, 32, 256, 256)
        D, H, K, F = (256, 16, 128, 1024)
        LN_EPS = 1e-05

        def _layer_norm(x, scale, offset):
            mu = jnp.mean(x, axis=-1, keepdims=True)
            var = jnp.var(x, axis=-1, keepdims=True)
            return (x - mu) * jax.lax.rsqrt(var + LN_EPS) * scale + offset

        def _cross_attention(q_in, kv_in, wq, bq, wk, bk, wv, bv, wo, bo, bias_k, bias_v):
            b, q_len, _ = q_in.shape
            t = kv_in.shape[1]
            qh = (q_in @ wq + bq).reshape(b, q_len, H, K)
            kh = (kv_in @ wk + bk).reshape(b, t, H, K)
            vh = (kv_in @ wv + bv).reshape(b, t, H, K)
            kh = jnp.concatenate([kh, jnp.broadcast_to(bias_k, (b, 1, H, K))], axis=1)
            vh = jnp.concatenate([vh, jnp.broadcast_to(bias_v, (b, 1, H, K))], axis=1)
            scale = jnp.sqrt(jnp.asarray(K, q_in.dtype))
            logits = jnp.einsum('bqhk,bthk->bhqt', qh, kh) / scale
            weights = jax.nn.softmax(logits, axis=-1)
            ctx = jnp.einsum('bhqt,bthk->bqhk', weights, vh).reshape(b, q_len, H * K)
            return ctx @ wo + bo

        def _forward(x, xf_1, xf_2, ln1_scale, ln1_offset, wq1, bq1, wk1, bk1, wv1, bv1, wo1, bo1, bias_k1, bias_v1, ln2_scale, ln2_offset, wq2, bq2, wk2, bk2, wv2, bv2, wo2, bo2, bias_k2, bias_v2, ln_mlp_scale, ln_mlp_offset, w_fc1, b_fc1, w_fc2, b_fc2):
            res = x
            h = _layer_norm(x, ln1_scale, ln1_offset)
            x = res + _cross_attention(h, xf_1, wq1, bq1, wk1, bk1, wv1, bv1, wo1, bo1, bias_k1, bias_v1)
            res = x
            h = _layer_norm(x, ln2_scale, ln2_offset)
            x = res + _cross_attention(h, xf_2, wq2, bq2, wk2, bk2, wv2, bv2, wo2, bo2, bias_k2, bias_v2)
            h = _layer_norm(x, ln_mlp_scale, ln_mlp_offset)
            h = jax.nn.gelu(h @ w_fc1 + b_fc1, approximate=False) @ w_fc2 + b_fc2
            return x + h
        key = jax.random.key(seed)
        ks = iter(jax.random.split(key, 64))

        def rn(shape, s=0.02):
            return jax.random.normal(next(ks), shape, jnp.float32) * s
        inp = {'x': rn((B, Q, D), 1.0), 'xf_1': rn((B, S1, D), 1.0), 'xf_2': rn((B, S2, D), 1.0)}
        for i in (1, 2):
            inp[f'ln{i}_scale'] = jnp.ones((D,), jnp.float32)
            inp[f'ln{i}_offset'] = jnp.zeros((D,), jnp.float32)
            inp[f'wq{i}'] = rn((D, H * K))
            inp[f'bq{i}'] = jnp.zeros((H * K,), jnp.float32)
            inp[f'wk{i}'] = rn((D, H * K))
            inp[f'bk{i}'] = jnp.zeros((H * K,), jnp.float32)
            inp[f'wv{i}'] = rn((D, H * K))
            inp[f'bv{i}'] = jnp.zeros((H * K,), jnp.float32)
            inp[f'wo{i}'] = rn((H * K, D))
            inp[f'bo{i}'] = jnp.zeros((D,), jnp.float32)
            inp[f'bias_k{i}'] = rn((1, 1, H, K))
            inp[f'bias_v{i}'] = rn((1, 1, H, K))
        inp['ln_mlp_scale'] = jnp.ones((D,), jnp.float32)
        inp['ln_mlp_offset'] = jnp.zeros((D,), jnp.float32)
        inp['w_fc1'] = rn((D, F))
        inp['b_fc1'] = jnp.zeros((F,), jnp.float32)
        inp['w_fc2'] = rn((F, D))
        inp['b_fc2'] = jnp.zeros((D,), jnp.float32)
        return inp
    _L1_xattn_all = _L1_xattn_setup()
    _L1_xattn_in = {k: v for k, v in _L1_xattn_all.items() if k in ('ln1_scale', 'ln1_offset', 'wq1', 'bq1', 'wk1', 'bk1', 'wv1', 'bv1', 'wo1', 'bo1', 'bias_k1', 'bias_v1', 'ln2_scale', 'ln2_offset', 'wq2', 'bq2', 'wk2', 'bk2', 'wv2', 'bv2', 'wo2', 'bo2', 'bias_k2', 'bias_v2', 'ln_mlp_scale', 'ln_mlp_offset', 'w_fc1', 'b_fc1', 'w_fc2', 'b_fc2')}
    del _L1_xattn_all
    return {'x': x, 'ctx_2048': ctx_2048, 'L0_xattn_w_q': _L0_xattn_in['w_q'], 'L0_xattn_w_k': _L0_xattn_in['w_k'], 'L0_xattn_w_v': _L0_xattn_in['w_v'], 'L0_xattn_w_o': _L0_xattn_in['w_o'], 'L0_xattn_alpha': _L0_xattn_in['alpha'], 'L1_xattn_ln1_scale': _L1_xattn_in['ln1_scale'], 'L1_xattn_ln1_offset': _L1_xattn_in['ln1_offset'], 'L1_xattn_wq1': _L1_xattn_in['wq1'], 'L1_xattn_bq1': _L1_xattn_in['bq1'], 'L1_xattn_wk1': _L1_xattn_in['wk1'], 'L1_xattn_bk1': _L1_xattn_in['bk1'], 'L1_xattn_wv1': _L1_xattn_in['wv1'], 'L1_xattn_bv1': _L1_xattn_in['bv1'], 'L1_xattn_wo1': _L1_xattn_in['wo1'], 'L1_xattn_bo1': _L1_xattn_in['bo1'], 'L1_xattn_bias_k1': _L1_xattn_in['bias_k1'], 'L1_xattn_bias_v1': _L1_xattn_in['bias_v1'], 'L1_xattn_ln2_scale': _L1_xattn_in['ln2_scale'], 'L1_xattn_ln2_offset': _L1_xattn_in['ln2_offset'], 'L1_xattn_wq2': _L1_xattn_in['wq2'], 'L1_xattn_bq2': _L1_xattn_in['bq2'], 'L1_xattn_wk2': _L1_xattn_in['wk2'], 'L1_xattn_bk2': _L1_xattn_in['bk2'], 'L1_xattn_wv2': _L1_xattn_in['wv2'], 'L1_xattn_bv2': _L1_xattn_in['bv2'], 'L1_xattn_wo2': _L1_xattn_in['wo2'], 'L1_xattn_bo2': _L1_xattn_in['bo2'], 'L1_xattn_bias_k2': _L1_xattn_in['bias_k2'], 'L1_xattn_bias_v2': _L1_xattn_in['bias_v2'], 'L1_xattn_ln_mlp_scale': _L1_xattn_in['ln_mlp_scale'], 'L1_xattn_ln_mlp_offset': _L1_xattn_in['ln_mlp_offset'], 'L1_xattn_w_fc1': _L1_xattn_in['w_fc1'], 'L1_xattn_b_fc1': _L1_xattn_in['b_fc1'], 'L1_xattn_w_fc2': _L1_xattn_in['w_fc2'], 'L1_xattn_b_fc2': _L1_xattn_in['b_fc2']}

def reference(x, ctx_2048, L0_xattn_w_q, L0_xattn_w_k, L0_xattn_w_v, L0_xattn_w_o, L0_xattn_alpha, L1_xattn_ln1_scale, L1_xattn_ln1_offset, L1_xattn_wq1, L1_xattn_bq1, L1_xattn_wk1, L1_xattn_bk1, L1_xattn_wv1, L1_xattn_bv1, L1_xattn_wo1, L1_xattn_bo1, L1_xattn_bias_k1, L1_xattn_bias_v1, L1_xattn_ln2_scale, L1_xattn_ln2_offset, L1_xattn_wq2, L1_xattn_bq2, L1_xattn_wk2, L1_xattn_bk2, L1_xattn_wv2, L1_xattn_bv2, L1_xattn_wo2, L1_xattn_bo2, L1_xattn_bias_k2, L1_xattn_bias_v2, L1_xattn_ln_mlp_scale, L1_xattn_ln_mlp_offset, L1_xattn_w_fc1, L1_xattn_b_fc1, L1_xattn_w_fc2, L1_xattn_b_fc2):
    import jax
    import jax.numpy as jnp

    def _L0_xattn_ref(h_english, h_lojban, w_q, w_k, w_v, w_o, alpha):
        import jax, jax.numpy as jnp
        import numpy as np
        H = 256
        B, L, S = (4, 512, 10)
        h = h_english.shape[-1]
        q = jnp.einsum('blh,oh->blo', h_english, w_q)
        k = jnp.einsum('bsh,oh->bso', h_lojban, w_k)
        v = jnp.einsum('bsh,oh->bso', h_lojban, w_v)
        scores = jnp.einsum('blh,bsh->bls', q, k) / jnp.sqrt(jnp.float32(h))
        probs = jax.nn.softmax(scores, axis=-1)
        context = jnp.einsum('bls,bsh->blh', probs, v)
        delta = jnp.einsum('blh,oh->blo', context, w_o)
        return h_english + alpha * delta

    def _L1_xattn_ref(x, xf_1, xf_2, ln1_scale, ln1_offset, wq1, bq1, wk1, bk1, wv1, bv1, wo1, bo1, bias_k1, bias_v1, ln2_scale, ln2_offset, wq2, bq2, wk2, bk2, wv2, bv2, wo2, bo2, bias_k2, bias_v2, ln_mlp_scale, ln_mlp_offset, w_fc1, b_fc1, w_fc2, b_fc2):
        import jax, jax.numpy as jnp
        import numpy as np
        B, Q, S1, S2 = (4, 32, 256, 256)
        D, H, K, F = (256, 16, 128, 1024)
        LN_EPS = 1e-05

        def _layer_norm(x, scale, offset):
            mu = jnp.mean(x, axis=-1, keepdims=True)
            var = jnp.var(x, axis=-1, keepdims=True)
            return (x - mu) * jax.lax.rsqrt(var + LN_EPS) * scale + offset

        def _cross_attention(q_in, kv_in, wq, bq, wk, bk, wv, bv, wo, bo, bias_k, bias_v):
            b, q_len, _ = q_in.shape
            t = kv_in.shape[1]
            qh = (q_in @ wq + bq).reshape(b, q_len, H, K)
            kh = (kv_in @ wk + bk).reshape(b, t, H, K)
            vh = (kv_in @ wv + bv).reshape(b, t, H, K)
            kh = jnp.concatenate([kh, jnp.broadcast_to(bias_k, (b, 1, H, K))], axis=1)
            vh = jnp.concatenate([vh, jnp.broadcast_to(bias_v, (b, 1, H, K))], axis=1)
            scale = jnp.sqrt(jnp.asarray(K, q_in.dtype))
            logits = jnp.einsum('bqhk,bthk->bhqt', qh, kh) / scale
            weights = jax.nn.softmax(logits, axis=-1)
            ctx = jnp.einsum('bhqt,bthk->bqhk', weights, vh).reshape(b, q_len, H * K)
            return ctx @ wo + bo

        def _forward(x, xf_1, xf_2, ln1_scale, ln1_offset, wq1, bq1, wk1, bk1, wv1, bv1, wo1, bo1, bias_k1, bias_v1, ln2_scale, ln2_offset, wq2, bq2, wk2, bk2, wv2, bv2, wo2, bo2, bias_k2, bias_v2, ln_mlp_scale, ln_mlp_offset, w_fc1, b_fc1, w_fc2, b_fc2):
            res = x
            h = _layer_norm(x, ln1_scale, ln1_offset)
            x = res + _cross_attention(h, xf_1, wq1, bq1, wk1, bk1, wv1, bv1, wo1, bo1, bias_k1, bias_v1)
            res = x
            h = _layer_norm(x, ln2_scale, ln2_offset)
            x = res + _cross_attention(h, xf_2, wq2, bq2, wk2, bk2, wv2, bv2, wo2, bo2, bias_k2, bias_v2)
            h = _layer_norm(x, ln_mlp_scale, ln_mlp_offset)
            h = jax.nn.gelu(h @ w_fc1 + b_fc1, approximate=False) @ w_fc2 + b_fc2
            return x + h
        return _forward(x, xf_1, xf_2, ln1_scale, ln1_offset, wq1, bq1, wk1, bk1, wv1, bv1, wo1, bo1, bias_k1, bias_v1, ln2_scale, ln2_offset, wq2, bq2, wk2, bk2, wv2, bv2, wo2, bo2, bias_k2, bias_v2, ln_mlp_scale, ln_mlp_offset, w_fc1, b_fc1, w_fc2, b_fc2)
    x = _L0_xattn_ref(x, ctx_2048, L0_xattn_w_q, L0_xattn_w_k, L0_xattn_w_v, L0_xattn_w_o, L0_xattn_alpha)
    x = _L1_xattn_ref(x, ctx_2048, ctx_2048, L1_xattn_ln1_scale, L1_xattn_ln1_offset, L1_xattn_wq1, L1_xattn_bq1, L1_xattn_wk1, L1_xattn_bk1, L1_xattn_wv1, L1_xattn_bv1, L1_xattn_wo1, L1_xattn_bo1, L1_xattn_bias_k1, L1_xattn_bias_v1, L1_xattn_ln2_scale, L1_xattn_ln2_offset, L1_xattn_wq2, L1_xattn_bq2, L1_xattn_wk2, L1_xattn_bk2, L1_xattn_wv2, L1_xattn_bv2, L1_xattn_wo2, L1_xattn_bo2, L1_xattn_bias_k2, L1_xattn_bias_v2, L1_xattn_ln_mlp_scale, L1_xattn_ln_mlp_offset, L1_xattn_w_fc1, L1_xattn_b_fc1, L1_xattn_w_fc2, L1_xattn_b_fc2)
    return x

_drawn_inputs = setup_inputs


def setup_inputs(seed=0):
    import zlib

    import numpy as np

    out = dict(_drawn_inputs(seed))
    spreads = {'L1_xattn_ln1_scale': (1.0, 0.6),
     'L1_xattn_ln1_offset': (0.0, 0.8),
     'L1_xattn_bq1': (0.0, 0.8),
     'L1_xattn_bk1': (0.0, 2.0),
     'L1_xattn_bv1': (0.0, 0.1),
     'L1_xattn_bo1': (0.0, 0.1),
     'L1_xattn_ln2_scale': (1.0, 0.6),
     'L1_xattn_ln2_offset': (0.0, 0.8),
     'L1_xattn_bq2': (0.0, 0.8),
     'L1_xattn_bk2': (0.0, 2.0),
     'L1_xattn_bv2': (0.0, 0.1),
     'L1_xattn_bo2': (0.0, 0.1),
     'L1_xattn_ln_mlp_scale': (1.0, 0.6),
     'L1_xattn_ln_mlp_offset': (0.0, 0.677),
     'L1_xattn_b_fc1': (0.0, 0.1),
     'L1_xattn_b_fc2': (0.0, 0.1)}
    factors = {'L0_xattn_w_q': 2.983,
     'L0_xattn_w_k': 3.01,
     'L1_xattn_wq1': 8.0,
     'L1_xattn_wk1': 8.0,
     'L1_xattn_bias_k1': 64.0,
     'L1_xattn_bias_v1': 64.0,
     'L1_xattn_wq2': 8.0,
     'L1_xattn_wk2': 8.0,
     'L1_xattn_bias_k2': 64.0,
     'L1_xattn_bias_v2': 64.0}
    for name, (base, spread) in spreads.items():
        noise = np.random.default_rng([zlib.crc32(name.encode()), seed]).standard_normal(out[name].shape)
        drawn = base * np.exp(spread * noise) if base else spread * noise
        out[name] = jnp.asarray(drawn.astype(out[name].dtype))
    for name, factor in factors.items():
        out[name] = (out[name] * factor).astype(out[name].dtype)
    return out
```

```python
from contextlib import ExitStack

import concourse.bass as bass
from concourse import mybir

F32 = mybir.dt.float32
F32R = mybir.dt.float32r
ALU = mybir.AluOpType
ACT = mybir.ActivationFunctionType
AX_X = mybir.AxisListType.X

P = 128
B, LQ, D = 4, 256, 256
T = 512
HEADS, DH = 16, 128
F = 1024
QT = LQ // P
DC = D // P
TC = T // P
FC = F // P
PAIRS = HEADS // 2
PW = 2 * DH
UNITS = 2 * B
EPS = 1e-5
SCALE0 = float(D) ** -0.5
SCALE = float(DH) ** -0.5
WK, WQ, WV, WO = range(4)
HI, LO = 0, 1
PASSES = ((HI, LO), (LO, HI), (HI, HI))
BQ, BK, BV, BIAS_K, BIAS_V, LN_G, LN_O, FC1_B = 0, 16, 32, 48, 64, 80, 82, 84
CHUNK_H = 4
CHUNKS = HEADS // CHUNK_H


def startup_fills():
    pro = ["vec", "M", "xT0", "cT00", "cT01", "G0"]
    slots = []
    for b in range(B):
        ahead = [f"xT{b+1}", f"cT{b+1}0", f"cT{b+1}1"] + (["WoT", "N"] if b == 0 else []) + [f"G{b+1}"] if b < B - 1 else []
        extra = [f"RA{2*b}", f"RA{2*b+1}"] + [[], ["K0", "K1"], ["Va", "Vb"], []][b]
        slots.append((ahead, extra))
    tail = ["Q", "RB0", "RB1"]
    order = list(pro)
    for ahead, extra in slots:
        order += ahead + extra
    return pro, slots, tail, order + tail


def xattn_kernel(nc, A):
    pro_fills, slot_fills, tail_fills, fill_order = startup_fills()
    FILL = {name: n for n, name in enumerate(fill_order)}
    NF0 = len(fill_order)
    MLP_FILL = NF0 + 2 * 5 * B * PAIRS - 5

    def unit(l, r, k):
        return r * UNITS + (B + UNITS * PAIRS * l + k)

    def step_fill(l, r, b, f):
        return r * (5 * B) + (NF0 + 5 * B * PAIRS * l + 5 * b + f - 5)

    OB0 = 3 * B
    OB_LAYER = B * (PAIRS - 1) + 4 * B

    def ob_out(l, r, b):
        return r * B + (OB0 + OB_LAYER * l + b)

    def ob_last(l, b, what):
        per = 4 if l == 0 else 3
        return OB0 + OB_LAYER * l + B * (PAIRS - 1) + per * b + ["pbT", "out", "lnT", "sb"].index(what)

    def ob_use(l, r, b):
        return ob_last(l, b, "out") if isinstance(r, int) and r == PAIRS - 1 else ob_out(l, r, b)

    OB_MLP = OB0 + OB_LAYER + B * (PAIRS - 1) + 3 * B

    with ExitStack() as ctx:
        def sb(name, shape, dt=F32):
            return ctx.enter_context(nc.sbuf_tensor(name, shape, dt))

        def ps(name, shape):
            return ctx.enter_context(nc.psum_tensor(name, shape, F32))

        def sem(name):
            return ctx.enter_context(nc.semaphore(name))

        scores = ps("scores", [P, QT, T])
        probsT_ps = ps("probsT_ps", [P, TC, LQ])
        proj = [ps(f"proj{i}", [P, 512]) for i in range(2)]
        mix_ps = ps("mix_ps", [P, 512])
        out_ps = ps("out_ps", [P, 512])

        cT = sb("cT", [P, 2, DC, B * T], F32R)
        hT = sb("hT", [P, 2, DC, B * LQ], F32R)
        wS = sb("wS", [P, 2, 4, DC, PW], F32R)
        kT = sb("kT", [P, 2, 2, T], F32R)
        qT = sb("qT", [P, 2, 2, LQ], F32R)
        vS = sb("vS", [P, 2, 2, TC, PW], F32R)
        probsT = sb("probsT", [P, 2, TC, LQ], F32R)
        mixT = sb("mixT", [P, 2, 2, LQ], F32R)
        arena = sb("arena", [P, 8192], F32R)
        nat = arena[:, 0:4096].rearrange("p (n s c d) -> p n s c d", n=2, s=2, c=TC)
        w0S = arena[:, 4096:8192].rearrange("p (s w c d) -> p s w c d", s=2, w=4, c=DC)
        w1S = arena[:, 0:4096].rearrange("p (s c f) -> p s c f", s=2, c=DC)
        w2S = arena[:, 4096:8192].rearrange("p (s c d) -> p s c d", s=2, c=FC)
        nS = w0S[:, :, WK]
        mS = sb("mS", [P, 2, DC, D], F32R)
        gS = sb("gS", [P, 2, DC, LQ], F32R)
        rS = sb("rS", [P, 2, 2, D], F32R)
        wbS = sb("wbS", [P, 2, 2, DC, HEADS], F32R)
        pbT = sb("pbT", [P, 2, LQ], F32R)
        gelu_hi = vS[:].rearrange("p s n c d -> p (s n c d)").rearrange("p (f q) -> p f q", f=FC)
        gelu_lo = wS[:].rearrange("p s w c d -> p (s w c d)").rearrange("p (f q) -> p f q", f=FC)

        x = sb("x", [P, B * QT, D])
        w_raw = sb("w_raw", [P, 4, DC, PW])
        nat_raw = sb("nat_raw", [P, 2, TC, D])
        ck_wq = sb("ck_wq", [P, DC, CHUNK_H * DH])
        ck_wo = sb("ck_wo", [P, CHUNK_H, D])
        ck_bk = sb("ck_bk", [P, CHUNK_H * DH])
        probs = sb("probs", [P, QT, T])
        gelu_full = probs
        xn = sb("xn", [P, QT, D])
        h_full = sb("h_full", [P, DC, LQ])
        p_bias = sb("p_bias", [P, B * QT, P])
        vec_raw = sb("vec_raw", [P, 2, P])
        vecT = sb("vecT", [P, 2, P])
        ident = sb("ident", [P, P])
        ones = sb("ones", [P, P])
        b2_row = sb("b2_row", [P, D])
        bo_row = sb("bo_row", [P, 2, D])
        alpha = sb("alpha", [P, 1])
        vt2 = sb("vt2", [P, 2, HEADS, 2])
        bqk = sb("bqk", [P, 2, HEADS])
        wb_full = sb("wb_full", [P, 2, DC, HEADS])
        rt_raw = sb("rt_raw", [P, 2, 2, CHUNKS, DC, CHUNK_H])
        rt = sb("rt", [P, DC, P])
        r_full = sb("r_full", [P, D])
        p_pair = sb("p_pair", [P, B * QT, 2])
        act_bias = sb("act_bias", [P, 2, 2])
        nsb = sb("nsb", [P, B * QT, HEADS])
        mx = sb("mx", [P, QT])
        shift = sb("shift", [P, QT])
        z = sb("z", [P, QT])
        eb = sb("eb", [P, QT])
        zsum = sb("zsum", [P, QT])
        rz = sb("rz", [P, QT])
        rz0 = sb("rz0", [P, B, QT])
        bn = sb("bn", [P, QT, 6])
        mv = sb("mv", [P, QT, 2])
        std = sb("std", [P, QT])
        rstd = sb("rstd", [P, QT])

        d_w0 = [sem(f"d_w0_{i}") for i in range(4)]
        d_nat = [sem(f"d_nat{i}") for i in range(2)]
        d_x = sem("d_x")
        d_vec = sem("d_vec")
        d_small = sem("d_small")
        d_wq, d_wo, d_bk = sem("d_ck_wq"), sem("d_ck_wo"), sem("d_ck_bk")
        d_w = [sem(f"d_w_{n}") for n in "kqvo"]
        d_out = sem("d_out")
        fill_done, fill_hi, fill_lo = sem("fill_done"), sem("fill_hi"), sem("fill_lo")
        scores_done, max_ready, shift_ready, exp_done = sem("scores_done"), sem("max_ready"), sem("shift_ready"), sem("exp_done")
        act_bias_ready, eb_ready, zsum_ready, rz_ready, norm_done = sem("act_bias_ready"), sem("eb_ready"), sem("zsum_ready"), sem("rz_ready"), sem("norm_done")
        pt_done, pt_hi, pt_lo = sem("pt_done"), sem("pt_hi"), sem("pt_lo")
        mix_done, mix_hi, mix_lo = sem("mix_done"), sem("mix_hi"), sem("mix_lo")
        out_done, out_free = sem("out_done"), sem("out_free")
        w_ready = [sem(f"w_ready_{n}") for n in "kqvo"]
        split_hi = [sem(f"split_hi_{n}") for n in "kqvo"]
        w0_hi, w0_ready = sem("w0_hi"), sem("w0_ready")
        nat_hi, nat_ready = sem("nat_hi"), sem("nat_ready")
        consts_ready = sem("consts_ready")
        pool_chain, chain = sem("pool_chain"), sem("dve_chain")
        var_ready, std_ready, xn_ready, h_full_ready, hT_ready = (sem(n) for n in ("var_ready", "std_ready", "xn_ready", "h_full_ready", "hT_ready"))
        nsb_ready, pb_ready, pbT_hi, pbT_ready = sem("nsb_ready"), sem("pb_ready"), sem("pbT_hi"), sem("pbT_ready")
        vec_ready, rt_ready, wb_used, wb_ready = sem("vec_ready"), sem("rt_ready"), sem("wb_used"), sem("wb_ready")
        mlp_hi, mlp_ready = sem("mlp_hi"), sem("mlp_ready")
        down_done, result_ready = sem("down_done"), sem("result_ready")

        w0_dram = [A["L0_xattn_w_k"], A["L0_xattn_w_q"], A["L0_xattn_w_v"], A["L0_xattn_w_o"]]

        def stage_dram(l, name):
            return A[f"L1_xattn_{name}{l + 1}"]

        def pair_dram(l, w, r):
            if w == WO:
                v = stage_dram(l, "wo").rearrange("(h d) n -> d h n", d=DH)
                return v[:, bass.ds(r * 2, 2), :]
            v = stage_dram(l, {WK: "wk", WQ: "wq", WV: "wv"}[w]).rearrange("(c p) n -> p c n", p=P)
            return v[:, :, bass.ds(r * PW, PW)]

        block = ctx.enter_context(nc.Block())

        @block.sync
        def _(sp):
            for w in (WQ, WK):
                sp.dma_start(w_raw[:, w], w0_dram[w].rearrange("(c p) n -> p c n", p=P)).then_inc(d_w0[w], 16)
            ctx_dram = A["ctx_2048"].rearrange("b (c p) d -> b p c d", p=P)
            sp.dma_start(nat_raw[:, 0], ctx_dram[0]).then_inc(d_nat[0], 16)
            sp.dma_start(x[:], A["x"].rearrange("b (t p) d -> p (b t) d", p=P)).then_inc(d_x, 16)
            sp.wait_ge(consts_ready, 5)
            rows = [("bq", BQ), ("bk", BK), ("bv", BV), ("bias_k", BIAS_K), ("bias_v", BIAS_V)]
            for l in range(2):
                for name, at in rows:
                    v = stage_dram(l, name)
                    if len(v.shape) == 4:
                        v = v.rearrange("a b h k -> (a b h) k")
                    else:
                        v = v.rearrange("(h k) -> h k", k=DH)
                    sp.dma_start(vec_raw[at:at + HEADS, l, :], v).then_inc(d_vec, 16)
                for v, at in ((A[f"L1_xattn_ln{l+1}_scale"], LN_G), (A[f"L1_xattn_ln{l+1}_offset"], LN_O)):
                    sp.dma_start(vec_raw[at:at + DC, l, :], v.rearrange("(c k) -> c k", k=P)).then_inc(d_vec, 16)
            for v, at, n in ((A["L1_xattn_b_fc1"], FC1_B, FC), (A["L1_xattn_ln_mlp_scale"], FC1_B + FC, DC),
                             (A["L1_xattn_ln_mlp_offset"], FC1_B + FC + DC, DC)):
                sp.dma_start(vec_raw[at:at + n, 0, :], v.rearrange("(c k) -> c k", k=P)).then_inc(d_vec, 16)
            for w in (WV, WO):
                sp.dma_start(w_raw[:, w], w0_dram[w].rearrange("(c p) n -> p c n", p=P)).then_inc(d_w0[w], 16)
            sp.dma_start(nat_raw[:, 1], ctx_dram[1]).then_inc(d_nat[1], 16)
            sp.dma_start(alpha[:], A["L0_xattn_alpha"].partition_broadcast(P)).then_inc(d_small, 16)
            sp.dma_start(b2_row[:], A["L1_xattn_b_fc2"].partition_broadcast(P)).then_inc(d_small, 16)
            for l in range(2):
                sp.dma_start(bo_row[0:1, l, :], stage_dram(l, "bo").rearrange("(a n) -> a n", a=1)).then_inc(d_small, 16)

            def chunk(n):
                l, c = divmod(n, CHUNKS)
                if n:
                    sp.wait_ge(wb_used, n)
                sp.dma_start(ck_wq[:], stage_dram(l, "wq").rearrange("(c p) n -> p c n", p=P)[
                    :, :, c * CHUNK_H * DH:(c + 1) * CHUNK_H * DH]).then_inc(d_wq, 16)
                sp.dma_start(ck_bk[:], stage_dram(l, "bias_k").rearrange("a b h k -> (a b h k)")[
                    c * CHUNK_H * DH:(c + 1) * CHUNK_H * DH].partition_broadcast(P)).then_inc(d_bk, 16)
                if n:
                    sp.wait_ge(fill_done, FILL[f"RA{n-1}"] + 1)
                sp.dma_start(ck_wo[:], stage_dram(l, "wo").rearrange("(h d) n -> d h n", d=DH)[
                    :, c * CHUNK_H:(c + 1) * CHUNK_H, :]).then_inc(d_wo, 16)

            def ctx_batch(b):
                sp.wait_ge(fill_done, FILL[f"cT{b-2}1"] + 1)
                sp.wait_ge(nat_ready, b - 1)
                sp.dma_start(nat_raw[:, b % 2], ctx_dram[b]).then_inc(d_nat[b % 2], 16)

            chunk(0)
            ctx_batch(2)
            chunk(1)
            sp.wait_ge(w0_ready, 3)
            sp.wait_ge(fill_done, FILL["WoT"] + 1)
            for w in (WK, WQ, WV, WO):
                sp.dma_start(w_raw[:, w], pair_dram(0, w, 0)).then_inc(d_w[w], 16)
            ctx_batch(3)
            for n in range(2, 2 * CHUNKS):
                chunk(n)

            def next_pair(l, r, ln, rn):
                for w in (WK, WQ, WV, WO):
                    sp.wait_ge(w_ready[w], r + (PAIRS * l + 1))
                    sp.dma_start(w_raw[:, w], pair_dram(ln, w, rn)).then_inc(d_w[w], 16)

            with sp.Fori(0, PAIRS - 1) as r:
                next_pair(0, r, 0, r + 1)
            next_pair(0, PAIRS - 1, 1, 0)
            with sp.Fori(0, PAIRS - 1) as r:
                next_pair(1, r, 1, r + 1)
            for w in range(4):
                sp.wait_ge(w_ready[w], 2 * PAIRS)
            w1_raw = w_raw[:].rearrange("p w c n -> p (w c n)").rearrange("p (c f) -> p c f", c=DC)
            sp.dma_start(w1_raw, A["L1_xattn_w_fc1"].rearrange("(c p) f -> p c f", p=P)).then_inc(d_w0[0], 16)
            w2_raw = nat_raw[:].rearrange("p n c d -> p (n c) d")
            sp.dma_start(w2_raw, A["L1_xattn_w_fc2"].rearrange("(c p) n -> p c n", p=P)).then_inc(d_w0[1], 16)
            out_dram = A["out"].rearrange("b (t p) d -> b p t d", p=P)
            for b in range(B):
                sp.wait_ge(result_ready, b + 1)
                sp.dma_start(out_dram[b], x[:, QT * b:QT * (b + 1), :]).then_inc(d_out, 16)
            sp.wait_ge(d_out, 16 * B)

        @block.gpsimd
        def _(pool):
            links = [0]

            def link(ins):
                links[0] += 1
                ins.then_inc(pool_chain, 1)
                pool.wait_ge(pool_chain, links[0])

            nc.gpsimd.memset(vec_raw[:], 0.0).then_inc(consts_ready, 1)
            link(nc.gpsimd.memset(ident[:], 0.0))
            nc.gpsimd.affine_select(out=ident[:], in_=ident[:], compare_op=ALU.not_equal, fill=1.0, base=0,
                                    pattern=[[-1, P]], channel_multiplier=1).then_inc(consts_ready, 1)
            nc.gpsimd.memset(ones[:], 1.0).then_inc(consts_ready, 1)
            nc.gpsimd.memset(rt[:], 0.0).then_inc(consts_ready, 1)
            link(nc.gpsimd.memset(p_bias[:], 0.0))
            nc.gpsimd.memset(p_bias[:, :, 0:1], 1.0).then_inc(consts_ready, 1)

            def split(hi, lo, raw, hi_sem, hi_count, done_sem):
                one = ones[:, 0:1].rearrange("p (a b) -> p a b", a=1).broadcast_to(raw.shape)
                nc.gpsimd.tensor_tensor(hi, raw, one, ALU.mult).then_inc(hi_sem, 1)
                pool.wait_ge(hi_sem, hi_count)
                nc.gpsimd.tensor_tensor(lo, raw, hi.bitcast(F32), ALU.subtract).then_inc(done_sem, 1)

            def split_ctx(b):
                pool.wait_ge(d_nat[b % 2], 16 * (b // 2 + 1))
                if b >= 2:
                    pool.wait_ge(mix_done, b - 1)
                split(nat[:, b % 2, HI], nat[:, b % 2, LO], nat_raw[:, b % 2], nat_hi, b + 1, nat_ready)

            def split_w(w, l, r, used=None):
                pool.wait_ge(d_w[w], r * 16 + 16 * (PAIRS * l + 1))
                if used:
                    pool.wait_ge(*used)
                split(wS[:, HI, w], wS[:, LO, w], w_raw[:, w], split_hi[w], r + (PAIRS * l + 1), w_ready[w])

            split_ctx(0)
            split_ctx(1)
            for w in (WK, WV, WQ):
                split_w(w, 0, 0)
            split_ctx(2)
            split_ctx(3)

            def normalise(l, r, k):
                b, h = k // 2, k % 2
                u = unit(l, r, k)
                pool.wait_ge(rz_ready, u - B + 1)
                nc.gpsimd.tensor_tensor(p_pair[:, QT * b:QT * (b + 1), h], eb[:], rz[:], ALU.mult)
                for t in range(QT):
                    ins = nc.gpsimd.tensor_scalar(probs[:, t], probs[:, t], rz[:, t:t + 1], 1.0, ALU.mult, ALU.mult)
                ins.then_inc(norm_done, 1)

            normalise(0, 0, 0)

            def body(l, r, nxt):
                for k in range(UNITS):
                    b = k // 2
                    if k < UNITS - 1:
                        normalise(l, r, k + 1)
                    elif nxt:
                        normalise(nxt[0], nxt[1], 0)
                    if k == 0:
                        split_w(WO, l, r, used=(out_done, ob_out(l, r, -1) + 1))
                    if nxt and k == 5:
                        split_w(WK, *nxt, used=(fill_done, step_fill(l, r, 3, 2) + 1))
                        split_w(WQ, *nxt)
                    if nxt and k == 6:
                        split_w(WV, *nxt, used=(fill_done, step_fill(l, r, 3, 4) + 1))

            def layer(l):
                with pool.Fori(0, PAIRS - 1) as r:
                    body(l, r, (l, r + 1))

            layer(0)
            body(0, PAIRS - 1, (1, 0))
            layer(1)
            body(1, PAIRS - 1, None)
            w1_raw = w_raw[:].rearrange("p w c n -> p (w c n)").rearrange("p (c f) -> p c f", c=DC)
            w2_raw = nat_raw[:].rearrange("p n c d -> p (n c) d")
            pool.wait_ge(d_w0[0], 32)
            split(w1S[:, HI], w1S[:, LO], w1_raw, mlp_hi, 1, mlp_ready)
            pool.wait_ge(d_w0[1], 32)
            split(w2S[:, HI], w2S[:, LO], w2_raw, mlp_hi, 2, mlp_ready)

        @block.scalar
        def _(act):
            def hi_copy(f, dst, src):
                act.wait_ge(fill_done, f + 1)
                return nc.scalar.activation(dst, src, ACT.Copy)

            def hi_biased(f, l, r, dst_src_row):
                act.wait_ge(fill_done, f + 1)
                act.wait_ge(act_bias_ready, r + (PAIRS * l + 1))
                for dst, src, (which, h) in dst_src_row:
                    ins = nc.scalar.activation(dst, src, ACT.Identity, bias=act_bias[:, which, h:h + 1])
                return ins

            def pair_bias(l, r):
                both = vecT[:, l, 0:2 * HEADS].rearrange("p (w h) -> p w h", w=2)
                nc.scalar.activation(act_bias[:], both[:, :, bass.ds(r * 2, 2)], ACT.Copy).then_inc(act_bias_ready, 1)

            def startup_fill(name):
                f = FILL[name]
                pj = proj[f % 2]
                halves = pj[:].rearrange("p (a n) -> p a n", a=2)
                b = int(name[2]) if name[0] in "xc" else 0
                if name == "vec":
                    ins = hi_copy(f, vecT[:], pj[:, 0:2 * P].rearrange("p (a n) -> p a n", a=2))
                elif name == "M":
                    ins = hi_copy(f, mS[:, HI], halves)
                elif name[:2] == "xT":
                    ins = hi_copy(f, hT[:, HI, :, b * LQ:(b + 1) * LQ], halves)
                elif name[:2] == "cT":
                    ins = hi_copy(f, cT[:, HI, int(name[3]), b * T:(b + 1) * T], pj[:])
                elif name == "WoT":
                    ins = hi_copy(f, w0S[:, HI, WO], halves)
                elif name == "N":
                    ins = hi_copy(f, nS[:, HI], halves)
                elif name[0] == "G":
                    ins = hi_copy(f, gS[:, HI], halves)
                elif name[:2] == "RA":
                    l, c = divmod(int(name[2]), CHUNKS)
                    half = pj[:, 0:DC * CHUNK_H * 2].rearrange("p (c h v) -> p c h v", c=DC, v=2)[:, :, :, 0]
                    ins = hi_copy(f, rt_raw[:, l, 0, c], half)
                elif name[:2] == "RB":
                    if name[2] == "1":
                        act.wait_ge(fill_lo, FILL["RB0"] + 1)
                    ins = hi_copy(f, r_full[:], pj[:, 0:D])
                else:
                    return step_fill_hi(f, {"K0": 0, "Q": 1, "K1": 2, "Va": 3, "Vb": 4}[name], 0, 0, 0, f % 2)
                ins.then_inc(fill_hi, 1)

            def step_fill_hi(f, kind, l, r, b, bank):
                pj = proj[bank]
                if kind in (0, 2):
                    h = kind // 2
                    ins = hi_biased(f, l, r, [(kT[:, HI, h], pj[:], (1, h))])
                elif kind == 1:
                    ins = hi_biased(f, l, r, [(qT[:, HI, h], pj[:, h * LQ:(h + 1) * LQ], (0, h)) for h in range(2)])
                else:
                    c = 2 * (kind - 3)
                    ins = hi_copy(f, vS[:, HI, b % 2, c:c + 2], pj[:].rearrange("p (c n) -> p c n", c=2))
                ins.then_inc(fill_hi, 1)

            def probsT_hi(u):
                for j in range(2):
                    act.wait_ge(pt_done, u * 2 + (j + 1))
                    nc.scalar.activation(probsT[:, HI, 2 * j:2 * j + 2], probsT_ps[:, 2 * j:2 * j + 2], ACT.Copy).then_inc(pt_hi, 1)

            def mix_hi_copy(u, dst, src):
                act.wait_ge(mix_done, u + 1)
                nc.scalar.activation(dst, src, ACT.Copy).then_inc(mix_hi, 1)

            def exps0(b):
                act.wait_ge(shift_ready, b + 1)
                for t in range(QT):
                    nc.scalar.activation(probs[:, t], scores[:, t], ACT.Exp, bias=shift[:, t:t + 1], scale=SCALE0,
                                         accum_out=z[:, t:t + 1]).then_inc(exp_done, 1)

            def exps(l, r, k):
                b, h = k // 2, k % 2
                act.wait_ge(shift_ready, unit(l, r, k) + 1)
                for t in range(QT):
                    nc.scalar.activation(probs[:, t], scores[:, t], ACT.Exp, bias=shift[:, t:t + 1], scale=SCALE,
                                         accum_out=z[:, t:t + 1]).then_inc(exp_done, 1)
                for t in range(QT):
                    ins = nc.scalar.activation(eb[:, t:t + 1], nsb[:, QT * b + t, bass.ds(r * 2 + h, 1)], ACT.Exp,
                                               bias=shift[:, t:t + 1], scale=-1.0)
                ins.then_inc(eb_ready, 1)

            def ln_std(n):
                act.wait_ge(var_ready, n + 1)
                nc.scalar.activation(std[:], rstd[:], ACT.Sqrt).then_inc(std_ready, 1)

            def ln_full(n, use, l):
                act.wait_ge(out_done, use + 1)
                if n:
                    act.wait_ge(hT_ready, n)
                g, o = (LN_G, LN_O) if l < 2 else (FC1_B + FC, FC1_B + FC + DC)
                src = out_ps[:].rearrange("p (c q) -> p c q", c=DC)
                for c in range(DC):
                    ins = nc.scalar.activation(h_full[:, c], src[:, c], ACT.Identity, bias=vecT[:, l % 2, o + c:o + c + 1],
                                               scale=vecT[:, l % 2, g + c:g + c + 1])
                ins.then_inc(h_full_ready, 1)

            for n, w in enumerate((WQ, WK)):
                act.wait_ge(d_w0[w], 16)
                nc.scalar.activation(w0S[:, HI, w], w_raw[:, w], ACT.Copy).then_inc(w0_hi, 1)
            for name in pro_fills:
                startup_fill(name)
            act.wait_ge(fill_hi, FILL["vec"] + 1)
            pair_bias(0, 0)
            act.wait_ge(d_w0[WV], 16)
            nc.scalar.activation(w0S[:, HI, WV], w_raw[:, WV], ACT.Copy).then_inc(w0_hi, 1)
            exps0(0)
            for b in range(B):
                ahead, extra = slot_fills[b]
                for name in ahead:
                    startup_fill(name)
                probsT_hi(b)
                if b < B - 1:
                    exps0(b + 1)
                for name in extra:
                    startup_fill(name)
                mix_hi_copy(b, mixT[:, HI], mix_ps[:].rearrange("p (c q) -> p c q", c=DC))
                if b:
                    ln_full(b - 1, 2 * b - 1, 0)
                ln_std(b)
            ln_full(B - 1, 2 * B - 1, 0)
            startup_fill("Q")
            exps(0, 0, 0)
            startup_fill("RB0")
            startup_fill("RB1")

            def body(l, r, nxt):
                last = isinstance(r, int)
                for k in range(UNITS):
                    b, h = k // 2, k % 2
                    u = unit(l, r, k)
                    to = (l, r, b + 1) if b < B - 1 else (nxt + (0,) if nxt else None)
                    if last and h == 1 and b:
                        ln_full(4 * (l + 1) + b - 1, ob_last(l, b - 1, "lnT"), l + 1)
                    probsT_hi(u)
                    if k < UNITS - 1:
                        exps(l, r, k + 1)
                    elif nxt:
                        exps(nxt[0], nxt[1], 0)
                    if last and h == 0 and b:
                        ln_std(4 * (l + 1) + b - 1)
                    kinds = ((0, 1), (2,)) if h == 0 else ((3,), (4,))

                    def fills(kinds):
                        for kind in kinds:
                            if to:
                                step_fill_hi(step_fill(l, r, b + 1, kind), kind, *to, (NF0 + 5 * b + kind) % 2)

                    fills(kinds[0])
                    if last and h == 1:
                        act.wait_ge(out_done, ob_last(l, b, "pbT") + 1)
                        nc.scalar.activation(pbT[:, HI], out_ps[:, 0:LQ], ACT.Copy).then_inc(pbT_hi, 1)
                    mix_hi_copy(u, mixT[:, HI, h], mix_ps[:, 0:LQ])
                    fills(kinds[1])
                    if nxt and k == 5:
                        pair_bias(*nxt)

            for l in range(2):
                with act.Fori(0, PAIRS - 1) as r:
                    body(l, r, (l, r + 1))
                body(l, PAIRS - 1, (1, 0) if l == 0 else None)
                ln_std(4 * (l + 1) + B - 1)
                ln_full(4 * (l + 1) + B - 1, ob_last(l, B - 1, "lnT"), l + 1)

            for half in range(2):
                for f in range(FC):
                    n = half * FC + f
                    act.wait_ge(fill_done, MLP_FILL + n + 1)
                    if n >= 2:
                        act.wait_ge(fill_lo, MLP_FILL + n - 1)
                    nc.scalar.activation(gelu_full[:, n % 2], proj[(MLP_FILL + n) % 2][:], ACT.Gelu,
                                         bias=vecT[:, 0, FC1_B + f:FC1_B + f + 1]).then_inc(fill_hi, 1)


        @block.vector
        def _(dve):
            links = [0]

            def link(ins):
                links[0] += 1
                ins.then_inc(chain, 1)
                dve.wait_ge(chain, links[0])

            def lo_sub(f, dst, src, hi, bias=None):
                dve.wait_ge(fill_hi, f + 1)
                if bias is None:
                    return nc.vector.tensor_tensor(dst, src, hi.bitcast(F32), ALU.subtract)
                return nc.vector.scalar_tensor_tensor(dst, src, bias, hi.bitcast(F32), ALU.add, ALU.subtract)

            def split(hi, lo, full):
                link(nc.vector.tensor_copy(hi, full))
                return nc.vector.tensor_tensor(lo, full, hi.bitcast(F32), ALU.subtract)

            def startup_fill(name):
                f = FILL[name]
                pj = proj[f % 2]
                halves = pj[:].rearrange("p (a n) -> p a n", a=2)
                b = int(name[2]) if name[0] in "xc" else 0
                if name == "vec":
                    dve.wait_ge(fill_hi, f + 1)
                    for l in range(2):
                        v = vecT[:, l]
                        nc.vector.tensor_copy(vt2[:, l, :, 0], v[:, BV:BV + HEADS])
                        nc.vector.tensor_tensor(vt2[:, l, :, 1], v[:, BIAS_V:BIAS_V + HEADS], v[:, BV:BV + HEADS], ALU.subtract)
                        ins = nc.vector.tensor_tensor(bqk[:, l], v[:, BQ:BQ + HEADS], v[:, BIAS_K:BIAS_K + HEADS], ALU.mult)
                elif name == "M":
                    ins = lo_sub(f, mS[:, LO], halves, mS[:, HI])
                elif name[:2] == "xT":
                    ins = lo_sub(f, hT[:, LO, :, b * LQ:(b + 1) * LQ], halves, hT[:, HI, :, b * LQ:(b + 1) * LQ])
                elif name[:2] == "cT":
                    c = int(name[3])
                    ins = lo_sub(f, cT[:, LO, c, b * T:(b + 1) * T], pj[:], cT[:, HI, c, b * T:(b + 1) * T])
                elif name == "WoT":
                    ins = lo_sub(f, w0S[:, LO, WO], halves, w0S[:, HI, WO])
                elif name == "N":
                    ins = lo_sub(f, nS[:, LO], halves, nS[:, HI])
                elif name[0] == "G":
                    ins = lo_sub(f, gS[:, LO], halves, gS[:, HI])
                elif name[:2] == "RA":
                    n = int(name[2])
                    l, c = divmod(n, CHUNKS)
                    dve.wait_ge(d_wq, 16 * (n + 1))
                    dve.wait_ge(d_bk, 16 * (n + 1))
                    for i in range(DC):
                        ins = nc.vector.tensor_tensor(ck_wq[:, i], ck_wq[:, i], ck_bk[:], ALU.mult)
                    link(ins)
                    nc.vector.reduce_sum(wb_full[:, l, :, c * CHUNK_H:(c + 1) * CHUNK_H],
                                         ck_wq[:].rearrange("p c (h k) -> p c h k", k=DH), AX_X).then_inc(wb_used, 1)
                    dve.wait_ge(fill_hi, f + 1)
                    if c == CHUNKS - 1:
                        dve.wait_ge(wb_used, n + 1)
                        split(wbS[:, HI, l], wbS[:, LO, l], wb_full[:, l]).then_inc(wb_ready, 1)
                    half = pj[:, 0:DC * CHUNK_H * 2].rearrange("p (c h v) -> p c h v", c=DC, v=2)[:, :, :, 1]
                    ins = nc.vector.tensor_copy(rt_raw[:, l, 1, c], half)
                elif name[:2] == "RB":
                    l = int(name[2])
                    dve.wait_ge(fill_hi, f + 1)
                    dve.wait_ge(d_small, 64)
                    link(nc.vector.tensor_tensor(r_full[0:1, :], r_full[0:1, :], bo_row[0:1, l, :], ALU.add))
                    ins = split(rS[:, HI, l], rS[:, LO, l], r_full[:])
                else:
                    return step_fill_lo(f, {"K0": 0, "Q": 1, "K1": 2, "Va": 3, "Vb": 4}[name], 0, 0, 0, f % 2)
                ins.then_inc(fill_lo, 1)

            def r_columns(l):
                if l:
                    dve.wait_ge(fill_done, FILL["RB0"] + 1)
                dve.wait_ge(consts_ready, 5)
                for c in range(DC):
                    nc.vector.tensor_reduce(rt[:, c, 0:1], rt_raw[:, l, 0, :, c], mybir.AxisListType.XY, ALU.add)
                    ins = nc.vector.tensor_copy(rt[:, c, 1:1 + HEADS].rearrange("p (k h) -> p k h", k=CHUNKS), rt_raw[:, l, 1, :, c])
                ins.then_inc(rt_ready, 1)

            def step_fill_lo(f, kind, l, r, b, bank):
                pj = proj[bank]
                if kind in (0, 2):
                    h = kind // 2
                    ins = lo_sub(f, kT[:, LO, h], pj[:], kT[:, HI, h], vecT[:, l, bass.ds(r * 2 + (BK + h), 1)])
                elif kind == 1:
                    for h in range(2):
                        ins = lo_sub(f, qT[:, LO, h], pj[:, h * LQ:(h + 1) * LQ], qT[:, HI, h], vecT[:, l, bass.ds(r * 2 + (BQ + h), 1)])
                else:
                    c = 2 * (kind - 3)
                    ins = lo_sub(f, vS[:, LO, b % 2, c:c + 2], pj[:].rearrange("p (c n) -> p c n", c=2), vS[:, HI, b % 2, c:c + 2])
                ins.then_inc(fill_lo, 1)

            def probsT_lo(u):
                for j in range(2):
                    dve.wait_ge(pt_hi, u * 2 + (j + 1))
                    nc.vector.tensor_tensor(probsT[:, LO, 2 * j:2 * j + 2], probsT_ps[:, 2 * j:2 * j + 2],
                                            probsT[:, HI, 2 * j:2 * j + 2].bitcast(F32), ALU.subtract).then_inc(pt_lo, 1)

            def mix_lo_sub(u, dst, src, hi):
                dve.wait_ge(mix_hi, u + 1)
                nc.vector.tensor_tensor(dst, src, hi.bitcast(F32), ALU.subtract).then_inc(mix_lo, 1)

            def maxima(u):
                dve.wait_ge(scores_done, u + 1)
                nc.vector.reduce_max(mx[:], scores[:], AX_X).then_inc(max_ready, 1)
                dve.wait_ge(max_ready, u + 1)

            def shift0(b):
                maxima(b)
                nc.vector.tensor_scalar(shift[:], mx[:], -SCALE0, None, ALU.mult).then_inc(shift_ready, 1)

            def shifts(l, r, k):
                b, h = k // 2, k % 2
                maxima(unit(l, r, k))
                nc.vector.scalar_tensor_tensor(shift[:].rearrange("p (t a) -> p t a", a=1),
                                               mx[:].rearrange("p (t a) -> p t a", a=1), -SCALE,
                                               nsb[:, QT * b:QT * (b + 1), bass.ds(r * 2 + h, 1)],
                                               ALU.mult, ALU.min).then_inc(shift_ready, 1)

            def sums(l, r, k):
                u = unit(l, r, k)
                dve.wait_ge(eb_ready, u - B + 1)
                nc.vector.tensor_tensor(zsum[:], z[:], eb[:], ALU.add).then_inc(zsum_ready, 1)
                dve.wait_ge(zsum_ready, u - B + 1)
                nc.vector.reciprocal(rz[:], zsum[:]).then_inc(rz_ready, 1)

            def pair_weights(l, r, b0, b1):
                dve.wait_ge(norm_done, unit(l, r, 2 * b1) - B)
                tiles = slice(QT * b0, QT * b1)
                nc.vector.tensor_tensor(p_bias[:, tiles, bass.ds(r * 2 + 1, 2)], p_pair[:, tiles], p_pair[:, tiles], ALU.max).then_inc(pb_ready, 1)

            def add_out(use, b):
                dve.wait_ge(out_done, use + 1)
                xb = x[:, QT * b:QT * (b + 1)]
                nc.vector.tensor_tensor(xb, out_ps[:].rearrange("p (t n) -> p t n", t=QT), xb, ALU.add).then_inc(out_free, 1)

            def ln_var(use, b):
                dve.wait_ge(out_free, use + 1)
                for t in range(QT):
                    ins = nc.vector.bn_stats(bn[:, t], x[:, QT * b + t])
                link(ins)
                for t in range(QT):
                    ins = nc.vector.bn_aggr(mv[:, t], bn[:, t])
                link(ins)
                nc.vector.tensor_scalar(rstd[:], mv[:, :, 1], EPS, None, ALU.add).then_inc(var_ready, 1)

            def ln_x(n, b, mlp=False):
                dve.wait_ge(std_ready, n + 1)
                link(nc.vector.reciprocal(rstd[:], std[:]))
                for t in range(QT):
                    ins = nc.vector.tensor_scalar(xn[:, t], x[:, QT * b + t], mv[:, t, 0:1], rstd[:, t:t + 1], ALU.subtract, ALU.mult)
                ins.then_inc(xn_ready, 1)
                if mlp:
                    for t in range(QT):
                        nc.vector.tensor_tensor(x[:, QT * b + t], x[:, QT * b + t], b2_row[:], ALU.add)

            def ln_split(n, use, b):
                dve.wait_ge(h_full_ready, n + 1)
                hi, lo = (hT[:, s, :, b * LQ:(b + 1) * LQ] for s in (HI, LO))
                nc.vector.tensor_copy(hi, h_full[:]).then_inc(out_free, 1)
                dve.wait_ge(out_free, use + 1)
                nc.vector.tensor_tensor(lo, h_full[:], hi.bitcast(F32), ALU.subtract).then_inc(hT_ready, 1)

            def bias_logits(use, b):
                dve.wait_ge(out_done, use + 1)
                nc.vector.tensor_scalar(nsb[:, QT * b:QT * (b + 1)],
                                        out_ps[:, 0:QT * HEADS].rearrange("p (t h) -> p t h", t=QT),
                                        -SCALE, None, ALU.mult).then_inc(out_free, 1)

            for n, w in enumerate((WQ, WK)):
                dve.wait_ge(w0_hi, n + 1)
                nc.vector.tensor_tensor(w0S[:, LO, w], w_raw[:, w], w0S[:, HI, w].bitcast(F32), ALU.subtract).then_inc(w0_ready, 1)
            for name in pro_fills:
                startup_fill(name)
            dve.wait_ge(w0_hi, 3)
            nc.vector.tensor_tensor(w0S[:, LO, WV], w_raw[:, WV], w0S[:, HI, WV].bitcast(F32), ALU.subtract).then_inc(w0_ready, 1)
            dve.wait_ge(d_small, 64)
            dve.wait_ge(d_x, 16)

            def sums0(b):
                dve.wait_ge(exp_done, 2 * b + 2)
                link(nc.vector.reciprocal(rz0[:, b], z[:]))
                link(nc.vector.tensor_scalar(rz0[:, b], rz0[:, b], alpha[:], None, ALU.mult))

            shift0(0)
            sums0(0)
            for b in range(B):
                ahead, extra = slot_fills[b]
                for name in ahead:
                    startup_fill(name)
                if b < B - 1:
                    shift0(b + 1)
                probsT_lo(b)
                if b < B - 1:
                    sums0(b + 1)
                for name in extra:
                    startup_fill(name)
                mix_lo_sub(b, mixT[:, LO], mix_ps[:].rearrange("p (c q) -> p c q", c=DC), mixT[:, HI])
                if b:
                    ln_split(b - 1, 2 * b - 1, b - 1)
                dve.wait_ge(out_done, 2 * b + 1)
                for t in range(QT):
                    xt = x[:, QT * b + t]
                    ins = nc.vector.scalar_tensor_tensor(xt, out_ps[:, t * D:(t + 1) * D], rz0[:, b, t:t + 1], xt, ALU.mult, ALU.add)
                ins.then_inc(out_free, 1)
                ln_var(2 * b, b)
                ln_x(b, b)
            ln_split(B - 1, 2 * B - 1, B - 1)
            startup_fill("Q")
            for b in range(B):
                bias_logits(2 * B + b, b)
            shifts(0, 0, 0)
            sums(0, 0, 0)
            r_columns(0)
            startup_fill("RB0")
            r_columns(1)
            startup_fill("RB1")

            def body(l, r, nxt):
                last = isinstance(r, int)
                for k in range(UNITS):
                    b, h = k // 2, k % 2
                    u = unit(l, r, k)
                    to = (l, r, b + 1) if b < B - 1 else (nxt + (0,) if nxt else None)
                    after = (l, r, k + 1) if k < UNITS - 1 else (nxt + (0,) if nxt else None)
                    if after:
                        shifts(*after)
                    probsT_lo(u)
                    if h == 0 and b:
                        add_out(ob_use(l, r, b - 1), b - 1)
                        if last:
                            ln_var(ob_last(l, b - 1, "out"), b - 1)
                    if last and h == 1 and b:
                        ln_split(4 * (l + 1) + b - 1, ob_last(l, b - 1, "lnT"), b - 1)
                    if last and h == 1:
                        pair_weights(l, r, b, b + 1)
                    elif k == UNITS - 1:
                        pair_weights(l, r, 0, B)
                    if after:
                        sums(*after)
                    kinds = ((0, 1), (2,)) if h == 0 else ((3,), (4,))

                    def fills(kinds):
                        for kind in kinds:
                            if to:
                                step_fill_lo(step_fill(l, r, b + 1, kind), kind, *to, (NF0 + 5 * b + kind) % 2)

                    fills(kinds[0])
                    if last and h == 0 and b:
                        ln_x(4 * (l + 1) + b - 1, b - 1, mlp=l == 1)
                    if last and h == 1:
                        if b and l == 0:
                            bias_logits(ob_last(l, b - 1, "sb"), b - 1)
                        dve.wait_ge(pbT_hi, B * l + b + 1)
                        nc.vector.tensor_tensor(pbT[:, LO], out_ps[:, 0:LQ], pbT[:, HI].bitcast(F32), ALU.subtract).then_inc(out_free, 1)
                    mix_lo_sub(u, mixT[:, LO, h], mix_ps[:, 0:LQ], mixT[:, HI, h])
                    fills(kinds[1])
                add_out(ob_use(l, r, B - 1), B - 1)

            for l in range(2):
                with dve.Fori(0, PAIRS - 1) as r:
                    body(l, r, (l, r + 1))
                body(l, PAIRS - 1, (1, 0) if l == 0 else None)
                n = 4 * (l + 1) + B - 1
                ln_var(ob_last(l, B - 1, "out"), B - 1)
                ln_x(n, B - 1, mlp=l == 1)
                ln_split(n, ob_last(l, B - 1, "lnT"), B - 1)
                if l == 0:
                    bias_logits(ob_last(l, B - 1, "sb"), B - 1)

            for half in range(2):
                for f in range(FC):
                    n = half * FC + f
                    dve.wait_ge(fill_hi, MLP_FILL + n + 1)
                    link(nc.vector.tensor_copy(gelu_hi[:, f], gelu_full[:, n % 2]))
                    nc.vector.tensor_tensor(gelu_lo[:, f], gelu_full[:, n % 2], gelu_hi[:, f].bitcast(F32), ALU.subtract).then_inc(fill_lo, 1)
                for i in range(2):
                    b = 2 * half + i
                    dve.wait_ge(down_done, b + 1)
                    xb = x[:, QT * b:QT * (b + 1)]
                    bank = (out_ps, mix_ps)[i]
                    nc.vector.tensor_tensor(xb, bank[:].rearrange("p (t n) -> p t n", t=QT), xb, ALU.add).then_inc(result_ready, 1)

        @block.tensor
        def _(pe):
            def product(out, pairs):
                n = len(pairs) * len(PASSES)
                i = 0
                for a, b_ in pairs:
                    for s, t in PASSES:
                        ins = nc.tensor.matmul(out, a(s), b_(t), start=(i == 0), stop=(i == n - 1))
                        i += 1
                return ins

            def fill_bank(f):
                if isinstance(f, int) and f < 2:
                    return
                pe.wait_ge(fill_lo, f - 1)

            def startup_fill(name):
                f = FILL[name]
                pj = proj[f % 2]
                b = int(name[2]) if name[0] in "xc" else 0
                fill_bank(f)
                if name == "vec":
                    pe.wait_ge(consts_ready, 5)
                    pe.wait_ge(d_vec, 17 * 16)
                    for l in range(2):
                        ins = nc.tensor.transpose(pj[:, l * P:(l + 1) * P], vec_raw[:, l], ident[:])
                elif name == "M":
                    pe.wait_ge(w0_ready, 2)
                    for i in range(DC):
                        ins = product(pj[:, i * D:(i + 1) * D],
                                      [(lambda s, o=o: w0S[:, s, WQ, o, i * P:(i + 1) * P], lambda s, o=o: w0S[:, s, WK, o]) for o in range(DC)])
                elif name[:2] == "xT":
                    pe.wait_ge(d_x, 16)
                    for c in range(DC):
                        for t in range(QT):
                            ins = nc.tensor.transpose(pj[:, (c * QT + t) * P:(c * QT + t + 1) * P], x[:, QT * b + t, c * P:(c + 1) * P], ident[:])
                elif name[:2] == "cT":
                    c = int(name[3])
                    pe.wait_ge(d_nat[b % 2], 16 * (b // 2 + 1))
                    for t in range(TC):
                        ins = nc.tensor.transpose(pj[:, t * P:(t + 1) * P], nat_raw[:, b % 2, t, c * P:(c + 1) * P], ident[:])
                elif name == "WoT":
                    pe.wait_ge(d_w0[WO], 16)
                    for v in range(DC):
                        for o in range(DC):
                            ins = nc.tensor.transpose(pj[:, (v * DC + o) * P:(v * DC + o + 1) * P], w_raw[:, WO, o, v * P:(v + 1) * P], ident[:])
                elif name == "N":
                    pe.wait_ge(w0_ready, 3)
                    pe.wait_ge(fill_lo, FILL["WoT"] + 1)
                    for i in range(DC):
                        ins = product(pj[:, i * D:(i + 1) * D],
                                      [(lambda s, v=v: w0S[:, s, WV, v, i * P:(i + 1) * P], lambda s, v=v: w0S[:, s, WO, v]) for v in range(DC)])
                elif name[0] == "G":
                    b = int(name[1])
                    pe.wait_ge(fill_lo, max(FILL["M"], FILL[f"xT{b}"]) + 1)
                    for j in range(DC):
                        ins = product(pj[:, j * LQ:(j + 1) * LQ],
                                      [(lambda s, i=i: mS[:, s, i, j * P:(j + 1) * P], lambda s, i=i: hT[:, s, i, b * LQ:(b + 1) * LQ]) for i in range(DC)])
                elif name[:2] == "RA":
                    n = int(name[2])
                    pe.wait_ge(d_wo, 16 * (n + 1))
                    l, ck = divmod(n, CHUNKS)
                    for c in range(DC):
                        for h in range(CHUNK_H):
                            at = (c * CHUNK_H + h) * 2
                            ins = nc.tensor.matmul(pj[:, at:at + 2], ck_wo[:, h, c * P:(c + 1) * P], vt2[:, l, ck * CHUNK_H + h, :], start=True, stop=True)
                elif name[:2] == "RB":
                    pe.wait_ge(rt_ready, int(name[2]) + 1)
                    for c in range(DC):
                        ins = nc.tensor.transpose(pj[:, c * P:(c + 1) * P], rt[:, c], ident[:])
                else:
                    return step_fill_mm(f, {"K0": 0, "Q": 1, "K1": 2, "Va": 3, "Vb": 4}[name], 0, 0, 0, f % 2, wait=False)
                ins.then_inc(fill_done, 1)

            def step_fill_mm(f, kind, l, r, b, bank, wait=True):
                pj = proj[bank]
                if wait:
                    fill_bank(f)
                if b == 0:
                    w = {0: WK, 1: WQ, 3: WV}.get(kind)
                    if w is not None:
                        pe.wait_ge(w_ready[w], r + (PAIRS * l + 1))
                if kind in (0, 2):
                    h = kind // 2
                    ins = product(pj[:], [(lambda s, c=c: wS[:, s, WK, c, h * DH:(h + 1) * DH], lambda s, c=c: cT[:, s, c, b * T:(b + 1) * T]) for c in range(DC)])
                elif kind == 1:
                    for h in range(2):
                        ins = product(pj[:, h * LQ:(h + 1) * LQ],
                                      [(lambda s, c=c: wS[:, s, WQ, c, h * DH:(h + 1) * DH], lambda s, c=c: hT[:, s, c, b * LQ:(b + 1) * LQ]) for c in range(DC)])
                else:
                    for j in range(2):
                        at = b * T + (2 * (kind - 3) + j) * P
                        ins = product(pj[:, j * PW:(j + 1) * PW],
                                      [(lambda s, c=c: cT[:, s, c, at:at + P], lambda s, c=c: wS[:, s, WV, c]) for c in range(DC)])
                ins.then_inc(fill_done, 1)

            def unit_scores(l, r, k, ready):
                h = k % 2
                u = unit(l, r, k)
                pe.wait_ge(fill_lo, ready + 1)
                pe.wait_ge(exp_done, u * 2)
                for t in range(QT):
                    ins = product(scores[:, t], [(lambda s: qT[:, s, h, t * P:(t + 1) * P], lambda s: kT[:, s, h])])
                ins.then_inc(scores_done, 1)

            def transposes(u):
                for j in range(2):
                    if not (isinstance(u, int) and u == 0):
                        pe.wait_ge(pt_lo, u * 2 + (j - 1))
                    for c in (2 * j, 2 * j + 1):
                        for t in range(QT):
                            ins = nc.tensor.transpose(probsT_ps[:, c, t * P:(t + 1) * P], probs[:, t, c * P:(c + 1) * P], ident[:])
                    ins.then_inc(pt_done, 1)

            def mix(l, r, k, ready):
                b, h = k // 2, k % 2
                u = unit(l, r, k)
                pe.wait_ge(mix_lo, u)
                if ready is not None:
                    pe.wait_ge(fill_lo, ready + 1)
                n = 0
                for c in range(TC):
                    if c % 2 == 0:
                        pe.wait_ge(pt_lo, u * 2 + (c // 2 + 1))
                    for s, t in PASSES:
                        ins = nc.tensor.matmul(mix_ps[:, 0:LQ], vS[:, s, b % 2, c, h * DH:(h + 1) * DH], probsT[:, t, c],
                                               start=(n == 0), stop=(n == 3 * TC - 1))
                        n += 1
                ins.then_inc(mix_done, 1)

            def step_out(l, r, b):
                last = isinstance(r, int)
                pe.wait_ge(mix_lo, unit(l, r, 2 * b + 2))
                if b == 0:
                    pe.wait_ge(w_ready[WO], r + (PAIRS * l + 1))
                use = ob_use(l, r, b)
                pe.wait_ge(out_free, use)
                for t in range(QT):
                    terms = [(lambda s, h=h: mixT[:, s, h, t * P:(t + 1) * P], lambda s, h=h: wS[:, s, WO, h]) for h in range(2)]
                    if last:
                        terms.append((lambda s: pbT[:, s, t * P:(t + 1) * P], lambda s: rS[:, s, l]))
                    ins = product(out_ps[:, t * D:(t + 1) * D], terms)
                ins.then_inc(out_done, 1)

            def ln_transposes(n, use):
                pe.wait_ge(xn_ready, n + 1)
                pe.wait_ge(out_free, use)
                for c in range(DC):
                    for t in range(QT):
                        ins = nc.tensor.transpose(out_ps[:, (c * QT + t) * P:(c * QT + t + 1) * P], xn[:, t, c * P:(c + 1) * P], ident[:])
                ins.then_inc(out_done, 1)

            def bias_logits(n, use, l, b):
                pe.wait_ge(hT_ready, n + 1)
                pe.wait_ge(out_free, use)
                pe.wait_ge(wb_ready, l + 1)
                for t in range(QT):
                    out = out_ps[:, t * HEADS:(t + 1) * HEADS]
                    i = 0
                    for c in range(DC):
                        for s, s2 in PASSES:
                            nc.tensor.matmul(out, hT[:, s, c, b * LQ + t * P:b * LQ + (t + 1) * P], wbS[:, s2, l, c], start=(i == 0), stop=False)
                            i += 1
                    ins = nc.tensor.matmul(out, ones[:], bqk[:, l], start=False, stop=True)
                ins.then_inc(out_done, 1)

            def scores0(b):
                pe.wait_ge(fill_lo, FILL[f"G{b}"] + 1)
                if b:
                    pe.wait_ge(exp_done, 2 * b)
                for t in range(QT):
                    ins = product(scores[:, t], [(lambda s, j=j: gS[:, s, j, t * P:(t + 1) * P], lambda s, j=j: cT[:, s, j, b * T:(b + 1) * T])
                                                 for j in range(DC)])
                ins.then_inc(scores_done, 1)

            for name in pro_fills:
                startup_fill(name)
            scores0(0)
            for b in range(B):
                ahead, extra = slot_fills[b]
                for name in ahead:
                    startup_fill(name)
                if b < B - 1:
                    scores0(b + 1)
                pe.wait_ge(exp_done, 2 * b + 2)
                transposes(b)
                for name in extra:
                    startup_fill(name)
                pe.wait_ge(nat_ready, b + 1)
                if b:
                    pe.wait_ge(mix_lo, b)
                pe.wait_ge(pt_lo, 2 * b + 2)
                for i in range(DC):
                    ins = product(mix_ps[:, i * LQ:(i + 1) * LQ],
                                  [(lambda s, c=c: nat[:, b % 2, s, c, i * P:(i + 1) * P], lambda s, c=c: probsT[:, s, c]) for c in range(TC)])
                ins.then_inc(mix_done, 1)
                if b:
                    ln_transposes(b - 1, 2 * b - 1)
                pe.wait_ge(mix_lo, b + 1)
                if b:
                    pe.wait_ge(out_free, 2 * b)
                for t in range(QT):
                    ins = product(out_ps[:, t * D:(t + 1) * D],
                                  [(lambda s, i=i: mixT[:, s, i, t * P:(t + 1) * P], lambda s, i=i: nS[:, s, i]) for i in range(DC)])
                ins.then_inc(out_done, 1)
            ln_transposes(B - 1, 2 * B - 1)
            pe.wait_ge(hT_ready, 1)
            startup_fill("Q")
            for b in range(B):
                bias_logits(b, 2 * B + b, 0, b)
            unit_scores(0, 0, 0, FILL["Q"])
            startup_fill("RB0")
            startup_fill("RB1")

            def body(l, r, nxt):
                last = isinstance(r, int)
                for k in range(UNITS):
                    b, h = k // 2, k % 2
                    u = unit(l, r, k)
                    to = (l, r, b + 1) if b < B - 1 else (nxt + (0,) if nxt else None)
                    after = (l, r, k + 1) if k < UNITS - 1 else (nxt + (0,) if nxt else None)
                    if after:
                        unit_scores(*after, step_fill(l, r, b, 2) if h == 0 else step_fill(l, r, b + 1, 1))
                    pe.wait_ge(norm_done, u - B + 1)
                    transposes(u)

                    def fill(kind):
                        if to:
                            step_fill_mm(step_fill(l, r, b + 1, kind), kind, *to, (NF0 + 5 * b + kind) % 2)

                    if h == 0:
                        fill(0)
                        fill(1)
                        mix(l, r, k, step_fill(l, r, b, 4))
                        if last and b:
                            ln_transposes(4 * (l + 1) + b - 1, ob_last(l, b - 1, "lnT"))
                        fill(2)
                    else:
                        fill(3)
                        if last:
                            if b and l == 0:
                                bias_logits(4 * (l + 1) + b - 1, ob_last(l, b - 1, "sb"), 1, b - 1)
                            pe.wait_ge(out_free, ob_last(l, b, "pbT"))
                            pe.wait_ge(pb_ready, (PAIRS - 1 + B) * l + PAIRS + b)
                            for t in range(QT):
                                ins = nc.tensor.transpose(out_ps[:, t * P:(t + 1) * P], p_bias[:, QT * b + t], ident[:])
                            ins.then_inc(out_done, 1)
                        mix(l, r, k, None)
                        fill(4)
                        step_out(l, r, b)

            for l in range(2):
                with pe.Fori(0, PAIRS - 1) as r:
                    body(l, r, (l, r + 1))
                body(l, PAIRS - 1, (1, 0) if l == 0 else None)
                n = 4 * (l + 1) + B - 1
                ln_transposes(n, ob_last(l, B - 1, "lnT"))
                if l == 0:
                    bias_logits(n, ob_last(l, B - 1, "sb"), 1, B - 1)

            for half in range(2):
                for f in range(FC):
                    n = half * FC + f
                    fill_bank(MLP_FILL + n)
                    if n == 0:
                        pe.wait_ge(mlp_ready, 1)
                    if f == 0:
                        pe.wait_ge(hT_ready, 8 + 2 * half + 2)
                    ins = product(proj[(MLP_FILL + n) % 2][:],
                                  [(lambda s, c=c: w1S[:, s, c, f * P:(f + 1) * P], lambda s, c=c: hT[:, s, c, half * 2 * LQ:(half + 1) * 2 * LQ]) for c in range(DC)])
                    ins.then_inc(fill_done, 1)
                if half == 0:
                    pe.wait_ge(mlp_ready, 2)
                pe.wait_ge(fill_lo, MLP_FILL + (half + 1) * FC)
                if half == 0:
                    pe.wait_ge(out_free, OB_MLP)
                for i in range(2):
                    b = 2 * half + i
                    if half:
                        pe.wait_ge(result_ready, b - 1)
                    gelu = (gelu_hi, gelu_lo)
                    for t in range(QT):
                        q0 = i * LQ + t * P
                        ins = product((out_ps, mix_ps)[i][:, t * D:(t + 1) * D],
                                      [(lambda s, f=f: gelu[s][:, f, q0:q0 + P], lambda s, f=f: w2S[:, s, f]) for f in range(FC)])
                    ins.then_inc(down_done, 1)


_INS = (["x", "ctx_2048", "L0_xattn_w_q", "L0_xattn_w_k", "L0_xattn_w_v", "L0_xattn_w_o", "L0_xattn_alpha"]
        + [f"L1_xattn_{n}{i}{s}" for i in (1, 2) for n, s in (("ln", "_scale"), ("ln", "_offset"), ("wq", ""), ("bq", ""), ("wk", ""),
           ("bk", ""), ("wv", ""), ("bv", ""), ("wo", ""), ("bo", ""), ("bias_k", ""), ("bias_v", ""))]
        + ["L1_xattn_ln_mlp_scale", "L1_xattn_ln_mlp_offset", "L1_xattn_w_fc1", "L1_xattn_b_fc1", "L1_xattn_w_fc2", "L1_xattn_b_fc2"])


def kernel(**inputs):
    import numpy as _np
    import concourse.bacc as _bacc
    from concourse import mybir as _mybir
    from concourse.bass_utils import run_bass_kernel_spmd as _run

    nc = _bacc.Bacc("TRN2", target_bir_lowering=False, num_devices=1)
    arrays, aps = {}, {}
    for name in _INS:
        a = _np.ascontiguousarray(inputs[name])
        if a.ndim == 0:
            a = a.reshape(1)
        arrays[f"in_{name}_dram"] = a
        aps[name] = nc.dram_tensor(f"in_{name}_dram", a.shape, _mybir.dt.from_np(a.dtype), kind="ExternalInput").ap()
    aps["out"] = nc.dram_tensor("out_0_dram", (B, LQ, D), _mybir.dt.float32, kind="ExternalOutput").ap()
    xattn_kernel(nc, aps)
    r = _run(nc, [arrays], core_ids=[0])
    return r.results[0]["out_0_dram"]
```

```python
from contextlib import ExitStack

import concourse.bass as bass
from concourse import mybir

F32 = mybir.dt.float32
F32R = mybir.dt.float32r
ALU = mybir.AluOpType
ACT = mybir.ActivationFunctionType
AX_X = mybir.AxisListType.X

P = 128
B, LQ, D = 4, 256, 256
T = 512
HEADS, DH = 16, 128
F = 1024
QT = LQ // P
DC = D // P
TC = T // P
FC = F // P
PAIRS = HEADS // 2
PW = 2 * DH
UNITS = 2 * B
EPS = 1e-5
SCALE0 = float(D) ** -0.5
SCALE = float(DH) ** -0.5
WK, WQ, WV, WO = range(4)
HI, LO = 0, 1
PASSES = ((HI, LO), (LO, HI), (HI, HI))
BQ, BK, BV, BIAS_K, BIAS_V, LN_G, LN_O, FC1_B = 0, 16, 32, 48, 64, 80, 82, 84
CHUNK_H = 4
CHUNKS = HEADS // CHUNK_H


def startup_fills():
    first = ["xT0", "cT00", "cT01", "M", "G0"]
    second = ["xT1", "cT10", "cT11", "G1"]
    slots = []
    for b in range(B):
        ahead = [f"xT{b+2}", f"cT{b+2}0", f"cT{b+2}1", f"G{b+2}"] if b < B - 2 else []
        slots.append((["vec", "WoT", "N"] if b == 0 else []) + ahead + [[], ["K0", "K1"], ["Va", "Vb", "RA0"], ["RA1", "RA2"]][b])
    tail = ["Q", "RA3", "RB0"]
    return first, second, slots, tail, first + second + sum(slots, []) + tail


def xattn_kernel(nc, A):
    first_fills, second_fills, slot_fills, tail_fills, fill_order = startup_fills()
    FILL = {name: n for n, name in enumerate(fill_order)}
    NF0 = len(fill_order)
    MLP_FILL = NF0 + 2 * 5 * B * PAIRS - 5

    def unit(l, r, k):
        return r * UNITS + (B + UNITS * PAIRS * l + k)

    def step_fill(l, r, b, f):
        return r * (5 * B) + (NF0 + 5 * B * PAIRS * l + 5 * b + f - 5)

    USES0 = ["delta0", "lnT0", "delta1", "lnT1", "delta2", "lnT2", "delta3", "sb0", "sb1", "sb2", "lnT3", "sb3"]
    LAST = [["pbT0", "out0", "ra", "lnT0", "pbT1", "out1", "sb0", "lnT1", "pbT2", "out2", "sb1", "lnT2",
             "pbT3", "out3", "sb2", "lnT3", "sb3", "rb"],
            ["pbT0", "out0", "lnT0", "pbT1", "out1", "lnT1", "pbT2", "out2", "lnT2", "pbT3", "out3", "lnT3"]]
    PER_PAIR = [B + 1, B]
    LOOP_AT = [len(USES0), len(USES0) + PER_PAIR[0] * (PAIRS - 1) + len(LAST[0])]
    LAST_AT = [LOOP_AT[l] + PER_PAIR[l] * (PAIRS - 1) for l in range(2)]

    def use0(what):
        return USES0.index(what)

    def use_last(l, what):
        return LAST_AT[l] + LAST[l].index(what)

    def use_out(l, r, b):
        if isinstance(r, int) and r == PAIRS - 1:
            return use_last(l, f"out{b}")
        return r * PER_PAIR[l] + (LOOP_AT[l] + (b + 1 if l == 0 and b else b))

    def use_ra(r):
        return use_last(0, "ra") if isinstance(r, int) else r * PER_PAIR[0] + (LOOP_AT[0] + 1)

    USES = LAST_AT[1] + len(LAST[1])
    with ExitStack() as ctx:
        def sb(name, shape, dt=F32):
            return ctx.enter_context(nc.sbuf_tensor(name, shape, dt))

        def ps(name, shape):
            return ctx.enter_context(nc.psum_tensor(name, shape, F32))

        def sem(name):
            return ctx.enter_context(nc.semaphore(name))

        scores = ps("scores", [P, QT, T])
        probsT_ps = ps("probsT_ps", [P, TC, LQ])
        proj = [ps(f"proj{i}", [P, 512]) for i in range(2)]
        mix_ps = ps("mix_ps", [P, 512])
        out_ps = ps("out_ps", [P, 512])

        cT = sb("cT", [P, 2, DC, B * T], F32R)
        hT = sb("hT", [P, 2, DC, B * LQ], F32R)
        wS = sb("wS", [P, 2, 4, DC, PW], F32R)
        kT = sb("kT", [P, 2, 2, T], F32R)
        qT = sb("qT", [P, 2, 2, LQ], F32R)
        vS = sb("vS", [P, 2, 2, TC, PW], F32R)
        probsT = sb("probsT", [P, 2, TC, LQ], F32R)
        mixT = sb("mixT", [P, 2, 2, LQ], F32R)
        arena = sb("arena", [P, 8192], F32R)
        nat = arena[:, 0:4096].rearrange("p (n s c d) -> p n s c d", n=2, s=2, c=TC)
        w0S = arena[:, 4096:8192].rearrange("p (s w c d) -> p s w c d", s=2, w=4, c=DC)
        w1S = arena[:, 0:4096].rearrange("p (s c f) -> p s c f", s=2, c=DC)
        w2S = arena[:, 4096:8192].rearrange("p (s c d) -> p s c d", s=2, c=FC)
        nS = w0S[:, :, WK]
        mS = sb("mS", [P, 2, DC, D], F32R)
        gS = sb("gS", [P, 2, DC, LQ], F32R)
        rS = sb("rS", [P, 2, 2, D], F32R)
        wbS = sb("wbS", [P, 2, 2, DC, HEADS], F32R)
        pbT = sb("pbT", [P, 2, LQ], F32R)
        gelu_hi = vS[:].rearrange("p s n c d -> p (s n c d)").rearrange("p (f q) -> p f q", f=FC)
        gelu_lo = wS[:].rearrange("p s w c d -> p (s w c d)").rearrange("p (f q) -> p f q", f=FC)

        x = sb("x", [P, B * QT, D])
        w_raw = sb("w_raw", [P, 4, DC, PW])
        nat_raw = sb("nat_raw", [P, 2, TC, D])
        ck_wq = sb("ck_wq", [P, DC, CHUNK_H * DH])
        ck_wo = sb("ck_wo", [P, CHUNK_H, D])
        ck_bk = sb("ck_bk", [P, CHUNK_H * DH])
        probs = sb("probs", [P, QT, T])
        gelu_full = probs
        xn = sb("xn", [P, QT, D])
        h_full = sb("h_full", [P, DC, LQ])
        p_bias = sb("p_bias", [P, B * QT, P])
        vec_raw = sb("vec_raw", [P, 2, P])
        vecT = sb("vecT", [P, 2, P])
        ident = sb("ident", [P, P])
        ones = sb("ones", [P, P])
        b2_row = sb("b2_row", [P, D])
        bo_row = sb("bo_row", [P, 2, D])
        alpha = sb("alpha", [P, 1])
        vt2 = sb("vt2", [P, 2, HEADS, 2])
        bqk = sb("bqk", [P, 2, HEADS])
        wb_full = sb("wb_full", [P, 2, DC, HEADS])
        rt_raw = sb("rt_raw", [P, 2, 2, DC, HEADS])
        rt = sb("rt", [P, DC, P])
        r_full = sb("r_full", [P, D])
        wb_two = sb("wb_two", [P, DC, 2])
        p_pair = sb("p_pair", [P, B * QT, 2])
        act_bias = sb("act_bias", [P, 2, 2])
        nsb = sb("nsb", [P, B * QT, HEADS])
        mx = sb("mx", [P, QT])
        shift = sb("shift", [P, QT])
        z = sb("z", [P, QT])
        eb = sb("eb", [P, QT])
        zsum = sb("zsum", [P, QT])
        rz = sb("rz", [P, QT])
        rz0 = sb("rz0", [P, B, QT])
        bn = sb("bn", [P, QT, 6])
        mv = sb("mv", [P, QT, 2])
        var = sb("var", [P, QT])
        minus_half = sb("minus_half", [P, QT])
        rstd = sb("rstd", [P, QT])

        d_w0 = [sem(f"d_w0_{i}") for i in range(4)]
        d_nat = [sem(f"d_nat{i}") for i in range(2)]
        d_x = sem("d_x")
        d_vec = sem("d_vec")
        d_small = sem("d_small")
        d_wq, d_wo, d_bk = sem("d_ck_wq"), sem("d_ck_wo"), sem("d_ck_bk")
        d_w = [sem(f"d_w_{n}") for n in "kqvo"]
        d_out = sem("d_out")
        fill_done, fill_hi, fill_lo = sem("fill_done"), sem("fill_hi"), sem("fill_lo")
        scores_done, max_ready, shift_ready, exp_done = sem("scores_done"), sem("max_ready"), sem("shift_ready"), sem("exp_done")
        act_bias_ready, eb_ready, zsum_ready, rz_ready, norm_done = sem("act_bias_ready"), sem("eb_ready"), sem("zsum_ready"), sem("rz_ready"), sem("norm_done")
        pt_done, pt_hi, pt_lo = sem("pt_done"), sem("pt_hi"), sem("pt_lo")
        mix_done, mix_hi, mix_lo = sem("mix_done"), sem("mix_hi"), sem("mix_lo")
        out_done, out_free = sem("out_done"), sem("out_free")
        w_ready = [sem(f"w_ready_{n}") for n in "kqvo"]
        split_hi = [sem(f"split_hi_{n}") for n in "kqvo"]
        w0_hi, w0_ready = sem("w0_hi"), sem("w0_ready")
        nat_hi, nat_ready = sem("nat_hi"), sem("nat_ready")
        consts_ready = sem("consts_ready")
        pool_chain, chain = sem("pool_chain"), sem("dve_chain")
        var_ready, rstd_ready, xn_ready, hT_ready = (sem(n) for n in ("var_ready", "rstd_ready", "xn_ready", "hT_ready"))
        nsb_ready, pb_ready, pbT_hi, pbT_ready = sem("nsb_ready"), sem("pb_ready"), sem("pbT_hi"), sem("pbT_ready")
        vec_ready, rt_ready, wb_used, wb_ready = sem("vec_ready"), sem("rt_ready"), sem("wb_used"), sem("wb_ready")
        wb_products, wb_pairs, r_ready = sem("wb_products"), sem("wb_pairs"), sem("r_ready")
        mlp_hi, mlp_ready = sem("mlp_hi"), sem("mlp_ready")
        down_done, result_ready = sem("down_done"), sem("result_ready")

        w0_dram = [A["L0_xattn_w_k"], A["L0_xattn_w_q"], A["L0_xattn_w_v"], A["L0_xattn_w_o"]]

        def stage_dram(l, name):
            return A[f"L1_xattn_{name}{l + 1}"]

        def pair_dram(l, w, r):
            if w == WO:
                v = stage_dram(l, "wo").rearrange("(h d) n -> d h n", d=DH)
                return v[:, bass.ds(r * 2, 2), :]
            v = stage_dram(l, {WK: "wk", WQ: "wq", WV: "wv"}[w]).rearrange("(c p) n -> p c n", p=P)
            return v[:, :, bass.ds(r * PW, PW)]

        block = ctx.enter_context(nc.Block())

        @block.sync
        def _(sp):
            ctx_dram = A["ctx_2048"].rearrange("b (c p) d -> b p c d", p=P)

            def load_w0(w):
                sp.dma_start(w_raw[:, w], w0_dram[w].rearrange("(c p) n -> p c n", p=P)).then_inc(d_w0[w], 16)

            def load_pair(l, w, r):
                sp.dma_start(w_raw[:, w], pair_dram(l, w, r)).then_inc(d_w[w], 16)

            sp.dma_start(nat_raw[:, 0], ctx_dram[0]).then_inc(d_nat[0], 16)
            load_w0(WQ)
            load_w0(WK)
            sp.dma_start(x[:], A["x"].rearrange("b (t p) d -> p (b t) d", p=P)).then_inc(d_x, 16)
            sp.dma_start(nat_raw[:, 1], ctx_dram[1]).then_inc(d_nat[1], 16)
            load_w0(WV)
            load_w0(WO)
            sp.dma_start(alpha[:], A["L0_xattn_alpha"].partition_broadcast(P)).then_inc(d_small, 16)
            sp.wait_ge(consts_ready, 5)
            rows = [("bq", BQ), ("bk", BK), ("bv", BV), ("bias_k", BIAS_K), ("bias_v", BIAS_V)]
            for l in range(2):
                for name, at in rows:
                    v = stage_dram(l, name)
                    if len(v.shape) == 4:
                        v = v.rearrange("a b h k -> (a b h) k")
                    else:
                        v = v.rearrange("(h k) -> h k", k=DH)
                    sp.dma_start(vec_raw[at:at + HEADS, l, :], v).then_inc(d_vec, 16)
                for v, at in ((A[f"L1_xattn_ln{l+1}_scale"], LN_G), (A[f"L1_xattn_ln{l+1}_offset"], LN_O)):
                    sp.dma_start(vec_raw[at:at + DC, l, :], v.rearrange("(c k) -> c k", k=P)).then_inc(d_vec, 16)
            for v, at, n in ((A["L1_xattn_b_fc1"], FC1_B, FC), (A["L1_xattn_ln_mlp_scale"], FC1_B + FC, DC),
                             (A["L1_xattn_ln_mlp_offset"], FC1_B + FC + DC, DC)):
                sp.dma_start(vec_raw[at:at + n, 0, :], v.rearrange("(c k) -> c k", k=P)).then_inc(d_vec, 16)

            def ctx_batch(b):
                sp.wait_ge(fill_done, FILL[f"cT{b-2}1"] + 1)
                sp.wait_ge(nat_ready, b - 1)
                sp.dma_start(nat_raw[:, b % 2], ctx_dram[b]).then_inc(d_nat[b % 2], 16)

            ctx_batch(2)
            sp.wait_ge(w0_ready, 3)
            for w in (WK, WQ, WV):
                load_pair(0, w, 0)

            wq_cols = [stage_dram(l, "wq").rearrange("(c p) n -> p c n", p=P) for l in range(2)]
            bk_cols = [stage_dram(l, "bias_k").rearrange("a b h k -> (a b h k)") for l in range(2)]
            wo_rows = [stage_dram(l, "wo").rearrange("(h d) n -> d h n", d=DH) for l in range(2)]

            def heads_of_wq(l, first, n):
                cols = bass.ds(first * DH, n * DH)
                sp.dma_start(ck_wq[:, :, 0:n * DH], wq_cols[l][:, :, cols]).then_inc(d_wq, 16)
                sp.dma_start(ck_bk[:, 0:n * DH], bk_cols[l][cols].partition_broadcast(P)).then_inc(d_bk, 16)

            def heads_of_wo(l, first, n):
                sp.dma_start(ck_wo[:, 0:n, :], wo_rows[l][:, bass.ds(first, n), :]).then_inc(d_wo, 16)

            heads_of_wq(0, 0, CHUNK_H)
            heads_of_wo(0, 0, CHUNK_H)
            sp.wait_ge(fill_done, FILL["WoT"] + 1)
            load_pair(0, WO, 0)
            ctx_batch(3)
            sp.dma_start(b2_row[:], A["L1_xattn_b_fc2"].partition_broadcast(P)).then_inc(d_small, 16)
            for l in range(2):
                sp.dma_start(bo_row[0:1, l, :], stage_dram(l, "bo").rearrange("(a n) -> a n", a=1)).then_inc(d_small, 16)
            for n in range(1, CHUNKS):
                sp.wait_ge(wb_used, n)
                heads_of_wq(0, n * CHUNK_H, CHUNK_H)
                sp.wait_ge(fill_done, FILL[f"RA{n-1}"] + 1)
                heads_of_wo(0, n * CHUNK_H, CHUNK_H)
            sp.wait_ge(wb_used, CHUNKS)
            heads_of_wq(1, 0, 2)
            sp.wait_ge(fill_done, FILL[f"RA{CHUNKS-1}"] + 1)
            heads_of_wo(1, 0, 2)

            def next_pair(l, r, ln, rn):
                for w in (WK, WQ, WV, WO):
                    sp.wait_ge(w_ready[w], r + (PAIRS * l + 1))
                    load_pair(ln, w, rn)

            with sp.Fori(0, PAIRS - 1) as r:
                next_pair(0, r, 0, r + 1)
                sp.wait_ge(wb_used, r + (CHUNKS + 1))
                heads_of_wq(1, r * 2 + 2, 2)
                sp.wait_ge(out_done, use_ra(r) + 1)
                heads_of_wo(1, r * 2 + 2, 2)
            next_pair(0, PAIRS - 1, 1, 0)
            with sp.Fori(0, PAIRS - 1) as r:
                next_pair(1, r, 1, r + 1)
            for w in range(4):
                sp.wait_ge(w_ready[w], 2 * PAIRS)
            w1_raw = w_raw[:].rearrange("p w c n -> p (w c n)").rearrange("p (c f) -> p c f", c=DC)
            sp.dma_start(w1_raw, A["L1_xattn_w_fc1"].rearrange("(c p) f -> p c f", p=P)).then_inc(d_w0[0], 16)
            w2_raw = nat_raw[:].rearrange("p n c d -> p (n c) d")
            sp.dma_start(w2_raw, A["L1_xattn_w_fc2"].rearrange("(c p) n -> p c n", p=P)).then_inc(d_w0[1], 16)
            out_dram = A["out"].rearrange("b (t p) d -> b p t d", p=P)
            for b in range(B):
                sp.wait_ge(result_ready, b + 1)
                sp.dma_start(out_dram[b], x[:, QT * b:QT * (b + 1), :]).then_inc(d_out, 16)
            sp.wait_ge(d_out, 16 * B)

        @block.gpsimd
        def _(pool):
            links = [0]

            def link(ins):
                links[0] += 1
                ins.then_inc(pool_chain, 1)
                pool.wait_ge(pool_chain, links[0])

            nc.gpsimd.memset(vec_raw[:], 0.0).then_inc(consts_ready, 1)
            link(nc.gpsimd.memset(ident[:], 0.0))
            nc.gpsimd.affine_select(out=ident[:], in_=ident[:], compare_op=ALU.not_equal, fill=1.0, base=0,
                                    pattern=[[-1, P]], channel_multiplier=1).then_inc(consts_ready, 1)
            nc.gpsimd.memset(minus_half[:], -0.5)
            nc.gpsimd.memset(ones[:], 1.0).then_inc(consts_ready, 1)
            nc.gpsimd.memset(rt[:], 0.0).then_inc(consts_ready, 1)
            link(nc.gpsimd.memset(p_bias[:], 0.0))
            nc.gpsimd.memset(p_bias[:, :, 0:1], 1.0).then_inc(consts_ready, 1)

            def split(hi, lo, raw, hi_sem, hi_count, done_sem):
                one = ones[:, 0:1].rearrange("p (a b) -> p a b", a=1).broadcast_to(raw.shape)
                nc.gpsimd.tensor_tensor(hi, raw, one, ALU.mult).then_inc(hi_sem, 1)
                pool.wait_ge(hi_sem, hi_count)
                nc.gpsimd.tensor_tensor(lo, raw, hi.bitcast(F32), ALU.subtract).then_inc(done_sem, 1)

            def split_ctx(b):
                pool.wait_ge(nat_hi, b + 1)
                nc.gpsimd.tensor_tensor(nat[:, b % 2, LO], nat_raw[:, b % 2], nat[:, b % 2, HI].bitcast(F32), ALU.subtract).then_inc(nat_ready, 1)

            def split_w(w, l, r, used=None):
                pool.wait_ge(d_w[w], r * 16 + 16 * (PAIRS * l + 1))
                if used:
                    pool.wait_ge(*used)
                split(wS[:, HI, w], wS[:, LO, w], w_raw[:, w], split_hi[w], r + (PAIRS * l + 1), w_ready[w])

            def ln_rstd(n):
                pool.wait_ge(var_ready, n + 1)
                nc.gpsimd.tensor_tensor(rstd[:], var[:], minus_half[:], ALU.pow).then_inc(rstd_ready, 1)

            split_ctx(0)
            split_ctx(1)
            for w in (WK, WV, WQ):
                split_w(w, 0, 0)
            for b in range(B):
                ln_rstd(b)
                if b < B - 2:
                    split_ctx(b + 2)
            def normalise(l, r, k):
                b, h = k // 2, k % 2
                u = unit(l, r, k)
                for t in range(QT):
                    pool.wait_ge(rz_ready, u * 2 + (t + 1 - 2 * B))
                    nc.gpsimd.tensor_tensor(p_pair[:, QT * b + t, h:h + 1], eb[:, t:t + 1], rz[:, t:t + 1], ALU.mult)
                    ins = nc.gpsimd.tensor_scalar(probs[:, t], probs[:, t], rz[:, t:t + 1], 1.0, ALU.mult, ALU.mult)
                ins.then_inc(norm_done, 1)

            normalise(0, 0, 0)

            def body(l, r, nxt):
                for k in range(UNITS):
                    b = k // 2
                    if k == 0:
                        split_w(WO, l, r, used=(out_done, use_last(l, "pbT0") if isinstance(r, int) else use_out(l, r, 0)))
                    if nxt and k == 5:
                        split_w(WK, *nxt, used=(fill_done, step_fill(l, r, 3, 2) + 1))
                        split_w(WQ, *nxt)
                    if nxt and k == 6:
                        split_w(WV, *nxt, used=(fill_done, step_fill(l, r, 3, 4) + 1))
                    if isinstance(r, int) and b and k % 2 == 0:
                        ln_rstd(4 * (l + 1) + b - 1)
                    if k < UNITS - 1:
                        normalise(l, r, k + 1)
                    elif nxt:
                        normalise(nxt[0], nxt[1], 0)

            def layer(l):
                with pool.Fori(0, PAIRS - 1) as r:
                    body(l, r, (l, r + 1))

            layer(0)
            body(0, PAIRS - 1, (1, 0))
            ln_rstd(4 + B - 1)
            layer(1)
            body(1, PAIRS - 1, None)
            ln_rstd(8 + B - 1)
            w1_raw = w_raw[:].rearrange("p w c n -> p (w c n)").rearrange("p (c f) -> p c f", c=DC)
            w2_raw = nat_raw[:].rearrange("p n c d -> p (n c) d")
            pool.wait_ge(d_w0[0], 32)
            split(w1S[:, HI], w1S[:, LO], w1_raw, mlp_hi, 1, mlp_ready)
            pool.wait_ge(d_w0[1], 32)
            split(w2S[:, HI], w2S[:, LO], w2_raw, mlp_hi, 2, mlp_ready)

        @block.scalar
        def _(act):
            def hi_copy(f, dst, src):
                act.wait_ge(fill_done, f + 1)
                return nc.scalar.activation(dst, src, ACT.Copy)

            def hi_biased(f, l, r, dst_src_row):
                act.wait_ge(fill_done, f + 1)
                act.wait_ge(act_bias_ready, r + (PAIRS * l + 1))
                for dst, src, (which, h) in dst_src_row:
                    ins = nc.scalar.activation(dst, src, ACT.Identity, bias=act_bias[:, which, h:h + 1])
                return ins

            def pair_bias(l, r):
                both = vecT[:, l, 0:2 * HEADS].rearrange("p (w h) -> p w h", w=2)
                nc.scalar.activation(act_bias[:], both[:, :, bass.ds(r * 2, 2)], ACT.Copy).then_inc(act_bias_ready, 1)

            def startup_fill(name):
                f = FILL[name]
                pj = proj[f % 2]
                halves = pj[:].rearrange("p (a n) -> p a n", a=2)
                b = int(name[2]) if name[0] in "xc" else 0
                if name == "vec":
                    ins = hi_copy(f, vecT[:], pj[:, 0:2 * P].rearrange("p (a n) -> p a n", a=2))
                elif name == "M":
                    ins = hi_copy(f, mS[:, HI], halves)
                elif name[:2] == "xT":
                    ins = hi_copy(f, hT[:, HI, :, b * LQ:(b + 1) * LQ], halves)
                elif name[:2] == "cT":
                    ins = hi_copy(f, cT[:, HI, int(name[3]), b * T:(b + 1) * T], pj[:])
                elif name == "WoT":
                    ins = hi_copy(f, w0S[:, HI, WO], halves)
                elif name == "N":
                    ins = hi_copy(f, nS[:, HI], halves)
                elif name[0] == "G":
                    ins = hi_copy(f, gS[:, HI], halves)
                elif name[:2] == "RA":
                    c = int(name[2])
                    half = pj[:, 0:DC * CHUNK_H * 2].rearrange("p (c h v) -> p c h v", c=DC, v=2)[:, :, :, 0]
                    ins = hi_copy(f, rt_raw[:, 0, 0, :, c * CHUNK_H:(c + 1) * CHUNK_H], half)
                elif name[:2] == "RB":
                    ins = hi_copy(f, r_full[:], pj[:, 0:D])
                else:
                    return step_fill_hi(f, {"K0": 0, "Q": 1, "K1": 2, "Va": 3, "Vb": 4}[name], 0, 0, 0, f % 2)
                ins.then_inc(fill_hi, 1)

            def step_fill_hi(f, kind, l, r, b, bank):
                pj = proj[bank]
                if kind in (0, 2):
                    h = kind // 2
                    ins = hi_biased(f, l, r, [(kT[:, HI, h], pj[:], (1, h))])
                elif kind == 1:
                    ins = hi_biased(f, l, r, [(qT[:, HI, h], pj[:, h * LQ:(h + 1) * LQ], (0, h)) for h in range(2)])
                else:
                    c = 2 * (kind - 3)
                    ins = hi_copy(f, vS[:, HI, b % 2, c:c + 2], pj[:].rearrange("p (c n) -> p c n", c=2))
                ins.then_inc(fill_hi, 1)

            def probsT_hi(u):
                for j in range(2):
                    act.wait_ge(pt_done, u * 2 + (j + 1))
                    nc.scalar.activation(probsT[:, HI, 2 * j:2 * j + 2], probsT_ps[:, 2 * j:2 * j + 2], ACT.Copy).then_inc(pt_hi, 1)

            def mix_hi_copy(u, dst, src):
                act.wait_ge(mix_done, u + 1)
                nc.scalar.activation(dst, src, ACT.Copy).then_inc(mix_hi, 1)

            def exps0(b):
                act.wait_ge(shift_ready, b + 1)
                for t in range(QT):
                    nc.scalar.activation(probs[:, t], scores[:, t], ACT.Exp, bias=shift[:, t:t + 1], scale=SCALE0,
                                         accum_out=z[:, t:t + 1]).then_inc(exp_done, 1)

            def exps(l, r, k, between=lambda: None):
                b, h = k // 2, k % 2
                act.wait_ge(shift_ready, unit(l, r, k) + 1)

                def tile_exp(t):
                    nc.scalar.activation(probs[:, t], scores[:, t], ACT.Exp, bias=shift[:, t:t + 1], scale=SCALE,
                                         accum_out=z[:, t:t + 1]).then_inc(exp_done, 1)

                tile_exp(0)
                between()
                for t in range(QT):
                    ins = nc.scalar.activation(eb[:, t:t + 1], nsb[:, QT * b + t, bass.ds(r * 2 + h, 1)], ACT.Exp,
                                               bias=shift[:, t:t + 1], scale=-1.0)
                ins.then_inc(eb_ready, 1)
                tile_exp(1)

            def ln_full(n, use, l):
                act.wait_ge(out_done, use + 1)
                if n:
                    act.wait_ge(hT_ready, n)
                g, o = (LN_G, LN_O) if l < 2 else (FC1_B + FC, FC1_B + FC + DC)
                src = out_ps[:].rearrange("p (c q) -> p c q", c=DC)
                for c in range(DC):
                    ins = nc.scalar.activation(h_full[:, c], src[:, c], ACT.Identity, bias=vecT[:, l % 2, o + c:o + c + 1],
                                               scale=vecT[:, l % 2, g + c:g + c + 1])
                ins.then_inc(out_free, 1)

            def ctx_hi(b):
                act.wait_ge(d_nat[b % 2], 16 * (b // 2 + 1))
                if b >= 2:
                    act.wait_ge(mix_done, b - 1)
                nc.scalar.activation(nat[:, b % 2, HI], nat_raw[:, b % 2], ACT.Copy).then_inc(nat_hi, 1)

            def w0_copy(w):
                act.wait_ge(d_w0[w], 16)
                nc.scalar.activation(w0S[:, HI, w], w_raw[:, w], ACT.Copy).then_inc(w0_hi, 1)

            ctx_hi(0)
            w0_copy(WQ)
            w0_copy(WK)
            for name in first_fills:
                startup_fill(name)
            for name in second_fills:
                startup_fill(name)
            w0_copy(WV)
            exps0(0)
            ctx_hi(1)
            for b in range(B):
                probsT_hi(b)
                if b < B - 1:
                    exps0(b + 1)
                if b in (1, 2):
                    ctx_hi(b + 1)
                for name in slot_fills[b]:
                    startup_fill(name)
                    if name == "vec":
                        act.wait_ge(fill_hi, FILL["vec"] + 1)
                        pair_bias(0, 0)
                mix_hi_copy(b, mixT[:, HI], mix_ps[:].rearrange("p (c q) -> p c q", c=DC))
                if b:
                    ln_full(b - 1, use0(f"lnT{b-1}"), 0)
            startup_fill("Q")
            exps(0, 0, 0)
            startup_fill("RA3")
            ln_full(B - 1, use0(f"lnT{B-1}"), 0)
            startup_fill("RB0")

            def body(l, r, nxt):
                last = isinstance(r, int)
                for k in range(UNITS):
                    b, h = k // 2, k % 2
                    u = unit(l, r, k)
                    to = (l, r, b + 1) if b < B - 1 else (nxt + (0,) if nxt else None)
                    after = (l, r, k + 1) if k < UNITS - 1 else (nxt + (0,) if nxt else None)

                    def fill(kind):
                        if to:
                            step_fill_hi(step_fill(l, r, b + 1, kind), kind, *to, (NF0 + 5 * b + kind) % 2)

                    def mix_out():
                        mix_hi_copy(u, mixT[:, HI, h], mix_ps[:, 0:LQ])
                        if last and h == 1:
                            act.wait_ge(out_done, use_last(l, f"pbT{b}") + 1)
                            nc.scalar.activation(pbT[:, HI], out_ps[:, 0:LQ], ACT.Copy).then_inc(pbT_hi, 1)

                    probsT_hi(u)
                    if h == 0:
                        exps(l, r, k + 1, between=lambda: fill(0))
                        fill(1)
                        mix_out()
                        fill(2)
                    else:
                        if last and b:
                            ln_full(4 * (l + 1) + b - 1, use_last(l, f"lnT{b - 1}"), l + 1)
                        fill(3)
                        if after:
                            exps(*after, between=mix_out)
                        else:
                            mix_out()
                        fill(4)
                    if nxt and k == 5:
                        pair_bias(*nxt)

            for l in range(2):
                with act.Fori(0, PAIRS - 1) as r:
                    body(l, r, (l, r + 1))
                body(l, PAIRS - 1, (1, 0) if l == 0 else None)
                ln_full(4 * (l + 1) + B - 1, use_last(l, f"lnT{B - 1}"), l + 1)

            for half in range(2):
                for f in range(FC):
                    n = half * FC + f
                    act.wait_ge(fill_done, MLP_FILL + n + 1)
                    if n >= 2:
                        act.wait_ge(fill_lo, MLP_FILL + n - 1)
                    nc.scalar.activation(gelu_full[:, n % 2], proj[(MLP_FILL + n) % 2][:], ACT.Gelu,
                                         bias=vecT[:, 0, FC1_B + f:FC1_B + f + 1]).then_inc(fill_hi, 1)


        @block.vector
        def _(dve):
            links = [0]

            def link(ins):
                links[0] += 1
                ins.then_inc(chain, 1)
                dve.wait_ge(chain, links[0])

            def lo_sub(f, dst, src, hi, bias=None):
                dve.wait_ge(fill_hi, f + 1)
                if bias is None:
                    return nc.vector.tensor_tensor(dst, src, hi.bitcast(F32), ALU.subtract)
                return nc.vector.scalar_tensor_tensor(dst, src, bias, hi.bitcast(F32), ALU.add, ALU.subtract)

            def split(hi, lo, full):
                link(nc.vector.tensor_copy(hi, full))
                return nc.vector.tensor_tensor(lo, full, hi.bitcast(F32), ALU.subtract)

            def startup_fill(name):
                f = FILL[name]
                pj = proj[f % 2]
                halves = pj[:].rearrange("p (a n) -> p a n", a=2)
                b = int(name[2]) if name[0] in "xc" else 0
                if name == "vec":
                    dve.wait_ge(fill_hi, f + 1)
                    for l in range(2):
                        v = vecT[:, l]
                        nc.vector.tensor_copy(vt2[:, l, :, 0], v[:, BV:BV + HEADS])
                        nc.vector.tensor_tensor(vt2[:, l, :, 1], v[:, BIAS_V:BIAS_V + HEADS], v[:, BV:BV + HEADS], ALU.subtract)
                        ins = nc.vector.tensor_tensor(bqk[:, l], v[:, BQ:BQ + HEADS], v[:, BIAS_K:BIAS_K + HEADS], ALU.mult)
                elif name == "M":
                    ins = lo_sub(f, mS[:, LO], halves, mS[:, HI])
                elif name[:2] == "xT":
                    ins = lo_sub(f, hT[:, LO, :, b * LQ:(b + 1) * LQ], halves, hT[:, HI, :, b * LQ:(b + 1) * LQ])
                elif name[:2] == "cT":
                    c = int(name[3])
                    ins = lo_sub(f, cT[:, LO, c, b * T:(b + 1) * T], pj[:], cT[:, HI, c, b * T:(b + 1) * T])
                elif name == "WoT":
                    ins = lo_sub(f, w0S[:, LO, WO], halves, w0S[:, HI, WO])
                elif name == "N":
                    ins = lo_sub(f, nS[:, LO], halves, nS[:, HI])
                elif name[0] == "G":
                    ins = lo_sub(f, gS[:, LO], halves, gS[:, HI])
                elif name[:2] == "RA":
                    c = int(name[2])
                    dve.wait_ge(fill_hi, f + 1)
                    half = pj[:, 0:DC * CHUNK_H * 2].rearrange("p (c h v) -> p c h v", c=DC, v=2)[:, :, :, 1]
                    ins = nc.vector.tensor_copy(rt_raw[:, 0, 1, :, c * CHUNK_H:(c + 1) * CHUNK_H], half)
                elif name[:2] == "RB":
                    dve.wait_ge(fill_hi, f + 1)
                    ins = r_split(0)
                else:
                    return step_fill_lo(f, {"K0": 0, "Q": 1, "K1": 2, "Va": 3, "Vb": 4}[name], 0, 0, 0, f % 2)
                ins.then_inc(fill_lo, 1)

            def wb_chunk(c):
                dve.wait_ge(d_wq, 16 * (c + 1))
                dve.wait_ge(d_bk, 16 * (c + 1))
                for i in range(DC):
                    ins = nc.vector.tensor_tensor(ck_wq[:, i], ck_wq[:, i], ck_bk[:], ALU.mult)
                link(ins)
                nc.vector.reduce_sum(wb_full[:, 0, :, c * CHUNK_H:(c + 1) * CHUNK_H],
                                     ck_wq[:].rearrange("p c (h k) -> p c h k", k=DH), AX_X).then_inc(wb_used, 1)
                if c == CHUNKS - 1:
                    dve.wait_ge(wb_used, c + 1)
                    split(wbS[:, HI, 0], wbS[:, LO, 0], wb_full[:, 0]).then_inc(wb_ready, 1)

            def wb_pair(r):
                dve.wait_ge(d_wq, r * 16 + 16 * (CHUNKS + 1))
                dve.wait_ge(d_bk, r * 16 + 16 * (CHUNKS + 1))
                for i in range(DC):
                    ins = nc.vector.tensor_tensor(ck_wq[:, i, 0:PW], ck_wq[:, i, 0:PW], ck_bk[:, 0:PW], ALU.mult)
                ins.then_inc(wb_products, 1)
                dve.wait_ge(wb_products, r + 1)
                nc.vector.reduce_sum(wb_two[:], ck_wq[:, :, 0:PW].rearrange("p c (h k) -> p c h k", k=DH), AX_X).then_inc(wb_used, 1)
                dve.wait_ge(wb_used, r + (CHUNKS + 1))
                nc.vector.tensor_tensor(wb_full[:, 1, :, bass.ds(r * 2, 2)], wb_two[:], wb_two[:], ALU.max).then_inc(wb_pairs, 1)

            def ra_pair(r):
                dve.wait_ge(out_done, use_ra(r) + 1)
                src = out_ps[:, 0:DC * 4].rearrange("p (c h v) -> p c h v", c=DC, v=2)
                for v in range(2):
                    ins = nc.vector.tensor_scalar(rt_raw[:, 1, v, :, bass.ds(r * 2, 2)], src[:, :, :, v], 1.0, None, ALU.mult)
                ins.then_inc(out_free, 1)

            def r_columns(l):
                dve.wait_ge(consts_ready, 5)
                nc.vector.reduce_sum(rt[:, :, 0:1], rt_raw[:, l, 0], AX_X)
                nc.vector.tensor_copy(rt[:, :, 1:1 + HEADS], rt_raw[:, l, 1]).then_inc(rt_ready, 1)

            def r_split(l):
                dve.wait_ge(d_small, 64)
                link(nc.vector.tensor_tensor(r_full[0:1, :], r_full[0:1, :], bo_row[0:1, l, :], ALU.add))
                return split(rS[:, HI, l], rS[:, LO, l], r_full[:])

            def step_fill_lo(f, kind, l, r, b, bank):
                pj = proj[bank]
                if kind in (0, 2):
                    h = kind // 2
                    ins = lo_sub(f, kT[:, LO, h], pj[:], kT[:, HI, h], vecT[:, l, bass.ds(r * 2 + (BK + h), 1)])
                elif kind == 1:
                    for h in range(2):
                        ins = lo_sub(f, qT[:, LO, h], pj[:, h * LQ:(h + 1) * LQ], qT[:, HI, h], vecT[:, l, bass.ds(r * 2 + (BQ + h), 1)])
                else:
                    c = 2 * (kind - 3)
                    ins = lo_sub(f, vS[:, LO, b % 2, c:c + 2], pj[:].rearrange("p (c n) -> p c n", c=2), vS[:, HI, b % 2, c:c + 2])
                ins.then_inc(fill_lo, 1)

            def probsT_lo(u):
                for j in range(2):
                    dve.wait_ge(pt_hi, u * 2 + (j + 1))
                    nc.vector.tensor_tensor(probsT[:, LO, 2 * j:2 * j + 2], probsT_ps[:, 2 * j:2 * j + 2],
                                            probsT[:, HI, 2 * j:2 * j + 2].bitcast(F32), ALU.subtract).then_inc(pt_lo, 1)

            def mix_lo_sub(u, dst, src, hi):
                dve.wait_ge(mix_hi, u + 1)
                nc.vector.tensor_tensor(dst, src, hi.bitcast(F32), ALU.subtract).then_inc(mix_lo, 1)

            def maxima(u):
                dve.wait_ge(scores_done, u + 1)
                nc.vector.reduce_max(mx[:], scores[:], AX_X).then_inc(max_ready, 1)
                dve.wait_ge(max_ready, u + 1)

            def shift0(b):
                maxima(b)
                nc.vector.tensor_scalar(shift[:], mx[:], -SCALE0, None, ALU.mult).then_inc(shift_ready, 1)

            def shifts(l, r, k):
                b, h = k // 2, k % 2
                maxima(unit(l, r, k))
                nc.vector.scalar_tensor_tensor(shift[:].rearrange("p (t a) -> p t a", a=1),
                                               mx[:].rearrange("p (t a) -> p t a", a=1), -SCALE,
                                               nsb[:, QT * b:QT * (b + 1), bass.ds(r * 2 + h, 1)],
                                               ALU.mult, ALU.min).then_inc(shift_ready, 1)

            def sums(l, r, k):
                u = unit(l, r, k)
                dve.wait_ge(eb_ready, u - B + 1)
                for t in range(QT):
                    if t:
                        dve.wait_ge(exp_done, u * 2 + 2)
                    nc.vector.tensor_tensor(zsum[:, t:t + 1], z[:, t:t + 1], eb[:, t:t + 1], ALU.add).then_inc(zsum_ready, 1)
                    dve.wait_ge(zsum_ready, u * 2 + (t + 1 - 2 * B))
                    nc.vector.reciprocal(rz[:, t:t + 1], zsum[:, t:t + 1]).then_inc(rz_ready, 1)

            def pair_weights(l, r, b0, b1):
                dve.wait_ge(norm_done, unit(l, r, 2 * b1) - B)
                tiles = slice(QT * b0, QT * b1)
                nc.vector.tensor_tensor(p_bias[:, tiles, bass.ds(r * 2 + 1, 2)], p_pair[:, tiles], p_pair[:, tiles], ALU.max).then_inc(pb_ready, 1)

            def add_out(use, b):
                dve.wait_ge(out_done, use + 1)
                xb = x[:, QT * b:QT * (b + 1)]
                nc.vector.tensor_tensor(xb, out_ps[:].rearrange("p (t n) -> p t n", t=QT), xb, ALU.add).then_inc(out_free, 1)

            def ln_stats(use, b):
                dve.wait_ge(out_free, use + 1)
                for t in range(QT):
                    ins = nc.vector.bn_stats(bn[:, t], x[:, QT * b + t])
                link(ins)
                for t in range(QT):
                    ins = nc.vector.bn_aggr(mv[:, t], bn[:, t])
                link(ins)
                nc.vector.tensor_scalar(var[:], mv[:, :, 1], EPS, None, ALU.add).then_inc(var_ready, 1)

            def ln_x(n, b, mlp=False):
                dve.wait_ge(rstd_ready, n + 1)
                for t in range(QT):
                    ins = nc.vector.tensor_scalar(xn[:, t], x[:, QT * b + t], mv[:, t, 0:1], rstd[:, t:t + 1], ALU.subtract, ALU.mult)
                ins.then_inc(xn_ready, 1)
                if mlp:
                    for t in range(QT):
                        nc.vector.tensor_tensor(x[:, QT * b + t], x[:, QT * b + t], b2_row[:], ALU.add)

            def ln_split(use, b):
                dve.wait_ge(out_free, use + 1)
                hi, lo = (hT[:, s, :, b * LQ:(b + 1) * LQ] for s in (HI, LO))
                split(hi, lo, h_full[:]).then_inc(hT_ready, 1)

            def bias_logits(use, b):
                dve.wait_ge(out_done, use + 1)
                nc.vector.tensor_scalar(nsb[:, QT * b:QT * (b + 1)],
                                        out_ps[:, 0:QT * HEADS].rearrange("p (t h) -> p t h", t=QT),
                                        -SCALE, None, ALU.mult).then_inc(out_free, 1)

            def w0_sub(n, w):
                dve.wait_ge(w0_hi, n + 1)
                nc.vector.tensor_tensor(w0S[:, LO, w], w_raw[:, w], w0S[:, HI, w].bitcast(F32), ALU.subtract).then_inc(w0_ready, 1)

            def sums0(b):
                dve.wait_ge(exp_done, 2 * b + 2)
                link(nc.vector.reciprocal(rz0[:, b], z[:]))
                link(nc.vector.tensor_scalar(rz0[:, b], rz0[:, b], alpha[:], None, ALU.mult))

            w0_sub(0, WQ)
            w0_sub(1, WK)
            for name in first_fills:
                startup_fill(name)
            shift0(0)
            for name in second_fills:
                startup_fill(name)
            w0_sub(2, WV)
            dve.wait_ge(d_small, 16)
            sums0(0)
            for b in range(B):
                if b < B - 1:
                    shift0(b + 1)
                probsT_lo(b)
                if b < B - 1:
                    sums0(b + 1)
                for name in slot_fills[b]:
                    startup_fill(name)
                if b:
                    wb_chunk(b - 1)
                mix_lo_sub(b, mixT[:, LO], mix_ps[:].rearrange("p (c q) -> p c q", c=DC), mixT[:, HI])
                if b:
                    ln_split(use0(f"lnT{b-1}"), b - 1)
                use = use0(f"delta{b}")
                dve.wait_ge(out_done, use + 1)
                for t in range(QT):
                    xt = x[:, QT * b + t]
                    ins = nc.vector.scalar_tensor_tensor(xt, out_ps[:, t * D:(t + 1) * D], rz0[:, b, t:t + 1], xt, ALU.mult, ALU.add)
                ins.then_inc(out_free, 1)
                ln_stats(use, b)
                ln_x(b, b)
            startup_fill("Q")
            wb_chunk(CHUNKS - 1)
            bias_logits(use0("sb0"), 0)
            shifts(0, 0, 0)
            sums(0, 0, 0)
            startup_fill("RA3")
            bias_logits(use0("sb1"), 1)
            bias_logits(use0("sb2"), 2)
            ln_split(use0(f"lnT{B-1}"), B - 1)
            r_columns(0)
            startup_fill("RB0")
            bias_logits(use0("sb3"), 3)

            def body(l, r, nxt):
                last = isinstance(r, int)
                for k in range(UNITS):
                    b, h = k // 2, k % 2
                    u = unit(l, r, k)
                    to = (l, r, b + 1) if b < B - 1 else (nxt + (0,) if nxt else None)
                    after = (l, r, k + 1) if k < UNITS - 1 else (nxt + (0,) if nxt else None)
                    if h == 0 and b:
                        add_out(use_out(l, r, b - 1), b - 1)
                        if last:
                            ln_stats(use_last(l, f"out{b - 1}"), b - 1)
                    if h == 0:
                        shifts(*after)
                    probsT_lo(u)
                    if h == 1 and after:
                        shifts(*after)

                    def fill(kind):
                        if to:
                            step_fill_lo(step_fill(l, r, b + 1, kind), kind, *to, (NF0 + 5 * b + kind) % 2)

                    if h == 0:
                        fill(0)
                        sums(*after)
                        if l == 0 and k == 2:
                            wb_pair(r)
                            ra_pair(r)
                            if last:
                                dve.wait_ge(wb_pairs, PAIRS)
                                split(wbS[:, HI, 1], wbS[:, LO, 1], wb_full[:, 1]).then_inc(wb_ready, 1)
                        if last and b:
                            ln_x(4 * (l + 1) + b - 1, b - 1, mlp=l == 1)
                        fill(1)
                        if last and l == 0 and b >= 2:
                            bias_logits(use_last(l, f"sb{b - 2}"), b - 2)
                        mix_lo_sub(u, mixT[:, LO, h], mix_ps[:, 0:LQ], mixT[:, HI, h])
                        fill(2)
                    else:
                        if last:
                            if b:
                                ln_split(use_last(l, f"lnT{b - 1}"), b - 1)
                            pair_weights(l, r, b, b + 1)
                        elif k == UNITS - 1:
                            pair_weights(l, r, 0, B)
                        fill(3)
                        mix_lo_sub(u, mixT[:, LO, h], mix_ps[:, 0:LQ], mixT[:, HI, h])
                        if last:
                            dve.wait_ge(pbT_hi, B * l + b + 1)
                            nc.vector.tensor_tensor(pbT[:, LO], out_ps[:, 0:LQ], pbT[:, HI].bitcast(F32), ALU.subtract).then_inc(out_free, 1)
                        if after:
                            sums(*after)
                        fill(4)
                add_out(use_out(l, r, B - 1), B - 1)

            for l in range(2):
                with dve.Fori(0, PAIRS - 1) as r:
                    body(l, r, (l, r + 1))
                body(l, PAIRS - 1, (1, 0) if l == 0 else None)
                ln_stats(use_last(l, f"out{B - 1}"), B - 1)
                ln_x(4 * (l + 1) + B - 1, B - 1, mlp=l == 1)
                if l == 0:
                    bias_logits(use_last(l, f"sb{B - 2}"), B - 2)
                ln_split(use_last(l, f"lnT{B - 1}"), B - 1)
                if l == 0:
                    bias_logits(use_last(l, f"sb{B - 1}"), B - 1)
                    r_columns(1)
                    use = use_last(0, "rb")
                    dve.wait_ge(out_done, use + 1)
                    nc.vector.tensor_copy(r_full[:], out_ps[:, 0:D]).then_inc(out_free, 1)
                    dve.wait_ge(out_free, use + 1)
                    r_split(1).then_inc(r_ready, 1)

            for half in range(2):
                for f in range(FC):
                    n = half * FC + f
                    dve.wait_ge(fill_hi, MLP_FILL + n + 1)
                    link(nc.vector.tensor_copy(gelu_hi[:, f], gelu_full[:, n % 2]))
                    nc.vector.tensor_tensor(gelu_lo[:, f], gelu_full[:, n % 2], gelu_hi[:, f].bitcast(F32), ALU.subtract).then_inc(fill_lo, 1)
                for i in range(2):
                    b = 2 * half + i
                    dve.wait_ge(down_done, b + 1)
                    xb = x[:, QT * b:QT * (b + 1)]
                    bank = (out_ps, mix_ps)[i]
                    nc.vector.tensor_tensor(xb, bank[:].rearrange("p (t n) -> p t n", t=QT), xb, ALU.add).then_inc(result_ready, 1)

        @block.tensor
        def _(pe):
            def product(out, pairs):
                n = len(pairs) * len(PASSES)
                i = 0
                for a, b_ in pairs:
                    for s, t in PASSES:
                        ins = nc.tensor.matmul(out, a(s), b_(t), start=(i == 0), stop=(i == n - 1))
                        i += 1
                return ins

            def fill_bank(f):
                if isinstance(f, int) and f < 2:
                    return
                pe.wait_ge(fill_lo, f - 1)

            def startup_fill(name):
                f = FILL[name]
                pj = proj[f % 2]
                b = int(name[2]) if name[0] in "xc" else 0
                fill_bank(f)
                if name == "vec":
                    pe.wait_ge(d_vec, 17 * 16)
                    for l in range(2):
                        ins = nc.tensor.transpose(pj[:, l * P:(l + 1) * P], vec_raw[:, l], ident[:])
                elif name == "M":
                    pe.wait_ge(w0_ready, 2)
                    for i in range(DC):
                        ins = product(pj[:, i * D:(i + 1) * D],
                                      [(lambda s, o=o: w0S[:, s, WQ, o, i * P:(i + 1) * P], lambda s, o=o: w0S[:, s, WK, o]) for o in range(DC)])
                elif name[:2] == "xT":
                    pe.wait_ge(d_x, 16)
                    for c in range(DC):
                        for t in range(QT):
                            ins = nc.tensor.transpose(pj[:, (c * QT + t) * P:(c * QT + t + 1) * P], x[:, QT * b + t, c * P:(c + 1) * P], ident[:])
                elif name[:2] == "cT":
                    c = int(name[3])
                    pe.wait_ge(d_nat[b % 2], 16 * (b // 2 + 1))
                    for t in range(TC):
                        ins = nc.tensor.transpose(pj[:, t * P:(t + 1) * P], nat_raw[:, b % 2, t, c * P:(c + 1) * P], ident[:])
                elif name == "WoT":
                    pe.wait_ge(d_w0[WO], 16)
                    for v in range(DC):
                        for o in range(DC):
                            ins = nc.tensor.transpose(pj[:, (v * DC + o) * P:(v * DC + o + 1) * P], w_raw[:, WO, o, v * P:(v + 1) * P], ident[:])
                elif name == "N":
                    pe.wait_ge(w0_ready, 3)
                    pe.wait_ge(fill_lo, FILL["WoT"] + 1)
                    for i in range(DC):
                        ins = product(pj[:, i * D:(i + 1) * D],
                                      [(lambda s, v=v: w0S[:, s, WV, v, i * P:(i + 1) * P], lambda s, v=v: w0S[:, s, WO, v]) for v in range(DC)])
                elif name[0] == "G":
                    b = int(name[1])
                    pe.wait_ge(fill_lo, max(FILL["M"], FILL[f"xT{b}"]) + 1)
                    for j in range(DC):
                        ins = product(pj[:, j * LQ:(j + 1) * LQ],
                                      [(lambda s, i=i: mS[:, s, i, j * P:(j + 1) * P], lambda s, i=i: hT[:, s, i, b * LQ:(b + 1) * LQ]) for i in range(DC)])
                elif name[:2] == "RA":
                    ck, l = int(name[2]), 0
                    pe.wait_ge(d_wo, 16 * (ck + 1))
                    for c in range(DC):
                        for h in range(CHUNK_H):
                            at = (c * CHUNK_H + h) * 2
                            ins = nc.tensor.matmul(pj[:, at:at + 2], ck_wo[:, h, c * P:(c + 1) * P], vt2[:, l, ck * CHUNK_H + h, :], start=True, stop=True)
                elif name[:2] == "RB":
                    pe.wait_ge(rt_ready, 1)
                    for c in range(DC):
                        ins = nc.tensor.transpose(pj[:, c * P:(c + 1) * P], rt[:, c], ident[:])
                else:
                    return step_fill_mm(f, {"K0": 0, "Q": 1, "K1": 2, "Va": 3, "Vb": 4}[name], 0, 0, 0, f % 2, wait=False)
                ins.then_inc(fill_done, 1)

            def step_fill_mm(f, kind, l, r, b, bank, wait=True):
                pj = proj[bank]
                if wait:
                    fill_bank(f)
                if b == 0:
                    w = {0: WK, 1: WQ, 3: WV}.get(kind)
                    if w is not None:
                        pe.wait_ge(w_ready[w], r + (PAIRS * l + 1))
                if kind in (0, 2):
                    h = kind // 2
                    ins = product(pj[:], [(lambda s, c=c: wS[:, s, WK, c, h * DH:(h + 1) * DH], lambda s, c=c: cT[:, s, c, b * T:(b + 1) * T]) for c in range(DC)])
                elif kind == 1:
                    for h in range(2):
                        ins = product(pj[:, h * LQ:(h + 1) * LQ],
                                      [(lambda s, c=c: wS[:, s, WQ, c, h * DH:(h + 1) * DH], lambda s, c=c: hT[:, s, c, b * LQ:(b + 1) * LQ]) for c in range(DC)])
                else:
                    for j in range(2):
                        at = b * T + (2 * (kind - 3) + j) * P
                        ins = product(pj[:, j * PW:(j + 1) * PW],
                                      [(lambda s, c=c: cT[:, s, c, at:at + P], lambda s, c=c: wS[:, s, WV, c]) for c in range(DC)])
                ins.then_inc(fill_done, 1)

            def unit_scores(l, r, k, ready):
                h = k % 2
                u = unit(l, r, k)
                pe.wait_ge(fill_lo, ready + 1)
                pe.wait_ge(exp_done, u * 2)
                for t in range(QT):
                    ins = product(scores[:, t], [(lambda s: qT[:, s, h, t * P:(t + 1) * P], lambda s: kT[:, s, h])])
                ins.then_inc(scores_done, 1)

            def transposes(u):
                for j in range(2):
                    if not (isinstance(u, int) and u == 0):
                        pe.wait_ge(pt_lo, u * 2 + (j - 1))
                    for c in (2 * j, 2 * j + 1):
                        for t in range(QT):
                            ins = nc.tensor.transpose(probsT_ps[:, c, t * P:(t + 1) * P], probs[:, t, c * P:(c + 1) * P], ident[:])
                    ins.then_inc(pt_done, 1)

            def mix(l, r, k, ready):
                b, h = k // 2, k % 2
                u = unit(l, r, k)
                pe.wait_ge(mix_lo, u)
                if ready is not None:
                    pe.wait_ge(fill_lo, ready + 1)
                n = 0
                for c in range(TC):
                    if c % 2 == 0:
                        pe.wait_ge(pt_lo, u * 2 + (c // 2 + 1))
                    for s, t in PASSES:
                        ins = nc.tensor.matmul(mix_ps[:, 0:LQ], vS[:, s, b % 2, c, h * DH:(h + 1) * DH], probsT[:, t, c],
                                               start=(n == 0), stop=(n == 3 * TC - 1))
                        n += 1
                ins.then_inc(mix_done, 1)

            def step_out(l, r, b):
                last = isinstance(r, int)
                pe.wait_ge(mix_lo, unit(l, r, 2 * b + 2))
                if b == 0:
                    pe.wait_ge(w_ready[WO], r + (PAIRS * l + 1))
                use = use_out(l, r, b)
                pe.wait_ge(out_free, use)
                for t in range(QT):
                    terms = [(lambda s, h=h: mixT[:, s, h, t * P:(t + 1) * P], lambda s, h=h: wS[:, s, WO, h]) for h in range(2)]
                    if last:
                        if l:
                            pe.wait_ge(r_ready, 1)
                        terms.append((lambda s: pbT[:, s, t * P:(t + 1) * P], lambda s: rS[:, s, l]))
                    ins = product(out_ps[:, t * D:(t + 1) * D], terms)
                ins.then_inc(out_done, 1)

            def ln_transposes(n, use):
                pe.wait_ge(xn_ready, n + 1)
                pe.wait_ge(out_free, use)
                for c in range(DC):
                    for t in range(QT):
                        ins = nc.tensor.transpose(out_ps[:, (c * QT + t) * P:(c * QT + t + 1) * P], xn[:, t, c * P:(c + 1) * P], ident[:])
                ins.then_inc(out_done, 1)

            def bias_logits(n, use, l, b):
                pe.wait_ge(hT_ready, n + 1)
                pe.wait_ge(out_free, use)
                pe.wait_ge(wb_ready, l + 1)
                for t in range(QT):
                    out = out_ps[:, t * HEADS:(t + 1) * HEADS]
                    i = 0
                    for c in range(DC):
                        for s, s2 in PASSES:
                            nc.tensor.matmul(out, hT[:, s, c, b * LQ + t * P:b * LQ + (t + 1) * P], wbS[:, s2, l, c], start=(i == 0), stop=False)
                            i += 1
                    ins = nc.tensor.matmul(out, ones[:], bqk[:, l], start=False, stop=True)
                ins.then_inc(out_done, 1)

            def scores0(b):
                pe.wait_ge(fill_lo, FILL[f"G{b}"] + 1)
                if b:
                    pe.wait_ge(exp_done, 2 * b)
                for t in range(QT):
                    ins = product(scores[:, t], [(lambda s, j=j: gS[:, s, j, t * P:(t + 1) * P], lambda s, j=j: cT[:, s, j, b * T:(b + 1) * T])
                                                 for j in range(DC)])
                ins.then_inc(scores_done, 1)

            pe.wait_ge(consts_ready, 5)
            for name in first_fills:
                startup_fill(name)
            scores0(0)
            for name in second_fills:
                startup_fill(name)
            for b in range(B):
                if b < B - 1:
                    scores0(b + 1)
                pe.wait_ge(exp_done, 2 * b + 2)
                transposes(b)
                for name in slot_fills[b]:
                    startup_fill(name)
                pe.wait_ge(nat_ready, b + 1)
                if b:
                    pe.wait_ge(mix_lo, b)
                pe.wait_ge(pt_lo, 2 * b + 2)
                for i in range(DC):
                    ins = product(mix_ps[:, i * LQ:(i + 1) * LQ],
                                  [(lambda s, c=c: nat[:, b % 2, s, c, i * P:(i + 1) * P], lambda s, c=c: probsT[:, s, c]) for c in range(TC)])
                ins.then_inc(mix_done, 1)
                if b:
                    ln_transposes(b - 1, use0(f"lnT{b-1}"))
                pe.wait_ge(mix_lo, b + 1)
                pe.wait_ge(fill_lo, FILL["N"] + 1)
                if b:
                    pe.wait_ge(out_free, use0(f"delta{b}"))
                for t in range(QT):
                    ins = product(out_ps[:, t * D:(t + 1) * D],
                                  [(lambda s, i=i: mixT[:, s, i, t * P:(t + 1) * P], lambda s, i=i: nS[:, s, i]) for i in range(DC)])
                ins.then_inc(out_done, 1)
            pe.wait_ge(hT_ready, 1)
            startup_fill("Q")
            bias_logits(0, use0("sb0"), 0, 0)
            unit_scores(0, 0, 0, FILL["Q"])
            startup_fill("RA3")
            bias_logits(1, use0("sb1"), 0, 1)
            bias_logits(2, use0("sb2"), 0, 2)
            ln_transposes(B - 1, use0(f"lnT{B-1}"))
            startup_fill("RB0")
            bias_logits(3, use0("sb3"), 0, 3)

            def ra_pair(r):
                pe.wait_ge(out_free, use_ra(r))
                pe.wait_ge(d_wo, r * 16 + 16 * (CHUNKS + 1))
                for c in range(DC):
                    for h in range(2):
                        at = (c * 2 + h) * 2
                        v = vt2[:, 1, bass.ds(r * 2 + h, 1), :].rearrange("p a v -> p (a v)")
                        ins = nc.tensor.matmul(out_ps[:, at:at + 2], ck_wo[:, h, c * P:(c + 1) * P], v, start=True, stop=True)
                ins.then_inc(out_done, 1)

            def body(l, r, nxt):
                last = isinstance(r, int)
                for k in range(UNITS):
                    b, h = k // 2, k % 2
                    u = unit(l, r, k)
                    to = (l, r, b + 1) if b < B - 1 else (nxt + (0,) if nxt else None)
                    after = (l, r, k + 1) if k < UNITS - 1 else (nxt + (0,) if nxt else None)
                    if h == 0 and after:
                        unit_scores(*after, step_fill(l, r, b, 2))
                    pe.wait_ge(norm_done, u - B + 1)
                    transposes(u)
                    if h == 1 and after:
                        unit_scores(*after, step_fill(l, r, b + 1, 1))

                    def fill(kind):
                        if to:
                            step_fill_mm(step_fill(l, r, b + 1, kind), kind, *to, (NF0 + 5 * b + kind) % 2)

                    if h == 0:
                        fill(0)
                        if l == 0 and k == 2:
                            ra_pair(r)
                        fill(1)
                        if last and l == 0 and b >= 2:
                            bias_logits(4 * (l + 1) + b - 2, use_last(l, f"sb{b - 2}"), 1, b - 2)
                        mix(l, r, k, step_fill(l, r, b, 4))
                        fill(2)
                        if last and b:
                            ln_transposes(4 * (l + 1) + b - 1, use_last(l, f"lnT{b - 1}"))
                    else:
                        fill(3)
                        mix(l, r, k, None)
                        if last:
                            pe.wait_ge(out_free, use_last(l, f"pbT{b}"))
                            pe.wait_ge(pb_ready, (PAIRS - 1 + B) * l + PAIRS + b)
                            for t in range(QT):
                                ins = nc.tensor.transpose(out_ps[:, t * P:(t + 1) * P], p_bias[:, QT * b + t], ident[:])
                            ins.then_inc(out_done, 1)
                        fill(4)
                        step_out(l, r, b)

            for l in range(2):
                with pe.Fori(0, PAIRS - 1) as r:
                    body(l, r, (l, r + 1))
                body(l, PAIRS - 1, (1, 0) if l == 0 else None)
                n = 4 * (l + 1) + B - 1
                if l == 0:
                    bias_logits(n - 1, use_last(l, f"sb{B - 2}"), 1, B - 2)
                ln_transposes(n, use_last(l, f"lnT{B - 1}"))
                if l == 0:
                    bias_logits(n, use_last(l, f"sb{B - 1}"), 1, B - 1)
                    pe.wait_ge(rt_ready, 2)
                    pe.wait_ge(out_free, use_last(0, "rb"))
                    for c in range(DC):
                        ins = nc.tensor.transpose(out_ps[:, c * P:(c + 1) * P], rt[:, c], ident[:])
                    ins.then_inc(out_done, 1)

            for half in range(2):
                for f in range(FC):
                    n = half * FC + f
                    fill_bank(MLP_FILL + n)
                    if n == 0:
                        pe.wait_ge(mlp_ready, 1)
                    if f == 0:
                        pe.wait_ge(hT_ready, 8 + 2 * half + 2)
                    ins = product(proj[(MLP_FILL + n) % 2][:],
                                  [(lambda s, c=c: w1S[:, s, c, f * P:(f + 1) * P], lambda s, c=c: hT[:, s, c, half * 2 * LQ:(half + 1) * 2 * LQ]) for c in range(DC)])
                    ins.then_inc(fill_done, 1)
                if half == 0:
                    pe.wait_ge(mlp_ready, 2)
                pe.wait_ge(fill_lo, MLP_FILL + (half + 1) * FC)
                if half == 0:
                    pe.wait_ge(out_free, USES)
                for i in range(2):
                    b = 2 * half + i
                    if half:
                        pe.wait_ge(result_ready, b - 1)
                    gelu = (gelu_hi, gelu_lo)
                    for t in range(QT):
                        q0 = i * LQ + t * P
                        ins = product((out_ps, mix_ps)[i][:, t * D:(t + 1) * D],
                                      [(lambda s, f=f: gelu[s][:, f, q0:q0 + P], lambda s, f=f: w2S[:, s, f]) for f in range(FC)])
                    ins.then_inc(down_done, 1)


_INS = (["x", "ctx_2048", "L0_xattn_w_q", "L0_xattn_w_k", "L0_xattn_w_v", "L0_xattn_w_o", "L0_xattn_alpha"]
        + [f"L1_xattn_{n}{i}{s}" for i in (1, 2) for n, s in (("ln", "_scale"), ("ln", "_offset"), ("wq", ""), ("bq", ""), ("wk", ""),
           ("bk", ""), ("wv", ""), ("bv", ""), ("wo", ""), ("bo", ""), ("bias_k", ""), ("bias_v", ""))]
        + ["L1_xattn_ln_mlp_scale", "L1_xattn_ln_mlp_offset", "L1_xattn_w_fc1", "L1_xattn_b_fc1", "L1_xattn_w_fc2", "L1_xattn_b_fc2"])


def kernel(**inputs):
    import numpy as _np
    import concourse.bacc as _bacc
    from concourse import mybir as _mybir
    from concourse.bass_utils import run_bass_kernel_spmd as _run

    nc = _bacc.Bacc("TRN2", target_bir_lowering=False, num_devices=1)
    arrays, aps = {}, {}
    for name in _INS:
        a = _np.ascontiguousarray(inputs[name])
        if a.ndim == 0:
            a = a.reshape(1)
        arrays[f"in_{name}_dram"] = a
        aps[name] = nc.dram_tensor(f"in_{name}_dram", a.shape, _mybir.dt.from_np(a.dtype), kind="ExternalInput").ap()
    aps["out"] = nc.dram_tensor("out_0_dram", (B, LQ, D), _mybir.dt.float32, kind="ExternalOutput").ap()
    xattn_kernel(nc, aps)
    r = _run(nc, [arrays], core_ids=[0])
    return r.results[0]["out_0_dram"]
```

```python
from contextlib import ExitStack

import concourse.bass as bass
from concourse import mybir

F32 = mybir.dt.float32
F32R = mybir.dt.float32r
ALU = mybir.AluOpType
ACT = mybir.ActivationFunctionType
AX_X = mybir.AxisListType.X

P = 128
B, LQ, D = 4, 256, 256
T = 512
HEADS, DH = 16, 128
F = 1024
QT = LQ // P
DC = D // P
TC = T // P
FC = F // P
PAIRS = HEADS // 2
PW = 2 * DH
RW = 1 + HEADS
UNITS = 2 * B
EPS = 1e-5
SCALE0 = float(D) ** -0.5
SCALE = float(DH) ** -0.5
WK, WQ, WV, WO = range(4)
HI, LO = 0, 1
PASSES = ((HI, LO), (LO, HI), (HI, HI))
BQ, BK, BV, BIAS_K, BIAS_V, LN_G, LN_O, FC1_B = 0, 16, 32, 48, 64, 80, 82, 84
CHUNK_H = 4
CHUNKS = HEADS // CHUNK_H


def startup_fills():
    first = ["xT0", "cT00", "M", "cT01", "xT1", "G0", "cT10"]
    second = ["cT11", "G1", "WoT"]
    slots = [(["xT2", "cT20", "cT21", "N"], ["G2", "vec"]),
             (["xT3", "cT30", "cT31", "K0", "K1"], ["G3", "bqk"]),
             (["Va"], ["Vb"]),
             ([], ["Q"])]
    return first, second, slots, first + second + sum((before + after for before, after in slots), [])


def xattn_kernel(nc, A):
    first_fills, second_fills, slot_fills, fill_order = startup_fills()
    FILL = {name: n for n, name in enumerate(fill_order)}
    NF0 = len(fill_order)
    MLP_FILL = NF0 + 2 * 5 * B * PAIRS - 5
    MLP_ORDER = [1, 0, 2, 3]

    def unit(l, r, k):
        return r * UNITS + (B + UNITS * PAIRS * l + k)

    def step_fill(l, r, b, f):
        return r * (5 * B) + (NF0 + 5 * B * PAIRS * l + 5 * b + f - 5)

    START = ["delta0", "lnT0.0", "delta1", "lnT0.1", "delta2", "lnT0.2", "delta3", "sbT0.0", "sb0.0", "sbT0.1", "sb0.1"]
    FIRST = [[f"sbT{l}.2", "r", f"sb{l}.2", f"lnT{l}.3", "out0", f"sbT{l}.3", f"sb{l}.3", "out1", "out2", "out3"] for l in range(2)]
    LAST = [["r", "pbT0", "out0", "lnT1.0", "pbT1", "out1", "sbT1.0", "sb1.0", "lnT1.1",
             "pbT2", "out2", "sbT1.1", "sb1.1", "lnT1.2", "pbT3", "out3"],
            ["r", "pbT0", "out0", "lnT2.0", "pbT1", "out1", "lnT2.1", "pbT2", "out2", "lnT2.2", "pbT3", "out3", "lnT2.3"]]
    PER_PAIR = B + 1
    FIRST_AT, LOOP_AT, LAST_AT, USES = [], [], [], len(START)
    for l in range(2):
        FIRST_AT.append(USES)
        LOOP_AT.append(USES + len(FIRST[l]))
        LAST_AT.append(LOOP_AT[l] + PER_PAIR * (PAIRS - 2))
        USES = LAST_AT[l] + len(LAST[l])
    NAMED = {}
    for at, names in zip([0] + FIRST_AT + LAST_AT, [START] + FIRST + LAST):
        for n, name in enumerate(names):
            if "." in name or name.startswith("delta"):
                NAMED[name] = at + n

    def is_first(r):
        return isinstance(r, int) and r == 0

    def is_last(r):
        return isinstance(r, int) and r == PAIRS - 1

    def use_of(l, r, what):
        at, names = (FIRST_AT, FIRST) if r == 0 else (LAST_AT, LAST)
        return at[l] + names[l].index(what)

    def use_out(l, r, b):
        if isinstance(r, int):
            return use_of(l, r, f"out{b}")
        return r * PER_PAIR + (LOOP_AT[l] - PER_PAIR + b + 1)

    def use_r(l, r):
        return use_of(l, r, "r") if isinstance(r, int) else r * PER_PAIR + (LOOP_AT[l] - PER_PAIR)

    def ln_of_step(l, r, b):
        if is_last(r) and b:
            return l + 1, b - 1, b - 2 if l == 0 and b >= 2 else None
        if is_first(r) and b < 2:
            return l, B - 1 if b == 0 else None, B - 2 + b
        return None, None, None

    with ExitStack() as ctx:
        def sb(name, shape, dt=F32):
            return ctx.enter_context(nc.sbuf_tensor(name, shape, dt))

        def ps(name, shape):
            return ctx.enter_context(nc.psum_tensor(name, shape, F32))

        def sem(name):
            return ctx.enter_context(nc.semaphore(name))

        scores = ps("scores", [P, QT, T])
        probsT_ps = ps("probsT_ps", [P, TC, LQ])
        proj = [ps(f"proj{i}", [P, 512]) for i in range(2)]
        mix_ps = ps("mix_ps", [P, 512])
        out_ps = ps("out_ps", [P, 512])

        down_ps = [[out_ps[:, 0:D], scores[:, 0, 0:D]], [mix_ps[:, 0:D], scores[:, 1, 0:D]]]

        cT = sb("cT", [P, 2, DC, B * T], F32R)
        hT = sb("hT", [P, 2, DC, B * LQ], F32R)
        wS = sb("wS", [P, 2, 4, DC, PW], F32R)
        kT = sb("kT", [P, 2, 2, T], F32R)
        qT = sb("qT", [P, 2, 2, LQ], F32R)
        vS = sb("vS", [P, 2, 2, TC, PW], F32R)
        probsT = sb("probsT", [P, 2, TC, LQ], F32R)
        mixT = sb("mixT", [P, 2, 2, LQ], F32R)
        arena = sb("arena", [P, 8192], F32R)
        nat = arena[:, 0:4096].rearrange("p (n s c d) -> p n s c d", n=2, s=2, c=TC)
        w0S = arena[:, 4096:8192].rearrange("p (s w c d) -> p s w c d", s=2, w=4, c=DC)
        w1S = arena[:, 0:4096].rearrange("p (s c f) -> p s c f", s=2, c=DC)
        w2S = arena[:, 4096:8192].rearrange("p (s c d) -> p s c d", s=2, c=FC)
        nS = w0S[:, :, WK]
        mS = sb("mS", [P, 2, DC, D], F32R)
        gS = sb("gS", [P, 2, DC, LQ], F32R)
        rS = sb("rS", [RW, 2, 2, D], F32R)
        ev = sb("ev", [P, 2, 2, HEADS, RW], F32R)
        ev_pair = sb("ev_pair", [P, 2, 2, RW], F32R)
        wbS = sb("wbS", [P, 2, 2, DC, HEADS], F32R)
        pbT = sb("pbT", [RW, 2, LQ], F32R)
        gelu = [[vS[:, (f // 2) % 2, f // 4, 2 * (f % 2):2 * (f % 2) + 2].rearrange("p c d -> p (c d)") for f in range(FC)],
                [wS[:, s, w].rearrange("p c d -> p (c d)") for w in (WK, WQ, WV, WO) for s in (HI, LO)]]

        x = sb("x", [P, B * QT, D])
        w_raw = sb("w_raw", [P, 4, DC, PW])
        nat_raw = sb("nat_raw", [P, 2, TC, D])
        ck_wq = sb("ck_wq", [P, 2, DC, CHUNK_H * DH])
        ck_bk = sb("ck_bk", [P, 2, CHUNK_H * DH])
        w1_raw = nat_raw[:].rearrange("p n c d -> p (n c d)").rearrange("p (c f) -> p c f", c=DC)
        w2_raw = w_raw[:].rearrange("p w c n -> p (w c) n")
        probs = sb("probs", [P, QT, T])
        gelu_full = ck_wq[:, 0]
        xn = sb("xn", [P, QT, D])
        h_full = sb("h_full", [P, DC, LQ])
        p_bias = sb("p_bias", [P, B * QT, RW])
        vec_raw = sb("vec_raw", [P, 2, P])
        vecT = sb("vecT", [P, 2, P])
        ident = sb("ident", [P, P])
        ones = sb("ones", [P, 1])
        b2_row = sb("b2_row", [P, D])
        alpha = sb("alpha", [P, 1])
        v_diff = sb("v_diff", [P, 2, HEADS])
        bqk = sb("bqk", [P, 2, HEADS])
        bqk_sum = sb("bqk_sum", [HEADS, 2])
        logits = sb("logits", [HEADS, LQ])
        wb_full = sb("wb_full", [P, 2, DC, HEADS])
        r_full = sb("r_full", [RW, 2, D])
        wb_two = sb("wb_two", [P, DC, 2])
        p_pair = sb("p_pair", [P, B * QT, 2])
        act_bias = sb("act_bias", [P, 2, 2])
        nsb = sb("nsb", [P, B * QT, HEADS])
        mx = sb("mx", [P, QT])
        shift = sb("shift", [P, QT])
        z = sb("z", [P, QT])
        eb = sb("eb", [P, QT])
        zsum = sb("zsum", [P, QT])
        rz = sb("rz", [P, QT])
        rz0 = sb("rz0", [P, B, QT])
        bn = sb("bn", [P, QT, 6])
        mv = sb("mv", [P, QT, 2])
        var = sb("var", [P, QT])
        minus_half = sb("minus_half", [P, QT])
        rstd = sb("rstd", [P, QT])

        d_w0 = [sem(f"d_w0_{i}") for i in range(4)]
        d_nat = [sem(f"d_nat{i}") for i in range(2)]
        d_x, d_alpha, d_out = sem("d_x"), sem("d_alpha"), sem("d_out")
        d_vec = sem("d_vec")
        d_small = sem("d_small")
        d_mlp = [sem(f"d_mlp_fc{i}") for i in (1, 2)]
        d_wq, d_bk = ([sem(f"d_{n}{i}") for i in range(2)] for n in ("ck_wq", "ck_bk"))
        d_w = [sem(f"d_w_{n}") for n in "kqvo"]

        consts_ready = sem("consts_ready")
        w0_hi, w0_ready = sem("w0_hi"), sem("w0_ready")
        nat_hi, nat_ready = sem("nat_hi"), sem("nat_ready")
        split_hi = [sem(f"split_hi_{n}") for n in "kqvo"]
        w_ready = [sem(f"w_ready_{n}") for n in "kqvo"]
        mlp_hi, mlp_ready = sem("mlp_hi"), sem("mlp_ready")
        wb_products, wb_used = sem("wb_products"), sem("wb_used")
        wb_pairs, wb_ready = sem("wb_pairs"), sem("wb_ready")
        act_bias_ready, ev_ready = sem("act_bias_ready"), sem("ev_ready")
        r_ready = sem("r_ready")

        fill_done, fill_hi, fill_lo = sem("fill_done"), sem("fill_hi"), sem("fill_lo")
        scores_done = sem("scores_done")
        pt_done, pt_hi, pt_lo = sem("pt_done"), sem("pt_hi"), sem("pt_lo")
        mix_done, mix_hi, mix_lo = sem("mix_done"), sem("mix_hi"), sem("mix_lo")
        out_done, out_free = sem("out_done"), sem("out_free")
        pbT_hi = sem("pbT_hi")
        down_done, result_ready = sem("down_done"), sem("result_ready")

        max_ready, shift_ready = sem("max_ready"), sem("shift_ready")
        exp_done, eb_ready = sem("exp_done"), sem("eb_ready")
        zsum_ready, rz_ready = sem("zsum_ready"), sem("rz_ready")
        norm_done, pb_ready = sem("norm_done"), sem("pb_ready")
        var_ready, rstd_ready, xn_ready, hT_ready = (sem(n) for n in ("var_ready", "rstd_ready", "xn_ready", "hT_ready"))
        pool_chain, chain = sem("pool_chain"), sem("dve_chain")

        w0_dram = [A["L0_xattn_w_k"], A["L0_xattn_w_q"], A["L0_xattn_w_v"], A["L0_xattn_w_o"]]

        def stage_dram(l, name):
            return A[f"L1_xattn_{name}{l + 1}"]

        def pair_dram(l, w, r):
            if w == WO:
                v = stage_dram(l, "wo").rearrange("(h d) n -> d h n", d=DH)
                return v[:, bass.ds(r * 2, 2), :]
            v = stage_dram(l, {WK: "wk", WQ: "wq", WV: "wv"}[w]).rearrange("(c p) n -> p c n", p=P)
            return v[:, :, bass.ds(r * PW, PW)]

        block = ctx.enter_context(nc.Block())

        @block.sync
        def _(sp):
            ctx_dram = A["ctx_2048"].rearrange("b (c p) d -> b p c d", p=P)

            def load_w0(w):
                sp.dma_start(w_raw[:, w], w0_dram[w].rearrange("(c p) n -> p c n", p=P)).then_inc(d_w0[w], 16)

            def load_pair(l, w, r):
                sp.dma_start(w_raw[:, w], pair_dram(l, w, r)).then_inc(d_w[w], 16)

            sp.dma_start(nat_raw[:, 0], ctx_dram[0]).then_inc(d_nat[0], 16)
            load_w0(WQ)
            load_w0(WK)
            sp.dma_start(x[:], A["x"].rearrange("b (t p) d -> p (b t) d", p=P)).then_inc(d_x, 16)
            sp.dma_start(nat_raw[:, 1], ctx_dram[1]).then_inc(d_nat[1], 16)
            load_w0(WV)
            load_w0(WO)
            sp.dma_start(alpha[:], A["L0_xattn_alpha"].partition_broadcast(P)).then_inc(d_alpha, 16)
            sp.wait_ge(consts_ready, 6)
            rows = [("bq", BQ), ("bk", BK), ("bv", BV), ("bias_k", BIAS_K), ("bias_v", BIAS_V)]
            for l in range(2):
                for name, at in rows:
                    v = stage_dram(l, name)
                    if len(v.shape) == 4:
                        v = v.rearrange("a b h k -> (a b h) k")
                    else:
                        v = v.rearrange("(h k) -> h k", k=DH)
                    sp.dma_start(vec_raw[at:at + HEADS, l, :], v).then_inc(d_vec, 16)
                for v, at in ((A[f"L1_xattn_ln{l+1}_scale"], LN_G), (A[f"L1_xattn_ln{l+1}_offset"], LN_O)):
                    sp.dma_start(vec_raw[at:at + DC, l, :], v.rearrange("(c k) -> c k", k=P)).then_inc(d_vec, 16)
            for v, at, n in ((A["L1_xattn_b_fc1"], FC1_B, FC), (A["L1_xattn_ln_mlp_scale"], FC1_B + FC, DC),
                             (A["L1_xattn_ln_mlp_offset"], FC1_B + FC + DC, DC)):
                sp.dma_start(vec_raw[at:at + n, 0, :], v.rearrange("(c k) -> c k", k=P)).then_inc(d_vec, 16)

            def ctx_batch(b):
                sp.wait_ge(fill_done, FILL[f"cT{b-2}1"] + 1)
                sp.wait_ge(nat_ready, b - 1)
                sp.dma_start(nat_raw[:, b % 2], ctx_dram[b]).then_inc(d_nat[b % 2], 16)

            ctx_batch(2)
            sp.wait_ge(w0_ready, 3)
            for w in (WK, WQ, WV):
                load_pair(0, w, 0)

            wq_cols = [stage_dram(l, "wq").rearrange("(c p) n -> p c n", p=P) for l in range(2)]
            bk_cols = [stage_dram(l, "bias_k").rearrange("a b h k -> (a b h k)") for l in range(2)]

            def heads_of_wq(l, first, n, c=0):
                cols = bass.ds(first * DH, n * DH)
                sp.dma_start(ck_wq[:, c % 2, :, 0:n * DH], wq_cols[l][:, :, cols]).then_inc(d_wq[c % 2], 16)
                sp.dma_start(ck_bk[:, c % 2, 0:n * DH], bk_cols[l][cols].partition_broadcast(P)).then_inc(d_bk[c % 2], 16)

            for c in range(2):
                heads_of_wq(0, c * CHUNK_H, CHUNK_H, c)
            sp.wait_ge(fill_done, FILL["WoT"] + 1)
            load_pair(0, WO, 0)
            ctx_batch(3)
            sp.dma_start(b2_row[:], A["L1_xattn_b_fc2"].partition_broadcast(P)).then_inc(d_small, 16)
            for l in range(2):
                sp.dma_start(r_full[0:1, l, :], stage_dram(l, "bo").rearrange("(a n) -> a n", a=1)).then_inc(d_small, 16)

            for c in range(2, CHUNKS):
                sp.wait_ge(wb_used, c - 1)
                heads_of_wq(0, c * CHUNK_H, CHUNK_H, c)
            sp.wait_ge(wb_used, CHUNKS)
            heads_of_wq(1, 0, 2)

            def next_pair(l, r, ln, rn):
                for w in (WK, WQ, WV, WO):
                    sp.wait_ge(w_ready[w], r + (PAIRS * l + 1))
                    load_pair(ln, w, rn)

            def next_heads(r):
                sp.wait_ge(wb_used, r + (CHUNKS + 1))
                heads_of_wq(1, r * 2 + 2, 2)

            next_pair(0, 0, 0, 1)
            next_heads(0)
            with sp.Fori(1, PAIRS - 1) as r:
                next_pair(0, r, 0, r + 1)
                next_heads(r)
            next_pair(0, PAIRS - 1, 1, 0)
            sp.dma_start(w1_raw, A["L1_xattn_w_fc1"].rearrange("(c p) f -> p c f", p=P)).then_inc(d_mlp[0], 16)
            with sp.Fori(0, PAIRS - 1) as r:
                next_pair(1, r, 1, r + 1)
            for w in range(4):
                sp.wait_ge(w_ready[w], 2 * PAIRS)
            sp.dma_start(w2_raw, A["L1_xattn_w_fc2"].rearrange("(c p) n -> p c n", p=P)).then_inc(d_mlp[1], 16)
            out_dram = A["out"].rearrange("b (t p) d -> b p t d", p=P)
            for n, b in enumerate(MLP_ORDER):
                sp.wait_ge(result_ready, n + 1)
                sp.dma_start(out_dram[b], x[:, QT * b:QT * (b + 1), :]).then_inc(d_out, 16)
            sp.wait_ge(d_out, 16 * B)

        @block.gpsimd
        def _(pool):
            links = [0]

            def link(ins):
                links[0] += 1
                ins.then_inc(pool_chain, 1)
                pool.wait_ge(pool_chain, links[0])

            nc.gpsimd.memset(vec_raw[:], 0.0).then_inc(consts_ready, 1)
            link(nc.gpsimd.memset(ident[:], 0.0))
            nc.gpsimd.affine_select(out=ident[:], in_=ident[:], compare_op=ALU.not_equal, fill=1.0, base=0,
                                    pattern=[[-1, P]], channel_multiplier=1).then_inc(consts_ready, 1)
            nc.gpsimd.memset(minus_half[:], -0.5)
            nc.gpsimd.memset(ones[:], 1.0).then_inc(consts_ready, 1)
            nc.gpsimd.memset(r_full[:], 0.0).then_inc(consts_ready, 1)
            nc.gpsimd.memset(ev[:].bitcast(F32), 0.0).then_inc(consts_ready, 1)
            link(nc.gpsimd.memset(p_bias[:], 0.0))
            nc.gpsimd.memset(p_bias[:, :, 0:1], 1.0).then_inc(consts_ready, 1)

            def split(hi, lo, raw, hi_sem, hi_count, done_sem):
                one = (ones[:, 0:1] if len(raw.shape) == 2 else ones[:, 0:1].rearrange("p (a b) -> p a b", a=1)).broadcast_to(raw.shape)
                nc.gpsimd.tensor_tensor(hi, raw, one, ALU.mult).then_inc(hi_sem, 1)
                pool.wait_ge(hi_sem, hi_count)
                nc.gpsimd.tensor_tensor(lo, raw, hi.bitcast(F32), ALU.subtract).then_inc(done_sem, 1)

            def split_ctx(b):
                pool.wait_ge(nat_hi, b + 1)
                nc.gpsimd.tensor_tensor(nat[:, b % 2, LO], nat_raw[:, b % 2], nat[:, b % 2, HI].bitcast(F32), ALU.subtract).then_inc(nat_ready, 1)

            def split_w(w, l, r, used=None):
                pool.wait_ge(d_w[w], r * 16 + 16 * (PAIRS * l + 1))
                if used:
                    pool.wait_ge(*used)
                split(wS[:, HI, w], wS[:, LO, w], w_raw[:, w], split_hi[w], r + (PAIRS * l + 1), w_ready[w])

            def ln_rstd(n):
                pool.wait_ge(var_ready, n + 1)
                nc.gpsimd.tensor_tensor(rstd[:], var[:], minus_half[:], ALU.pow).then_inc(rstd_ready, 1)

            split_ctx(0)
            split_ctx(1)
            for w in (WK, WV, WQ):
                split_w(w, 0, 0)

            def wb_product(c):
                pool.wait_ge(d_wq[c % 2], 16 * (c // 2 + 1))
                pool.wait_ge(d_bk[c % 2], 16 * (c // 2 + 1))
                for i in range(DC):
                    ins = nc.gpsimd.tensor_tensor(ck_wq[:, c % 2, i], ck_wq[:, c % 2, i], ck_bk[:, c % 2], ALU.mult)
                ins.then_inc(wb_products, 1)

            wb_product(0)
            ln_rstd(0)
            wb_product(1)
            split_ctx(2)
            ln_rstd(1)
            wb_product(2)
            split_ctx(3)
            wb_product(3)
            ln_rstd(2)
            ln_rstd(3)

            def normalise(l, r, k):
                b, h = k // 2, k % 2
                u = unit(l, r, k)
                for t in range(QT):
                    pool.wait_ge(rz_ready, u * 2 + (t + 1 - 2 * B))
                    nc.gpsimd.tensor_tensor(p_pair[:, QT * b + t, h:h + 1], eb[:, t:t + 1], rz[:, t:t + 1], ALU.mult)
                    ins = nc.gpsimd.tensor_scalar(probs[:, t], probs[:, t], rz[:, t:t + 1], 1.0, ALU.mult, ALU.mult)
                ins.then_inc(norm_done, 1)

            normalise(0, 0, 0)

            def mlp_part(k):
                if k is None:
                    return
                half, part = k // 4, k % 4
                if part == 0:
                    pool.wait_ge(d_mlp[half], 16)
                if half == 0:
                    at = (slice(None), part // 2, slice((part % 2) * 512, (part % 2 + 1) * 512))
                    hi, lo, raw = w1S[:, HI][at], w1S[:, LO][at], w1_raw[at]
                else:
                    at = slice(2 * part, 2 * part + 2)
                    hi, lo, raw = w2S[:, HI, at], w2S[:, LO, at], w2_raw[:, at]
                split(hi, lo, raw, mlp_hi, k + 1, mlp_ready)

            def body(l, r, nxt):
                for k in range(UNITS):
                    b = k // 2
                    if k == 0:
                        before = FIRST_AT[l] if is_first(r) else use_r(l, r)
                        split_w(WO, l, r, used=None if l == 0 and is_first(r) else (out_done, before))
                    if nxt and k == 5:
                        split_w(WK, *nxt, used=(fill_done, step_fill(l, r, 3, 2) + 1))
                        split_w(WQ, *nxt)
                    if nxt and k == 6:
                        split_w(WV, *nxt, used=(fill_done, step_fill(l, r, 3, 4) + 1))
                    if is_last(r) and b and k % 2 == 0:
                        ln_rstd(4 * (l + 1) + b - 1)
                    mlp_part(k if nxt is None else None)
                    if k < UNITS - 1:
                        normalise(l, r, k + 1)
                    elif nxt:
                        normalise(nxt[0], nxt[1], 0)

            def layer(l):
                body(l, 0, (l, 1))
                with pool.Fori(1, PAIRS - 1) as r:
                    body(l, r, (l, r + 1))

            layer(0)
            body(0, PAIRS - 1, (1, 0))
            ln_rstd(4 + B - 1)
            layer(1)
            body(1, PAIRS - 1, None)
            ln_rstd(8 + B - 1)

        @block.scalar
        def _(act):
            def hi_copy(f, dst, src):
                act.wait_ge(fill_done, f + 1)
                return nc.scalar.activation(dst, src, ACT.Copy)

            def hi_biased(f, l, r, dst_src_row):
                act.wait_ge(fill_done, f + 1)
                act.wait_ge(act_bias_ready, r + (PAIRS * l + 1))
                for dst, src, (which, h) in dst_src_row:
                    ins = nc.scalar.activation(dst, src, ACT.Identity, bias=act_bias[:, which, h:h + 1])
                return ins

            def pair_bias(l, r):
                both = vecT[:, l, 0:2 * HEADS].rearrange("p (w h) -> p w h", w=2)
                nc.scalar.activation(act_bias[:], both[:, :, bass.ds(r * 2, 2)], ACT.Copy).then_inc(act_bias_ready, 1)

            def pair_values(l, r):
                nc.scalar.activation(ev_pair[:], ev[:, :, l, bass.ds(r * 2, 2), :], ACT.Copy).then_inc(ev_ready, 1)

            def startup_fill(name):
                f = FILL[name]
                pj = proj[f % 2]
                halves = pj[:].rearrange("p (a n) -> p a n", a=2)
                b = int(name[2]) if name[0] in "xc" else 0
                if name == "vec":
                    ins = hi_copy(f, vecT[:], pj[:, 0:2 * P].rearrange("p (a n) -> p a n", a=2))
                elif name == "M":
                    ins = hi_copy(f, mS[:, HI], halves)
                elif name[:2] == "xT":
                    ins = hi_copy(f, hT[:, HI, :, b * LQ:(b + 1) * LQ], halves)
                elif name[:2] == "cT":
                    ins = hi_copy(f, cT[:, HI, int(name[3]), b * T:(b + 1) * T], pj[:])
                elif name == "WoT":
                    ins = hi_copy(f, w0S[:, HI, WO], halves)
                elif name == "N":
                    ins = hi_copy(f, nS[:, HI], halves)
                elif name[0] == "G":
                    ins = hi_copy(f, gS[:, HI], halves)
                elif name == "bqk":
                    ins = hi_copy(f, bqk_sum[:, 0:1], pj[0:HEADS, 0:1])
                else:
                    return step_fill_hi(f, {"K0": 0, "Q": 1, "K1": 2, "Va": 3, "Vb": 4}[name], 0, 0, 0, f % 2)
                ins.then_inc(fill_hi, 1)

            def step_fill_hi(f, kind, l, r, b, bank):
                pj = proj[bank]
                if kind in (0, 2):
                    h = kind // 2
                    ins = hi_biased(f, l, r, [(kT[:, HI, h], pj[:], (1, h))])
                elif kind == 1:
                    ins = hi_biased(f, l, r, [(qT[:, HI, h], pj[:, h * LQ:(h + 1) * LQ], (0, h)) for h in range(2)])
                else:
                    c = 2 * (kind - 3)
                    ins = hi_copy(f, vS[:, HI, b % 2, c:c + 2], pj[:].rearrange("p (c n) -> p c n", c=2))
                ins.then_inc(fill_hi, 1)

            def probsT_hi(u):
                for j in range(2):
                    act.wait_ge(pt_done, u * 2 + (j + 1))
                    nc.scalar.activation(probsT[:, HI, 2 * j:2 * j + 2], probsT_ps[:, 2 * j:2 * j + 2], ACT.Copy).then_inc(pt_hi, 1)

            def mix_hi_copy(u, dst, src):
                act.wait_ge(mix_done, u + 1)
                nc.scalar.activation(dst, src, ACT.Copy).then_inc(mix_hi, 1)

            def exps0(b):
                act.wait_ge(shift_ready, b + 1)
                for t in range(QT):
                    nc.scalar.activation(probs[:, t], scores[:, t], ACT.Exp, bias=shift[:, t:t + 1], scale=SCALE0,
                                         accum_out=z[:, t:t + 1]).then_inc(exp_done, 1)

            def exps(l, r, k, between=lambda: None):
                b, h = k // 2, k % 2
                act.wait_ge(shift_ready, unit(l, r, k) + 1)

                def tile_exp(t):
                    nc.scalar.activation(probs[:, t], scores[:, t], ACT.Exp, bias=shift[:, t:t + 1], scale=SCALE,
                                         accum_out=z[:, t:t + 1]).then_inc(exp_done, 1)

                tile_exp(0)
                between()
                for t in range(QT):
                    ins = nc.scalar.activation(eb[:, t:t + 1], nsb[:, QT * b + t, bass.ds(r * 2 + h, 1)], ACT.Exp,
                                               bias=shift[:, t:t + 1], scale=-1.0)
                ins.then_inc(eb_ready, 1)
                tile_exp(1)

            def ln_full(n, use, l):
                act.wait_ge(out_done, use + 1)
                if n:
                    act.wait_ge(hT_ready, n)
                g, o = (LN_G, LN_O) if l < 2 else (FC1_B + FC, FC1_B + FC + DC)
                src = out_ps[:].rearrange("p (c q) -> p c q", c=DC)
                for c in range(DC):
                    ins = nc.scalar.activation(h_full[:, c], src[:, c], ACT.Identity, bias=vecT[:, l % 2, o + c:o + c + 1],
                                               scale=vecT[:, l % 2, g + c:g + c + 1])
                ins.then_inc(out_free, 1)

            def mlp_gelu(n):
                f = n % FC
                act.wait_ge(fill_done, MLP_FILL + n + 1)
                if n >= 2:
                    act.wait_ge(fill_lo, MLP_FILL + n - 1)
                nc.scalar.activation(gelu_full[:, n % 2], proj[(MLP_FILL + n) % 2][:], ACT.Gelu,
                                     bias=vecT[:, 0, FC1_B + f:FC1_B + f + 1]).then_inc(fill_hi, 1)

            def ctx_hi(b):
                act.wait_ge(d_nat[b % 2], 16 * (b // 2 + 1))
                if b >= 2:
                    act.wait_ge(mix_done, b - 1)
                nc.scalar.activation(nat[:, b % 2, HI], nat_raw[:, b % 2], ACT.Copy).then_inc(nat_hi, 1)

            def w0_copy(w):
                act.wait_ge(d_w0[w], 16)
                nc.scalar.activation(w0S[:, HI, w], w_raw[:, w], ACT.Copy).then_inc(w0_hi, 1)

            ctx_hi(0)
            w0_copy(WQ)
            w0_copy(WK)
            for name in first_fills + second_fills[:1]:
                startup_fill(name)
            exps0(0)
            for name in second_fills[1:]:
                startup_fill(name)
            w0_copy(WV)
            ctx_hi(1)
            for b in range(B):
                before, behind = slot_fills[b]
                probsT_hi(b)
                for name in before[:2]:
                    startup_fill(name)
                if b < B - 1:
                    exps0(b + 1)
                for name in before[2:]:
                    startup_fill(name)
                if b in (1, 2):
                    ctx_hi(b + 1)
                mix_hi_copy(b, mixT[:, HI], mix_ps[:].rearrange("p (c q) -> p c q", c=DC))
                if b:
                    ln_full(b - 1, NAMED[f"lnT0.{b-1}"], 0)
                for name in behind:
                    startup_fill(name)
                    if name == "vec":
                        act.wait_ge(fill_hi, FILL["vec"] + 1)
                        pair_bias(0, 0)
            exps(0, 0, 0)
            pair_values(0, 0)

            def body(l, r, nxt):
                last = is_last(r)
                for k in range(UNITS):
                    b, h = k // 2, k % 2
                    u = unit(l, r, k)
                    to = (l, r, b + 1) if b < B - 1 else (nxt + (0,) if nxt else None)
                    ls, ln_b, _ = ln_of_step(l, r, b)
                    after = (l, r, k + 1) if k < UNITS - 1 else (nxt + (0,) if nxt else None)

                    def fill(kind):
                        if to:
                            step_fill_hi(step_fill(l, r, b + 1, kind), kind, *to, (NF0 + 5 * b + kind) % 2)
                        else:
                            mlp_gelu(kind)

                    def mix_out():
                        mix_hi_copy(u, mixT[:, HI, h], mix_ps[:, 0:LQ])
                        if last and h == 1:
                            act.wait_ge(out_done, use_of(l, r, f"pbT{b}") + 1)
                            nc.scalar.activation(pbT[:, HI], out_ps[0:RW, 0:LQ], ACT.Copy).then_inc(pbT_hi, 1)

                    probsT_hi(u)
                    if h == 0:
                        if to:
                            exps(l, r, k + 1, between=lambda: fill(0))
                        else:
                            exps(l, r, k + 1)
                            fill(0)
                        fill(1)
                        mix_out()
                        fill(2)
                    else:
                        if ln_b is not None:
                            ln_full(4 * ls + ln_b, NAMED[f"lnT{ls}.{ln_b}"], ls)
                        fill(3)
                        if after:
                            exps(*after, between=mix_out)
                        else:
                            mix_out()
                        fill(4)
                    if nxt and k == 5:
                        pair_bias(*nxt)
                        pair_values(*nxt)

            for l in range(2):
                body(l, 0, (l, 1))
                with act.Fori(1, PAIRS - 1) as r:
                    body(l, r, (l, r + 1))
                body(l, PAIRS - 1, (1, 0) if l == 0 else None)
            for n in range(5, FC):
                mlp_gelu(n)
            ln_full(8 + B - 1, NAMED[f"lnT2.{B - 1}"], 2)
            for n in range(FC, 2 * FC):
                mlp_gelu(n)

        @block.vector
        def _(dve):
            links = [0]

            def link(ins):
                links[0] += 1
                ins.then_inc(chain, 1)
                dve.wait_ge(chain, links[0])

            def lo_sub(f, dst, src, hi, bias=None):
                dve.wait_ge(fill_hi, f + 1)
                if bias is None:
                    return nc.vector.tensor_tensor(dst, src, hi.bitcast(F32), ALU.subtract)
                return nc.vector.scalar_tensor_tensor(dst, src, bias, hi.bitcast(F32), ALU.add, ALU.subtract)

            def split(hi, lo, full):
                link(nc.vector.tensor_copy(hi, full))
                return nc.vector.tensor_tensor(lo, full, hi.bitcast(F32), ALU.subtract)

            def startup_fill(name):
                f = FILL[name]
                pj = proj[f % 2]
                halves = pj[:].rearrange("p (a n) -> p a n", a=2)
                b = int(name[2]) if name[0] in "xc" else 0
                if name == "vec":
                    dve.wait_ge(fill_hi, f + 1)
                    for l in range(2):
                        v = vecT[:, l]
                        nc.vector.tensor_tensor(bqk[:, l], v[:, BQ:BQ + HEADS], v[:, BIAS_K:BIAS_K + HEADS], ALU.mult)
                        link(nc.vector.tensor_tensor(v_diff[:, l], v[:, BIAS_V:BIAS_V + HEADS], v[:, BV:BV + HEADS], ALU.subtract))
                        hi, lo = (ev[:, s, l].rearrange("p h c -> p (h c)") for s in (HI, LO))
                        for at, step, src in ((0, RW, v[:, BV:BV + HEADS]), (1, RW + 1, v_diff[:, l])):
                            cells = slice(at, at + (HEADS - 1) * step + 1, step)
                            ins = split(hi[:, cells], lo[:, cells], src)
                elif name == "M":
                    ins = lo_sub(f, mS[:, LO], halves, mS[:, HI])
                elif name[:2] == "xT":
                    ins = lo_sub(f, hT[:, LO, :, b * LQ:(b + 1) * LQ], halves, hT[:, HI, :, b * LQ:(b + 1) * LQ])
                elif name[:2] == "cT":
                    c = int(name[3])
                    ins = lo_sub(f, cT[:, LO, c, b * T:(b + 1) * T], pj[:], cT[:, HI, c, b * T:(b + 1) * T])
                elif name == "WoT":
                    ins = lo_sub(f, w0S[:, LO, WO], halves, w0S[:, HI, WO])
                elif name == "N":
                    ins = lo_sub(f, nS[:, LO], halves, nS[:, HI])
                elif name[0] == "G":
                    ins = lo_sub(f, gS[:, LO], halves, gS[:, HI])
                elif name == "bqk":
                    dve.wait_ge(fill_hi, f + 1)
                    ins = nc.vector.tensor_copy(bqk_sum[:, 1:2], pj[0:HEADS, 1:2])
                else:
                    return step_fill_lo(f, {"K0": 0, "Q": 1, "K1": 2, "Va": 3, "Vb": 4}[name], 0, 0, 0, f % 2)
                ins.then_inc(fill_lo, 1)

            def wb_chunk(c):
                dve.wait_ge(wb_products, c + 1)
                nc.vector.reduce_sum(wb_full[:, 0, :, c * CHUNK_H:(c + 1) * CHUNK_H],
                                     ck_wq[:, c % 2].rearrange("p c (h k) -> p c h k", k=DH), AX_X).then_inc(wb_used, 1)
                if c == CHUNKS - 1:
                    dve.wait_ge(wb_used, c + 1)
                    split(wbS[:, HI, 0], wbS[:, LO, 0], wb_full[:, 0]).then_inc(wb_ready, 1)

            def wb_pair(r):
                dve.wait_ge(d_wq[0], r * 16 + 16 * (CHUNKS // 2 + 1))
                dve.wait_ge(d_bk[0], r * 16 + 16 * (CHUNKS // 2 + 1))
                for i in range(DC):
                    ins = nc.vector.tensor_tensor(ck_wq[:, 0, i, 0:PW], ck_wq[:, 0, i, 0:PW], ck_bk[:, 0, 0:PW], ALU.mult)
                ins.then_inc(wb_products, 1)
                dve.wait_ge(wb_products, r + (CHUNKS + 1))
                nc.vector.reduce_sum(wb_two[:], ck_wq[:, 0, :, 0:PW].rearrange("p c (h k) -> p c h k", k=DH), AX_X).then_inc(wb_used, 1)
                dve.wait_ge(wb_used, r + (CHUNKS + 1))
                nc.vector.tensor_tensor(wb_full[:, 1, :, bass.ds(r * 2, 2)], wb_two[:], wb_two[:], ALU.max).then_inc(wb_pairs, 1)

            def r_add(l, r):
                use = use_r(l, r)
                dve.wait_ge(out_done, use + 1)
                if l == 0 and is_first(r):
                    dve.wait_ge(d_small, 48)
                nc.vector.tensor_tensor(r_full[:, l], out_ps[0:RW, 0:D], r_full[:, l], ALU.add).then_inc(out_free, 1)
                if is_last(r):
                    dve.wait_ge(out_free, use + 1)
                    split(rS[:, HI, l], rS[:, LO, l], r_full[:, l]).then_inc(r_ready, 1)

            def step_fill_lo(f, kind, l, r, b, bank):
                pj = proj[bank]
                if kind in (0, 2):
                    h = kind // 2
                    ins = lo_sub(f, kT[:, LO, h], pj[:], kT[:, HI, h], vecT[:, l, bass.ds(r * 2 + (BK + h), 1)])
                elif kind == 1:
                    for h in range(2):
                        ins = lo_sub(f, qT[:, LO, h], pj[:, h * LQ:(h + 1) * LQ], qT[:, HI, h], vecT[:, l, bass.ds(r * 2 + (BQ + h), 1)])
                else:
                    c = 2 * (kind - 3)
                    ins = lo_sub(f, vS[:, LO, b % 2, c:c + 2], pj[:].rearrange("p (c n) -> p c n", c=2), vS[:, HI, b % 2, c:c + 2])
                ins.then_inc(fill_lo, 1)

            def probsT_lo(u, halves=(0, 1)):
                for j in halves:
                    dve.wait_ge(pt_hi, u * 2 + (j + 1))
                    nc.vector.tensor_tensor(probsT[:, LO, 2 * j:2 * j + 2], probsT_ps[:, 2 * j:2 * j + 2],
                                            probsT[:, HI, 2 * j:2 * j + 2].bitcast(F32), ALU.subtract).then_inc(pt_lo, 1)

            def mix_lo_sub(u, dst, src, hi):
                dve.wait_ge(mix_hi, u + 1)
                nc.vector.tensor_tensor(dst, src, hi.bitcast(F32), ALU.subtract).then_inc(mix_lo, 1)

            def maxima(u):
                dve.wait_ge(scores_done, u + 1)
                nc.vector.reduce_max(mx[:], scores[:], AX_X).then_inc(max_ready, 1)
                dve.wait_ge(max_ready, u + 1)

            def shift0(b):
                maxima(b)
                nc.vector.tensor_scalar(shift[:], mx[:], -SCALE0, None, ALU.mult).then_inc(shift_ready, 1)

            def shifts(l, r, k):
                b, h = k // 2, k % 2
                maxima(unit(l, r, k))
                nc.vector.scalar_tensor_tensor(shift[:].rearrange("p (t a) -> p t a", a=1),
                                               mx[:].rearrange("p (t a) -> p t a", a=1), -SCALE,
                                               nsb[:, QT * b:QT * (b + 1), bass.ds(r * 2 + h, 1)],
                                               ALU.mult, ALU.min).then_inc(shift_ready, 1)

            def sums(l, r, k):
                u = unit(l, r, k)
                dve.wait_ge(eb_ready, u - B + 1)
                for t in range(QT):
                    if t:
                        dve.wait_ge(exp_done, u * 2 + 2)
                    nc.vector.tensor_tensor(zsum[:, t:t + 1], z[:, t:t + 1], eb[:, t:t + 1], ALU.add).then_inc(zsum_ready, 1)
                    dve.wait_ge(zsum_ready, u * 2 + (t + 1 - 2 * B))
                    nc.vector.reciprocal(rz[:, t:t + 1], zsum[:, t:t + 1]).then_inc(rz_ready, 1)

            def pair_weights(l, r, b0, b1):
                dve.wait_ge(norm_done, unit(l, r, 2 * b1) - B)
                tiles = slice(QT * b0, QT * b1)
                nc.vector.tensor_tensor(p_bias[:, tiles, bass.ds(r * 2 + 1, 2)], p_pair[:, tiles], p_pair[:, tiles], ALU.max).then_inc(pb_ready, 1)

            def add_out(use, b):
                dve.wait_ge(out_done, use + 1)
                xb = x[:, QT * b:QT * (b + 1)]
                nc.vector.tensor_tensor(xb, out_ps[:].rearrange("p (t n) -> p t n", t=QT), xb, ALU.add).then_inc(out_free, 1)

            def ln_stats(use, b):
                dve.wait_ge(out_free, use + 1)
                for t in range(QT):
                    ins = nc.vector.bn_stats(bn[:, t], x[:, QT * b + t])
                link(ins)
                for t in range(QT):
                    ins = nc.vector.bn_aggr(mv[:, t], bn[:, t])
                link(ins)
                nc.vector.tensor_scalar(var[:], mv[:, :, 1], EPS, None, ALU.add).then_inc(var_ready, 1)

            def ln_x(n, b, mlp=False):
                dve.wait_ge(rstd_ready, n + 1)
                for t in range(QT):
                    ins = nc.vector.tensor_scalar(xn[:, t], x[:, QT * b + t], mv[:, t, 0:1], rstd[:, t:t + 1], ALU.subtract, ALU.mult)
                ins.then_inc(xn_ready, 1)
                if mlp:
                    for t in range(QT):
                        nc.vector.tensor_tensor(x[:, QT * b + t], x[:, QT * b + t], b2_row[:], ALU.add)

            def ln_split(use, b):
                dve.wait_ge(out_free, use + 1)
                hi, lo = (hT[:, s, :, b * LQ:(b + 1) * LQ] for s in (HI, LO))
                split(hi, lo, h_full[:]).then_inc(hT_ready, 1)

            def bias_logits(use, l):
                dve.wait_ge(out_done, use + 1)
                nc.vector.tensor_scalar(logits[:], out_ps[0:HEADS, 0:LQ], bqk_sum[:, l:l + 1], -SCALE, ALU.add, ALU.mult).then_inc(out_free, 1)

            def logits_rows(use, b):
                dve.wait_ge(out_done, use + 1)
                nc.vector.tensor_copy(nsb[:, QT * b:QT * (b + 1)], out_ps[:, 0:QT * HEADS].rearrange("p (t h) -> p t h", t=QT)).then_inc(out_free, 1)

            def mlp_split(n):
                dve.wait_ge(fill_hi, MLP_FILL + n + 1)
                split(gelu[HI][n % FC], gelu[LO][n % FC], gelu_full[:, n % 2]).then_inc(fill_lo, 1)

            def w0_sub(n, w):
                dve.wait_ge(w0_hi, n + 1)
                nc.vector.tensor_tensor(w0S[:, LO, w], w_raw[:, w], w0S[:, HI, w].bitcast(F32), ALU.subtract).then_inc(w0_ready, 1)

            def sums0(b):
                dve.wait_ge(exp_done, 2 * b + 2)
                link(nc.vector.reciprocal(rz0[:, b], z[:]))
                link(nc.vector.tensor_scalar(rz0[:, b], rz0[:, b], alpha[:], None, ALU.mult))

            w0_sub(0, WQ)
            w0_sub(1, WK)
            for name in first_fills:
                startup_fill(name)
            shift0(0)
            for name in second_fills:
                startup_fill(name)
            w0_sub(2, WV)
            dve.wait_ge(d_alpha, 16)
            sums0(0)
            for b in range(B):
                before, behind = slot_fills[b]
                if b < B - 1:
                    shift0(b + 1)
                probsT_lo(b, halves=(0,) if b < 2 else (0, 1))
                for name in before[:2]:
                    startup_fill(name)
                if b < 2:
                    probsT_lo(b, halves=(1,))
                if b == B - 1:
                    ln_stats(NAMED[f"delta{b-1}"], b - 1)
                    wb_chunk(2)
                if b:
                    ln_x(b - 1, b - 1)
                if b < B - 1:
                    sums0(b + 1)
                for name in before[2:]:
                    startup_fill(name)
                if b >= 2:
                    ln_split(NAMED[f"lnT0.{b-2}"], b - 2)
                if b in (1, 2):
                    wb_chunk(b - 1)
                mix_lo_sub(b, mixT[:, LO], mix_ps[:].rearrange("p (c q) -> p c q", c=DC), mixT[:, HI])
                if b == B - 1:
                    wb_chunk(3)
                for name in behind:
                    startup_fill(name)
                use = NAMED[f"delta{b}"]
                dve.wait_ge(out_done, use + 1)
                for t in range(QT):
                    xt = x[:, QT * b + t]
                    ins = nc.vector.scalar_tensor_tensor(xt, out_ps[:, t * D:(t + 1) * D], rz0[:, b, t:t + 1], xt, ALU.mult, ALU.add)
                ins.then_inc(out_free, 1)
                if b != B - 2:
                    ln_stats(use, b)
            bias_logits(NAMED["sbT0.0"], 0)
            logits_rows(NAMED["sb0.0"], 0)
            shifts(0, 0, 0)
            bias_logits(NAMED["sbT0.1"], 0)
            logits_rows(NAMED["sb0.1"], 1)
            sums(0, 0, 0)
            ln_split(NAMED["lnT0.2"], 2)

            def body(l, r, nxt):
                last = is_last(r)
                for k in range(UNITS):
                    b, h = k // 2, k % 2
                    u = unit(l, r, k)
                    to = (l, r, b + 1) if b < B - 1 else (nxt + (0,) if nxt else None)
                    after = (l, r, k + 1) if k < UNITS - 1 else (nxt + (0,) if nxt else None)
                    ls, ln_b, sb_b = ln_of_step(l, r, b)
                    if h == 0 and b:
                        add_out(use_out(l, r, b - 1), b - 1)
                        if last:
                            ln_stats(use_out(l, r, b - 1), b - 1)
                    if h == 0:
                        shifts(*after)
                    probsT_lo(u)
                    if h == 1 and after:
                        shifts(*after)

                    def fill(kind):
                        if to:
                            step_fill_lo(step_fill(l, r, b + 1, kind), kind, *to, (NF0 + 5 * b + kind) % 2)
                        else:
                            mlp_split(kind)

                    if h == 0:
                        fill(0)
                        sums(*after)
                        if ln_b is not None:
                            ln_x(4 * ls + ln_b, ln_b, mlp=ls == 2)
                        if sb_b is not None:
                            bias_logits(NAMED[f"sbT{ls}.{sb_b}"], ls)
                        if l == 0 and k == 2:
                            wb_pair(r)
                            if last:
                                dve.wait_ge(wb_pairs, PAIRS)
                                split(wbS[:, HI, 1], wbS[:, LO, 1], wb_full[:, 1]).then_inc(wb_ready, 1)
                        fill(1)
                        mix_lo_sub(u, mixT[:, LO, h], mix_ps[:, 0:LQ], mixT[:, HI, h])
                        if k == 0:
                            r_add(l, r)
                        if sb_b is not None:
                            logits_rows(NAMED[f"sb{ls}.{sb_b}"], sb_b)
                        fill(2)
                    else:
                        if ln_b is not None:
                            ln_split(NAMED[f"lnT{ls}.{ln_b}"], ln_b)
                        if last:
                            pair_weights(l, r, b, b + 1)
                        elif k == UNITS - 1:
                            pair_weights(l, r, 0, B)
                        fill(3)
                        mix_lo_sub(u, mixT[:, LO, h], mix_ps[:, 0:LQ], mixT[:, HI, h])
                        if last:
                            dve.wait_ge(pbT_hi, B * l + b + 1)
                            nc.vector.tensor_tensor(pbT[:, LO], out_ps[0:RW, 0:LQ], pbT[:, HI].bitcast(F32), ALU.subtract).then_inc(out_free, 1)
                        if after:
                            sums(*after)
                        fill(4)
                add_out(use_out(l, r, B - 1), B - 1)

            for l in range(2):
                body(l, 0, (l, 1))
                with dve.Fori(1, PAIRS - 1) as r:
                    body(l, r, (l, r + 1))
                body(l, PAIRS - 1, (1, 0) if l == 0 else None)
                ln_stats(use_out(l, PAIRS - 1, B - 1), B - 1)
            ln_x(8 + B - 1, B - 1, mlp=True)
            for n in range(5, FC):
                mlp_split(n)

            def result(n):
                b = MLP_ORDER[n]
                dve.wait_ge(down_done, n + 1)
                for t in range(QT):
                    xt = x[:, QT * b + t]
                    ins = nc.vector.tensor_tensor(xt, down_ps[b % 2][t], xt, ALU.add)
                ins.then_inc(result_ready, 1)

            ln_split(NAMED[f"lnT2.{B - 1}"], B - 1)
            result(0)
            mlp_split(FC)
            result(1)
            for n in range(FC + 1, 2 * FC):
                mlp_split(n)
            result(2)
            result(3)


        @block.tensor
        def _(pe):
            def product(out, pairs):
                n = len(pairs) * len(PASSES)
                i = 0
                for a, b_ in pairs:
                    for s, t in PASSES:
                        ins = nc.tensor.matmul(out, a(s), b_(t), start=(i == 0), stop=(i == n - 1))
                        i += 1
                return ins

            def fill_bank(f):
                if isinstance(f, int) and f < 2:
                    return
                pe.wait_ge(fill_lo, f - 1)

            def startup_fill(name):
                f = FILL[name]
                pj = proj[f % 2]
                b = int(name[2]) if name[0] in "xc" else 0
                fill_bank(f)
                if name == "vec":
                    pe.wait_ge(d_vec, 17 * 16)
                    for l in range(2):
                        ins = nc.tensor.transpose(pj[:, l * P:(l + 1) * P], vec_raw[:, l], ident[:])
                elif name == "M":
                    pe.wait_ge(w0_ready, 2)
                    for i in range(DC):
                        ins = product(pj[:, i * D:(i + 1) * D],
                                      [(lambda s, o=o: w0S[:, s, WQ, o, i * P:(i + 1) * P], lambda s, o=o: w0S[:, s, WK, o]) for o in range(DC)])
                elif name[:2] == "xT":
                    pe.wait_ge(d_x, 16)
                    for c in range(DC):
                        for t in range(QT):
                            ins = nc.tensor.transpose(pj[:, (c * QT + t) * P:(c * QT + t + 1) * P], x[:, QT * b + t, c * P:(c + 1) * P], ident[:])
                elif name[:2] == "cT":
                    c = int(name[3])
                    pe.wait_ge(d_nat[b % 2], 16 * (b // 2 + 1))
                    for t in range(TC):
                        ins = nc.tensor.transpose(pj[:, t * P:(t + 1) * P], nat_raw[:, b % 2, t, c * P:(c + 1) * P], ident[:])
                elif name == "WoT":
                    pe.wait_ge(d_w0[WO], 16)
                    for v in range(DC):
                        for o in range(DC):
                            ins = nc.tensor.transpose(pj[:, (v * DC + o) * P:(v * DC + o + 1) * P], w_raw[:, WO, o, v * P:(v + 1) * P], ident[:])
                elif name == "N":
                    pe.wait_ge(w0_ready, 3)
                    pe.wait_ge(fill_lo, FILL["WoT"] + 1)
                    for i in range(DC):
                        ins = product(pj[:, i * D:(i + 1) * D],
                                      [(lambda s, v=v: w0S[:, s, WV, v, i * P:(i + 1) * P], lambda s, v=v: w0S[:, s, WO, v]) for v in range(DC)])
                elif name[0] == "G":
                    b = int(name[1])
                    pe.wait_ge(fill_lo, max(FILL["M"], FILL[f"xT{b}"]) + 1)
                    for j in range(DC):
                        ins = product(pj[:, j * LQ:(j + 1) * LQ],
                                      [(lambda s, i=i: mS[:, s, i, j * P:(j + 1) * P], lambda s, i=i: hT[:, s, i, b * LQ:(b + 1) * LQ]) for i in range(DC)])
                elif name == "bqk":
                    pe.wait_ge(fill_lo, FILL["vec"] + 1)
                    for l in range(2):
                        ins = nc.tensor.matmul(pj[0:HEADS, l:l + 1], bqk[:, l], ones[:, 0:1], start=True, stop=True)
                else:
                    return step_fill_mm(f, {"K0": 0, "Q": 1, "K1": 2, "Va": 3, "Vb": 4}[name], 0, 0, 0, f % 2, wait=False)
                ins.then_inc(fill_done, 1)

            def step_fill_mm(f, kind, l, r, b, bank, wait=True):
                pj = proj[bank]
                if wait:
                    fill_bank(f)
                if kind == 1 and is_first(r):
                    pe.wait_ge(hT_ready, B * l + b + 1)
                if b == 0:
                    w = {0: WK, 1: WQ, 3: WV}.get(kind)
                    if w is not None:
                        pe.wait_ge(w_ready[w], r + (PAIRS * l + 1))
                if kind in (0, 2):
                    h = kind // 2
                    ins = product(pj[:], [(lambda s, c=c: wS[:, s, WK, c, h * DH:(h + 1) * DH], lambda s, c=c: cT[:, s, c, b * T:(b + 1) * T]) for c in range(DC)])
                elif kind == 1:
                    for h in range(2):
                        ins = product(pj[:, h * LQ:(h + 1) * LQ],
                                      [(lambda s, c=c: wS[:, s, WQ, c, h * DH:(h + 1) * DH], lambda s, c=c: hT[:, s, c, b * LQ:(b + 1) * LQ]) for c in range(DC)])
                else:
                    for j in range(2):
                        at = b * T + (2 * (kind - 3) + j) * P
                        ins = product(pj[:, j * PW:(j + 1) * PW],
                                      [(lambda s, c=c: cT[:, s, c, at:at + P], lambda s, c=c: wS[:, s, WV, c]) for c in range(DC)])
                ins.then_inc(fill_done, 1)

            def unit_scores(l, r, k, ready):
                h = k % 2
                u = unit(l, r, k)
                pe.wait_ge(fill_lo, ready + 1)
                pe.wait_ge(exp_done, u * 2)
                for t in range(QT):
                    ins = product(scores[:, t], [(lambda s: qT[:, s, h, t * P:(t + 1) * P], lambda s: kT[:, s, h])])
                ins.then_inc(scores_done, 1)

            def transposes(u):
                for j in range(2):
                    if not (isinstance(u, int) and u == 0):
                        pe.wait_ge(pt_lo, u * 2 + (j - 1))
                    for c in (2 * j, 2 * j + 1):
                        for t in range(QT):
                            ins = nc.tensor.transpose(probsT_ps[:, c, t * P:(t + 1) * P], probs[:, t, c * P:(c + 1) * P], ident[:])
                    ins.then_inc(pt_done, 1)

            def mix(l, r, k, ready):
                b, h = k // 2, k % 2
                u = unit(l, r, k)
                pe.wait_ge(mix_lo, u)
                if ready is not None:
                    pe.wait_ge(fill_lo, ready + 1)
                n = 0
                for c in range(TC):
                    if c % 2 == 0:
                        pe.wait_ge(pt_lo, u * 2 + (c // 2 + 1))
                    for s, t in PASSES:
                        ins = nc.tensor.matmul(mix_ps[:, 0:LQ], vS[:, s, b % 2, c, h * DH:(h + 1) * DH], probsT[:, t, c],
                                               start=(n == 0), stop=(n == 3 * TC - 1))
                        n += 1
                ins.then_inc(mix_done, 1)

            def step_out(l, r, b):
                last = is_last(r)
                pe.wait_ge(mix_lo, unit(l, r, 2 * b + 2))
                use = use_out(l, r, b)
                pe.wait_ge(out_free, use)
                for t in range(QT):
                    terms = [(lambda s, h=h: mixT[:, s, h, t * P:(t + 1) * P], lambda s, h=h: wS[:, s, WO, h]) for h in range(2)]
                    if last:
                        pe.wait_ge(r_ready, l + 1)
                        terms.append((lambda s: pbT[:, s, t * P:(t + 1) * P], lambda s: rS[:, s, l]))
                    ins = product(out_ps[:, t * D:(t + 1) * D], terms)
                ins.then_inc(out_done, 1)

            def ln_transposes(n, use):
                pe.wait_ge(xn_ready, n + 1)
                pe.wait_ge(out_free, use)
                for c in range(DC):
                    for t in range(QT):
                        ins = nc.tensor.transpose(out_ps[:, (c * QT + t) * P:(c * QT + t + 1) * P], xn[:, t, c * P:(c + 1) * P], ident[:])
                ins.then_inc(out_done, 1)

            def bias_logits(n, use, l, b):
                pe.wait_ge(hT_ready, n + 1)
                pe.wait_ge(out_free, use)
                pe.wait_ge(wb_ready, l + 1)
                ins = product(out_ps[0:HEADS, 0:LQ],
                              [(lambda s, c=c: wbS[:, s, l, c], lambda s, c=c: hT[:, s, c, b * LQ:(b + 1) * LQ]) for c in range(DC)])
                ins.then_inc(out_done, 1)

            def logits_transposes(use):
                pe.wait_ge(out_free, use)
                for t in range(QT):
                    ins = nc.tensor.transpose(out_ps[:, t * HEADS:(t + 1) * HEADS], logits[:, t * P:(t + 1) * P], ident[0:HEADS, 0:HEADS])
                ins.then_inc(out_done, 1)

            def scores0(b):
                pe.wait_ge(fill_lo, max(FILL[f"G{b}"], FILL[f"cT{b}1"]) + 1)
                if b:
                    pe.wait_ge(exp_done, 2 * b)
                for t in range(QT):
                    ins = product(scores[:, t], [(lambda s, j=j: gS[:, s, j, t * P:(t + 1) * P], lambda s, j=j: cT[:, s, j, b * T:(b + 1) * T])
                                                 for j in range(DC)])
                ins.then_inc(scores_done, 1)

            pe.wait_ge(consts_ready, 6)
            for name in first_fills:
                startup_fill(name)
            scores0(0)
            for name in second_fills:
                startup_fill(name)
            for b in range(B):
                if b < B - 1:
                    scores0(b + 1)
                pe.wait_ge(exp_done, 2 * b + 2)
                transposes(b)
                before, behind = slot_fills[b]
                for name in before:
                    startup_fill(name)
                pe.wait_ge(nat_ready, b + 1)
                if b:
                    pe.wait_ge(mix_lo, b)
                pe.wait_ge(pt_lo, 2 * b + 2)
                for i in range(DC):
                    ins = product(mix_ps[:, i * LQ:(i + 1) * LQ],
                                  [(lambda s, c=c: nat[:, b % 2, s, c, i * P:(i + 1) * P], lambda s, c=c: probsT[:, s, c]) for c in range(TC)])
                ins.then_inc(mix_done, 1)
                if b:
                    ln_transposes(b - 1, NAMED[f"lnT0.{b-1}"])
                for name in behind:
                    startup_fill(name)
                pe.wait_ge(mix_lo, b + 1)
                pe.wait_ge(fill_lo, FILL["N"] + 1)
                if b:
                    pe.wait_ge(out_free, NAMED[f"delta{b}"])
                for t in range(QT):
                    ins = product(out_ps[:, t * D:(t + 1) * D],
                                  [(lambda s, i=i: mixT[:, s, i, t * P:(t + 1) * P], lambda s, i=i: nS[:, s, i]) for i in range(DC)])
                ins.then_inc(out_done, 1)
            bias_logits(0, NAMED["sbT0.0"], 0, 0)
            unit_scores(0, 0, 0, FILL["Q"])
            logits_transposes(NAMED["sb0.0"])
            bias_logits(1, NAMED["sbT0.1"], 0, 1)
            logits_transposes(NAMED["sb0.1"])

            def r_part(l, r):
                pe.wait_ge(w_ready[WO], r + (PAIRS * l + 1))
                pe.wait_ge(ev_ready, r + (PAIRS * l + 1))
                pe.wait_ge(out_free, use_r(l, r))
                ins = product(out_ps[0:RW, 0:D], [(lambda s, h=h: ev_pair[:, s, h], lambda s, h=h: wS[:, s, WO, h]) for h in range(2)])
                ins.then_inc(out_done, 1)

            def up(n):
                half, f = n // FC, n % FC
                if n >= 2:
                    pe.wait_ge(fill_hi, MLP_FILL + n - 1)
                else:
                    fill_bank(MLP_FILL + n)
                if n == 0:
                    pe.wait_ge(mlp_ready, 4)
                if f == 0:
                    pe.wait_ge(hT_ready, 8 + 2 * half + 2)
                ins = product(proj[(MLP_FILL + n) % 2][:],
                              [(lambda s, c=c: w1S[:, s, c, f * P:(f + 1) * P], lambda s, c=c: hT[:, s, c, half * 2 * LQ:(half + 1) * 2 * LQ]) for c in range(DC)])
                ins.then_inc(fill_done, 1)

            def down(i, t, f):
                q0 = i * LQ + t * P
                for j, (s, s2) in enumerate(PASSES):
                    ins = nc.tensor.matmul(down_ps[i][t], gelu[s][f][:, q0:q0 + P], w2S[:, s2, f],
                                           start=(f == 0 and j == 0), stop=(f == FC - 1 and j == len(PASSES) - 1))
                return ins

            def body(l, r, nxt):
                last = is_last(r)
                for k in range(UNITS):
                    b, h = k // 2, k % 2
                    u = unit(l, r, k)
                    to = (l, r, b + 1) if b < B - 1 else (nxt + (0,) if nxt else None)
                    ls, ln_b, sb_b = ln_of_step(l, r, b)
                    after = (l, r, k + 1) if k < UNITS - 1 else (nxt + (0,) if nxt else None)
                    if h == 0 and after:
                        unit_scores(*after, step_fill(l, r, b, 2))
                    pe.wait_ge(norm_done, u - B + 1)
                    transposes(u)
                    if h == 1 and after:
                        unit_scores(*after, step_fill(l, r, b + 1, 1))

                    def fill(kind):
                        if to:
                            step_fill_mm(step_fill(l, r, b + 1, kind), kind, *to, (NF0 + 5 * b + kind) % 2)
                        else:
                            up(kind)

                    if h == 0:
                        fill(0)
                        if sb_b is not None:
                            bias_logits(4 * ls + sb_b, NAMED[f"sbT{ls}.{sb_b}"], ls, sb_b)
                        fill(1)
                        mix(l, r, k, step_fill(l, r, b, 4))
                        if k == 0:
                            r_part(l, r)
                        fill(2)
                        if sb_b is not None:
                            logits_transposes(NAMED[f"sb{ls}.{sb_b}"])
                        if ln_b is not None:
                            ln_transposes(4 * ls + ln_b, NAMED[f"lnT{ls}.{ln_b}"])
                    else:
                        fill(3)
                        mix(l, r, k, None)
                        if last:
                            pe.wait_ge(out_free, use_of(l, r, f"pbT{b}"))
                            pe.wait_ge(pb_ready, (PAIRS - 1 + B) * l + PAIRS + b)
                            for t in range(QT):
                                ins = nc.tensor.transpose(out_ps[0:RW, t * P:(t + 1) * P], p_bias[:, QT * b + t], ident[:])
                            ins.then_inc(out_done, 1)
                        fill(4)
                        step_out(l, r, b)

            for l in range(2):
                body(l, 0, (l, 1))
                with pe.Fori(1, PAIRS - 1) as r:
                    body(l, r, (l, r + 1))
                body(l, PAIRS - 1, (1, 0) if l == 0 else None)
            for f in range(5, FC):
                up(f)
            ln_transposes(8 + B - 1, NAMED[f"lnT2.{B - 1}"])

            pe.wait_ge(mlp_ready, 8)
            pe.wait_ge(mix_lo, B + 2 * UNITS * PAIRS)
            for i in (1, 0):
                if i == 0:
                    pe.wait_ge(out_free, USES)
                for f in range(FC):
                    if i == 1:
                        pe.wait_ge(fill_lo, MLP_FILL + f + 1)
                    for t in range(QT):
                        ins = down(i, t, f)
                ins.then_inc(down_done, 1)
            for f in range(FC + 2):
                if f < FC:
                    up(FC + f)
                if f >= 2:
                    pe.wait_ge(fill_lo, MLP_FILL + FC + f - 1)
                    for i in range(2):
                        if f == 2:
                            pe.wait_ge(result_ready, 2 - i)
                        for t in range(QT):
                            ins = down(i, t, f - 2)
                        if f == FC + 1:
                            ins.then_inc(down_done, 1)


_INS = (["x", "ctx_2048", "L0_xattn_w_q", "L0_xattn_w_k", "L0_xattn_w_v", "L0_xattn_w_o", "L0_xattn_alpha"]
        + [f"L1_xattn_{n}{i}{s}" for i in (1, 2) for n, s in (("ln", "_scale"), ("ln", "_offset"), ("wq", ""), ("bq", ""), ("wk", ""),
           ("bk", ""), ("wv", ""), ("bv", ""), ("wo", ""), ("bo", ""), ("bias_k", ""), ("bias_v", ""))]
        + ["L1_xattn_ln_mlp_scale", "L1_xattn_ln_mlp_offset", "L1_xattn_w_fc1", "L1_xattn_b_fc1", "L1_xattn_w_fc2", "L1_xattn_b_fc2"])


def kernel(**inputs):
    import numpy as _np
    import concourse.bacc as _bacc
    from concourse import mybir as _mybir
    from concourse.bass_utils import run_bass_kernel_spmd as _run

    nc = _bacc.Bacc("TRN2", target_bir_lowering=False, num_devices=1)
    arrays, aps = {}, {}
    for name in _INS:
        a = _np.ascontiguousarray(inputs[name])
        if a.ndim == 0:
            a = a.reshape(1)
        arrays[f"in_{name}_dram"] = a
        aps[name] = nc.dram_tensor(f"in_{name}_dram", a.shape, _mybir.dt.from_np(a.dtype), kind="ExternalInput").ap()
    aps["out"] = nc.dram_tensor("out_0_dram", (B, LQ, D), _mybir.dt.float32, kind="ExternalOutput").ap()
    xattn_kernel(nc, aps)
    r = _run(nc, [arrays], core_ids=[0])
    return r.results[0]["out_0_dram"]
```
